# Optimizing a Trainium2 kernel written in Bass

```python
import numpy as np
import jax
import jax.numpy as jnp

def _softmax(x, axis=-1):
    return jax.nn.softmax(x, axis=axis)

def _gelu(x):
    return jax.nn.gelu(x, approximate=True)

def _silu(x):
    return jax.nn.silu(x)

def _sigmoid(x):
    return jax.nn.sigmoid(x)

def _layernorm(x, axis=-1, eps=1e-05):
    m = jnp.mean(x, axis=axis, keepdims=True)
    v = jnp.var(x, axis=axis, keepdims=True)
    return (x - m) / jnp.sqrt(v + eps)

def _scatter_add(tgt, idx, src, axis=0):
    return tgt.at[idx].add(src)

def _segment_sum(src, seg, n):
    return jax.ops.segment_sum(src, seg, n)
kernel_name = 'mk_flamingo_gated_d2_seqx_r4_02be8a'

def setup_inputs(seed: int=0):
    np.random.seed(seed)
    _w = jnp.asarray

    def _rec_inputs():
        import jax
        import jax.numpy as jnp
        _rk = jax.random.key(seed)
        x = -0.0002928 + 1 * jax.random.normal(jax.random.fold_in(_rk, 1), (4, 512, 256), jnp.float32)
        _lenS = 512 - jax.random.randint(jax.random.fold_in(_rk, 7), (4,), 0, max(1, 512 // 4) + 1, jnp.int32)
        _lenS2 = 64 - jax.random.randint(jax.random.fold_in(_rk, 8), (4,), 0, max(1, 64 // 4) + 1, jnp.int32)
        _ctx_1024P = jax.random.normal(jax.random.fold_in(_rk, 11), (4, 16, 256), jnp.float32)
        _ctx_1024c = jax.random.dirichlet(jax.random.fold_in(_rk, 511), 0.3 * jnp.ones((16,), jnp.float32), (4, 64))
        _ctx_1024t = jnp.einsum('bsk,bkd->bsd', _ctx_1024c, _ctx_1024P)
        _ctx_1024t = _ctx_1024t * jax.lax.rsqrt(jnp.mean(jnp.square(_ctx_1024t)) + 1e-12) * 0.953939
        ctx_1024 = -1.39393e-06 + 0.999914 * (_ctx_1024t + 0.3 * jax.random.normal(jax.random.fold_in(_rk, 611), (4, 64, 256), jnp.float32))
        _g = jax.random.normal(jax.random.fold_in(_rk, 9001), (2, 2), jnp.float32)
        _g = jnp.sign(_g) * jnp.maximum(jnp.abs(_g), 1.0) + (_g == 0) * 1.0
        g_xattn = _g[0]
        g_ffn = _g[1]
        return (x, ctx_1024, g_xattn, g_ffn)
    x, ctx_1024, g_xattn, g_ffn = _rec_inputs()

    def _L0_xattn_setup():
        import jax, jax.numpy as jnp
        import numpy as np
        EMBED_DIM = 256
        NUM_HEADS = 16
        HEAD_DIM = EMBED_DIM // NUM_HEADS
        key = jax.random.key(seed)
        ks = jax.random.split(key, 7)
        B, S, E = (2, 512, EMBED_DIM)
        bound = float(np.sqrt(6.0 / (E + E)))
        mkw = lambda k: jax.random.uniform(k, (E, E), jnp.float32, -bound, bound)
        return {'query': jax.random.normal(ks[0], (B, S, E), jnp.float32), 'key': jax.random.normal(ks[1], (B, S, E), jnp.float32), 'value': jax.random.normal(ks[2], (B, S, E), jnp.float32), 'Wq': mkw(ks[3]), 'Wk': mkw(ks[4]), 'Wv': mkw(ks[5]), 'Wo': mkw(ks[6])}
    _L0_xattn_all = _L0_xattn_setup()
    _L0_xattn_in = {k: v for k, v in _L0_xattn_all.items() if k in ('Wq', 'Wk', 'Wv', 'Wo')}
    del _L0_xattn_all

    def _L0_ffn_setup():
        import jax, jax.numpy as jnp
        import numpy as np
        TOP_K = 2
        key = jax.random.key(seed)
        ks = jax.random.split(key, 6)
        B, S, H, F, E = (4, 512, 256, 1024, 8)
        x = jax.random.normal(ks[0], (B, S, H), dtype=jnp.float32)
        gate_w = jax.random.normal(ks[1], (E, H), dtype=jnp.float32) * 0.02
        W1 = jax.random.normal(ks[2], (E, H, F), dtype=jnp.float32) * (1.0 / np.sqrt(H))
        b1 = jnp.zeros((E, F), dtype=jnp.float32)
        W2 = jax.random.normal(ks[3], (E, F, H), dtype=jnp.float32) * (1.0 / np.sqrt(F))
        b2 = jnp.zeros((E, H), dtype=jnp.float32)
        sW1 = jax.random.normal(ks[4], (H, F), dtype=jnp.float32) * (1.0 / np.sqrt(H))
        sb1 = jnp.zeros((F,), dtype=jnp.float32)
        sW2 = jax.random.normal(ks[5], (F, H), dtype=jnp.float32) * (1.0 / np.sqrt(F))
        sb2 = jnp.zeros((H,), dtype=jnp.float32)
        return {'x': x, 'gate_w': gate_w, 'W1': W1, 'b1': b1, 'W2': W2, 'b2': b2, 'sW1': sW1, 'sb1': sb1, 'sW2': sW2, 'sb2': sb2}
    _L0_ffn_all = _L0_ffn_setup()
    _L0_ffn_in = {k: v for k, v in _L0_ffn_all.items() if k in ('gate_w', 'W1', 'b1', 'W2', 'b2', 'sW1', 'sb1', 'sW2', 'sb2')}
    del _L0_ffn_all

    def _L1_xattn_setup():
        import jax, jax.numpy as jnp
        import numpy as np
        D_MODEL = 256
        N_HEADS = 16
        D_HEAD = D_MODEL // N_HEADS
        LN_EPS = 1e-05

        def layer_norm(x, gamma, beta):
            mu = jnp.mean(x, axis=-1, keepdims=True)
            var = jnp.mean(jnp.square(x - mu), axis=-1, keepdims=True)
            return (x - mu) * jax.lax.rsqrt(var + LN_EPS) * gamma + beta
        key = jax.random.key(seed)
        ks = jax.random.split(key, 8)
        B, T = (4, 512)
        s = 1.0 / np.sqrt(D_MODEL)
        return {'encoder_seq': jax.random.normal(ks[0], (B, T, D_MODEL), jnp.float32), 'decoder_seq': jax.random.normal(ks[1], (B, T, D_MODEL), jnp.float32), 'Wq': jax.random.normal(ks[2], (D_MODEL, D_MODEL), jnp.float32) * s, 'bq': jnp.zeros((D_MODEL,), jnp.float32), 'Wk': jax.random.normal(ks[3], (D_MODEL, D_MODEL), jnp.float32) * s, 'bk': jnp.zeros((D_MODEL,), jnp.float32), 'Wv': jax.random.normal(ks[4], (D_MODEL, D_MODEL), jnp.float32) * s, 'bv': jnp.zeros((D_MODEL,), jnp.float32), 'ln_gamma': jnp.ones((D_MODEL,), jnp.float32), 'ln_beta': jnp.zeros((D_MODEL,), jnp.float32)}
    _L1_xattn_all = _L1_xattn_setup()
    _L1_xattn_in = {k: v for k, v in _L1_xattn_all.items() if k in ('Wq', 'bq', 'Wk', 'bk', 'Wv', 'bv', 'ln_gamma', 'ln_beta')}
    del _L1_xattn_all

    def _L1_ffn_setup():
        import jax, jax.numpy as jnp
        import numpy as np
        DIM, E, K, H = (256, 8, 2, 1024)
        key = jax.random.key(seed)
        ks = jax.random.split(key, 5)
        s_in = 1.0 / np.sqrt(DIM)
        s_h = 1.0 / np.sqrt(H)
        return {'x': jax.random.normal(ks[0], (4, 512, DIM), dtype=jnp.float32), 'Wr': jax.random.normal(ks[1], (DIM, E), dtype=jnp.float32) * s_in, 'W1': jax.random.normal(ks[2], (E, DIM, H), dtype=jnp.float32) * s_in, 'b1': jnp.zeros((E, H), dtype=jnp.float32), 'W2': jax.random.normal(ks[3], (E, H, DIM), dtype=jnp.float32) * s_h, 'b2': jnp.zeros((E, DIM), dtype=jnp.float32)}
    _L1_ffn_all = _L1_ffn_setup()
    _L1_ffn_in = {k: v for k, v in _L1_ffn_all.items() if k in ('Wr', 'W1', 'b1', 'W2', 'b2')}
    del _L1_ffn_all
    return {'x': x, 'ctx_1024': ctx_1024, 'g_xattn': g_xattn, 'g_ffn': g_ffn, 'L0_xattn_Wq': _L0_xattn_in['Wq'], 'L0_xattn_Wk': _L0_xattn_in['Wk'], 'L0_xattn_Wv': _L0_xattn_in['Wv'], 'L0_xattn_Wo': _L0_xattn_in['Wo'], 'L0_ffn_gate_w': _L0_ffn_in['gate_w'], 'L0_ffn_W1': _L0_ffn_in['W1'], 'L0_ffn_b1': _L0_ffn_in['b1'], 'L0_ffn_W2': _L0_ffn_in['W2'], 'L0_ffn_b2': _L0_ffn_in['b2'], 'L0_ffn_sW1': _L0_ffn_in['sW1'], 'L0_ffn_sb1': _L0_ffn_in['sb1'], 'L0_ffn_sW2': _L0_ffn_in['sW2'], 'L0_ffn_sb2': _L0_ffn_in['sb2'], 'L1_xattn_Wq': _L1_xattn_in['Wq'], 'L1_xattn_bq': _L1_xattn_in['bq'], 'L1_xattn_Wk': _L1_xattn_in['Wk'], 'L1_xattn_bk': _L1_xattn_in['bk'], 'L1_xattn_Wv': _L1_xattn_in['Wv'], 'L1_xattn_bv': _L1_xattn_in['bv'], 'L1_xattn_ln_gamma': _L1_xattn_in['ln_gamma'], 'L1_xattn_ln_beta': _L1_xattn_in['ln_beta'], 'L1_ffn_Wr': _L1_ffn_in['Wr'], 'L1_ffn_W1': _L1_ffn_in['W1'], 'L1_ffn_b1': _L1_ffn_in['b1'], 'L1_ffn_W2': _L1_ffn_in['W2'], 'L1_ffn_b2': _L1_ffn_in['b2']}

def reference(x, ctx_1024, g_xattn, g_ffn, L0_xattn_Wq, L0_xattn_Wk, L0_xattn_Wv, L0_xattn_Wo, L0_ffn_gate_w, L0_ffn_W1, L0_ffn_b1, L0_ffn_W2, L0_ffn_b2, L0_ffn_sW1, L0_ffn_sb1, L0_ffn_sW2, L0_ffn_sb2, L1_xattn_Wq, L1_xattn_bq, L1_xattn_Wk, L1_xattn_bk, L1_xattn_Wv, L1_xattn_bv, L1_xattn_ln_gamma, L1_xattn_ln_beta, L1_ffn_Wr, L1_ffn_W1, L1_ffn_b1, L1_ffn_W2, L1_ffn_b2):
    import jax
    import jax.numpy as jnp

    def _L0_xattn_ref(query, key, value, Wq, Wk, Wv, Wo):
        import jax, jax.numpy as jnp
        import numpy as np
        EMBED_DIM = 256
        NUM_HEADS = 16
        HEAD_DIM = EMBED_DIM // NUM_HEADS
        B, L, E = query.shape
        H, D = (NUM_HEADS, HEAD_DIM)
        scale = D ** (-0.5)
        q = (query @ Wq.T).reshape(B, L, H, D) * scale
        k = (key @ Wk.T).reshape(B, -1, H, D)
        v = (value @ Wv.T).reshape(B, -1, H, D)
        scores = jax.nn.sigmoid(jnp.einsum('blhd,bshd->bhls', q, k))
        o = jnp.einsum('bhls,bshd->blhd', scores, v).reshape(B, L, E)
        return o @ Wo.T

    def _L0_ffn_ref(x, gate_w, W1, b1, W2, b2, sW1, sb1, sW2, sb2):
        import jax, jax.numpy as jnp
        import numpy as np
        TOP_K = 2
        B, S, H = x.shape
        E = gate_w.shape[0]
        x_flat = x.reshape(-1, H)
        logits = x_flat @ gate_w.T
        probs = jax.nn.softmax(logits.astype(jnp.float32), axis=-1)
        top_w, sel = jax.lax.top_k(probs, TOP_K)
        top_w = top_w / jnp.sum(top_w, axis=-1, keepdims=True)
        combine = jnp.sum(jax.nn.one_hot(sel, E, dtype=top_w.dtype) * top_w[..., None], axis=1)
        combine = combine.astype(x.dtype)
        h = jax.nn.gelu(jnp.einsum('th,ehf->tef', x_flat, W1) + b1[None], approximate=False)
        y = jnp.einsum('tef,efh->teh', h, W2) + b2[None]
        out = jnp.einsum('teh,te->th', y, combine)
        sh = jax.nn.gelu(x_flat @ sW1 + sb1, approximate=False)
        out = out + sh @ sW2 + sb2
        return out.reshape(B, S, H)

    def _L1_xattn_ref(encoder_seq, decoder_seq, Wq, bq, Wk, bk, Wv, bv, ln_gamma, ln_beta):
        import jax, jax.numpy as jnp
        import numpy as np
        D_MODEL = 256
        N_HEADS = 16
        D_HEAD = D_MODEL // N_HEADS
        LN_EPS = 1e-05

        def layer_norm(x, gamma, beta):
            mu = jnp.mean(x, axis=-1, keepdims=True)
            var = jnp.mean(jnp.square(x - mu), axis=-1, keepdims=True)
            return (x - mu) * jax.lax.rsqrt(var + LN_EPS) * gamma + beta
        B, T_dec, _ = decoder_seq.shape
        T_enc = encoder_seq.shape[1]
        q = (decoder_seq @ Wq.T + bq).reshape(B, T_dec, N_HEADS, D_HEAD)
        k = (encoder_seq @ Wk.T + bk).reshape(B, T_enc, N_HEADS, D_HEAD)
        v = (encoder_seq @ Wv.T + bv).reshape(B, T_enc, N_HEADS, D_HEAD)
        scale = 1.0 / np.sqrt(D_HEAD)
        kv = jnp.einsum('bthd,bthe->bhde', k, v)
        att = jnp.einsum('bqhd,bhde->bqhe', q, kv) * scale
        att = att.reshape(B, T_dec, D_MODEL)
        return layer_norm(att + decoder_seq, ln_gamma, ln_beta)

    def _L1_ffn_ref(x, Wr, W1, b1, W2, b2):
        import jax, jax.numpy as jnp
        import numpy as np
        DIM, E, K, H = (256, 8, 2, 1024)
        batch, seq, dim = x.shape
        x_flat = x.reshape(-1, dim)
        logits = x_flat @ Wr
        w, ind = jax.lax.top_k(logits, K)
        w = jax.nn.softmax(w, axis=-1)
        combine = jnp.einsum('tke,tk->te', jax.nn.one_hot(ind, E, dtype=x.dtype), w)

        def body(acc, params):
            W1e, b1e, W2e, b2e, ce = params
            h = jax.nn.gelu(x_flat @ W1e + b1e, approximate=False)
            y = h @ W2e + b2e
            return (acc + ce[:, None] * y, None)
        out0 = jnp.zeros_like(x_flat)
        out, _ = jax.lax.scan(body, out0, (W1, b1, W2, b2, combine.T))
        return out.reshape(batch, seq, dim)
    x = x + jnp.tanh(g_xattn[0]) * _L0_xattn_ref(_layernorm(x, axis=-1), ctx_1024, ctx_1024, L0_xattn_Wq, L0_xattn_Wk, L0_xattn_Wv, L0_xattn_Wo)
    x = x + jnp.tanh(g_ffn[0]) * _L0_ffn_ref(_layernorm(x, axis=-1), L0_ffn_gate_w, L0_ffn_W1, L0_ffn_b1, L0_ffn_W2, L0_ffn_b2, L0_ffn_sW1, L0_ffn_sb1, L0_ffn_sW2, L0_ffn_sb2)
    x = x + jnp.tanh(g_xattn[1]) * _L1_xattn_ref(ctx_1024, _layernorm(x, axis=-1), L1_xattn_Wq, L1_xattn_bq, L1_xattn_Wk, L1_xattn_bk, L1_xattn_Wv, L1_xattn_bv, L1_xattn_ln_gamma, L1_xattn_ln_beta)
    x = x + jnp.tanh(g_ffn[1]) * _L1_ffn_ref(_layernorm(x, axis=-1), L1_ffn_Wr, L1_ffn_W1, L1_ffn_b1, L1_ffn_W2, L1_ffn_b2)
    return x

_drawn_inputs = setup_inputs


def setup_inputs(seed=0):
    import zlib

    import numpy as np

    out = dict(_drawn_inputs(seed))
    spreads = {'g_ffn': (-1.0, 0.6),
     'L0_ffn_b1': (0.0, 2.0),
     'L0_ffn_b2': (0.0, 0.8),
     'L0_ffn_sb1': (0.0, 0.8),
     'L0_ffn_sb2': (0.0, 0.8),
     'L1_xattn_bq': (0.0, 0.8),
     'L1_xattn_bk': (0.0, 0.8),
     'L1_xattn_bv': (0.0, 0.791),
     'L1_xattn_ln_gamma': (1.0, 0.6),
     'L1_xattn_ln_beta': (0.0, 0.8),
     'L1_ffn_b1': (0.0, 2.0),
     'L1_ffn_b2': (0.0, 0.8)}
    factors = {}
    for name, (base, spread) in spreads.items():
        noise = np.random.default_rng([zlib.crc32(name.encode()), seed]).standard_normal(out[name].shape)
        drawn = base * np.exp(spread * noise) if base else spread * noise
        out[name] = jnp.asarray(drawn.astype(out[name].dtype))
    for name, factor in factors.items():
        out[name] = (out[name] * factor).astype(out[name].dtype)
    return out
```

```python
from contextlib import ExitStack

import numpy as np
import concourse.bass as bass
from concourse import mybir

F32 = mybir.dt.float32
F16 = mybir.dt.float16
BF16 = mybir.dt.bfloat16
I32 = mybir.dt.int32
ACT = mybir.ActivationFunctionType
ALU = mybir.AluOpType
AX = mybir.AxisListType.X

P = 128
B, S, D = 4, 512, 256
SC, H, DH = 64, 16, 16
E, F = 8, 1024
T = B * S
TT = T // P
TB = S // P
DC = D // P
FC = F // P
HP = H // 2
SHARED = E
ROUTED = (2 * T + E * (P - 1)) // P
W_SCALE = 64.0
ROW = 2 * D + 8
M_W2, M_DW, M_TOK, M_E1 = range(4)
EPS = 1e-5
SLOT = 4 * 2048


def constants():
    p = np.arange(P)
    c = {}
    c["before"] = (p[:, None] < p[None, :]) * 1.0
    c["vmask"] = ((np.arange(D)[None, :] // DH) % 2 == (p[:, None] // SC)) * 1.0
    c["kvmask"] = (p[:, None] // DH == p[None, :] // DH) * (float(DH) ** -0.5)
    c["kmask"] = ((p[:, None] // DH) % 2 == np.arange(2)[None, :]) * 1.0
    c["ident"] = np.eye(P)
    c["rev"] = np.broadcast_to(E - np.arange(E), (P, E))
    c["upto"] = np.broadcast_to((np.arange(E)[None, :] <= np.arange(E)[:, None]).reshape(-1), (P, E * E))
    c["full"] = np.broadcast_to(P * np.arange(TT), (P, TT))
    c["tile"] = np.broadcast_to(np.arange(ROUTED), (P, ROUTED))
    c["token"] = p[:, None] + P * np.arange(TT)[None, :]
    c["trash"] = T + p[:, None]
    at, where = 0, {}
    for k, v in c.items():
        where[k] = (at, v.shape[1])
        at += v.shape[1]
    return np.concatenate(list(c.values()), axis=1).astype(np.float32), where


CONST, WHERE = constants()
EARLY = WHERE["ident"][0]
NAMES = ["x", "ctx_1024", "g_xattn", "g_ffn", "L0_xattn_Wq", "L0_xattn_Wk", "L0_xattn_Wv", "L0_xattn_Wo",
         "L0_ffn_gate_w", "L0_ffn_W1", "L0_ffn_b1", "L0_ffn_W2", "L0_ffn_b2", "L0_ffn_sW1", "L0_ffn_sb1",
         "L0_ffn_sW2", "L0_ffn_sb2", "L1_xattn_Wq", "L1_xattn_bq", "L1_xattn_Wk", "L1_xattn_bk", "L1_xattn_Wv",
         "L1_xattn_bv", "L1_xattn_ln_gamma", "L1_xattn_ln_beta", "L1_ffn_Wr", "L1_ffn_W1", "L1_ffn_b1",
         "L1_ffn_W2", "L1_ffn_b2"]


def build(nc, a, const, out):
    with ExitStack() as ctx:
        def sb(name, shape, dt):
            return ctx.enter_context(nc.sbuf_tensor(name, shape, dt))

        def sem(name):
            return ctx.enter_context(nc.semaphore(name))

        def dram(name, shape, dt):
            return nc.dram_tensor(name, shape, dt, kind="Internal").ap()

        shared_tiles = [TT, 0]
        tiles = [shared_tiles[n] + ROUTED for n in range(2)]
        sorted_rows = [dram(f"sorted_rows{n}", [(tiles[n] + 1) * P, ROW // 2], I32) for n in range(2)]
        x_sum = [dram(f"x_sum{n}", [T + P, D], F32) for n in range(2)]
        kv_dram = dram("kv_dram", [P, B * DC * D], F32)
        kv_bias_dram = dram("kv_bias_dram", [P, B * D], F32)

        weights = sb("weights", [P, E + 1, SLOT], F16)
        raw = sb("raw", [P, 2, 1024], F32)
        const_sb = sb("const_sb", [P, CONST.shape[1] - EARLY], F32)
        const_early = weights[:, 3, :].bitcast(F32)[:, 2560:2560 + EARLY]

        def cst(name):
            at, n = WHERE[name]
            return const_early[:, at:at + n] if at < EARLY else const_sb[:, at - EARLY:at - EARLY + n]

        ident = cst("ident")
        ident16 = sb("ident16", [P, P], F16)
        before16 = sb("before16", [P, P], BF16)
        ones16 = sb("ones16", [P, P], BF16)
        gates = sb("gates", [P, 4], F32)
        b1_cols = [sb(f"b1_cols{n}", [P, FC, E + 1 - n], F32) for n in range(2)]
        gate_cols = sb("gate_cols", [P, 2, DC, E], F32)
        padding_row = sb("padding_row", [P, ROW], F16)
        ln_stats = sb("ln_stats", [P, TB, 6], F32)
        ln_mv = sb("ln_mv", [P, TB, 2], F32)
        ln_rstd = sb("ln_rstd", [P, TB], F32)
        minus_half = sb("minus_half", [P, TB], F32)
        lg = sb("lg", [P, TT, E], F32)
        r_a = sb("r_a", [P, TT, E], F32)
        pick = [sb(f"pick{k}", [P, TT, E], F32) for k in range(2)]
        picked16 = sb("picked16", [P, TT + 1, E], BF16)
        top = [sb(f"top{k}", [P, TT], F32) for k in range(2)]
        order = [sb(f"order{k}", [P, TT], F32) for k in range(2)]
        gate_w = [sb(f"gate_w{k}", [P, TT], F32) for k in range(2)]
        place = [sb(f"place{k}", [P, TT], I32) for k in range(2)]
        n_tiles = sb("n_tiles", [P, E], F32)
        end_tile = sb("end_tile", [P, E], F32)
        base_row = sb("base_row", [P, E], F32)
        tile_expert = sb("tile_expert", [P, tiles[0]], F32)
        tile_expert_i = sb("tile_expert_i", [P, tiles[0]], I32)
        meta = sb("meta", [P, 2, 4], F32)
        pick_w = sb("pick_w", [P, 2], F32)

        x_arena = sb("x_arena", [P, TT * D], F32)
        x_sb = x_arena[:, :].rearrange("p (t d) -> p t d", t=TT)
        rows_in = x_arena[:, 0:ROW].bitcast(F16).rearrange("p (k r) -> p k r", k=2)
        rows_in_words = x_arena[:, 0:ROW].bitcast(I32).rearrange("p (k r) -> p k r", k=2)
        xT = x_arena[:, ROW:ROW + 512].bitcast(F16).rearrange("p (k r) -> p k r", k=2)
        y_sb = x_arena[:, ROW + 512:ROW + 1024].rearrange("p (k d) -> p k d", k=2)
        b2_at = ROW + 1024
        b2_rows = x_arena[:, b2_at:b2_at + (E + 1) * D].rearrange("p (e d) -> p e d", e=E + 1)
        work = sb("work", [P, 4096], F32)
        xln = work[:, 0:2048].rearrange("p (k t d) -> p k t d", k=2, t=TB)
        xlnT = work[:, 2048:4096].rearrange("p (k c s) -> p k c s", k=2, c=DC)
        hid = work[:, 0:2048].rearrange("p (k f) -> p k f", k=2)
        hid_hi = work[:, 2048:3072].bitcast(F16).rearrange("p (k f) -> p k f", k=2)
        hid_lo = work[:, 3072:4096].bitcast(F16).rearrange("p (k f) -> p k f", k=2)
        row_arena = sb("row_arena", [P, TT * ROW // 2], F32)
        rows_out = row_arena[:, :].bitcast(F16).rearrange("p (t r) -> p t r", t=TT)
        row_words = row_arena[:, :].bitcast(I32).rearrange("p (t r) -> p t r", t=TT)
        rows_meta = row_arena[:, :].rearrange("p (t r) -> p t r", t=TT)[:, :, D:D + 4]
        k_heads = row_arena[:, 0:1024].rearrange("p (c b m) -> p c b m", c=DC, b=B)
        v_heads = row_arena[:, 1024:2048].rearrange("p (b d) -> p b d", b=B)
        ctx_in = row_arena[:, 2048:2560].rearrange("p (t d) -> p t d", t=2)
        ctxT = row_arena[:, 2560:3072].rearrange("p (c s) -> p c s", c=DC)
        ctxT2 = row_arena[:, 3072:4096].rearrange("p (c b m) -> p c b m", c=DC, b=B)
        att = weights[:, 6:8, :].rearrange("p e w -> p (e w)").bitcast(F32)
        probs = att[:, 0:4096].rearrange("p (h s) -> p h s", h=HP)
        wT = att[:, 4096:6144].rearrange("p (w c o) -> p w c o", w=4, c=DC)
        qT = att[:, 6144:7168].rearrange("p (c s) -> p c s", c=DC)
        oT = att[:, 7168:8192].rearrange("p (c s) -> p c s", c=DC)
        pre = weights[:, 4:6, :].rearrange("p e w -> p (e w)").bitcast(F32)
        w_in = pre[:, 0:3584].rearrange("p (w c i) -> p w c i", w=7, c=DC)
        wT1 = pre[:, 3584:4608].rearrange("p (w c o) -> p w c o", w=2, c=DC)
        kv1 = pre[:, 4608:5632].rearrange("p (w t d) -> p w t d", w=2, t=2)
        kv1_bias = pre[:, 5632:6144].rearrange("p (w d) -> p w d", w=2)
        kv_block = pre[:, 6144:7168].rearrange("p (b c e) -> p b c e", b=B, c=DC)
        bq_wide = pre[:, 7168:7424].rearrange("p (c m) -> p c m", c=DC)
        b1_in = pre[:, 7424:8192]
        few = weights[0:16, 3, :].bitcast(F32)
        b1_rows = [few[0:E + 1, 0:F], few[0:E, F:2 * F]]
        gate_rows = few[0:E, 2 * F:2 * F + D]
        bq_rows = few[0:DC, 2 * F + D:2 * F + D + P]
        kv_out = weights[:, 2, :].bitcast(F32)
        kvm_out = kv_out[:, 0:2048]
        kvb_out = kv_out[:, 2048:3072]
        late = weights[:, SHARED, :].bitcast(F32)
        kvm = late[:, 0:2048].rearrange("p (b c e) -> p b c e", b=B, c=DC)
        kvb = late[:, 2048:3072].rearrange("p (b d) -> p b d", b=B)
        gamma = late[:, 3072:3328]
        beta = late[:, 3328:3584]

        bank = [ctx.enter_context(nc.psum_tensor(f"bank{i}", [P, 512], F32)) for i in range(8)]
        tp_ps, q_ps, s_ps, p_ps = bank[0:2], bank[2:4], bank[4:6], bank[6:8]
        xT_ps = [bank[k][:, 0:256].bitcast(F16) for k in range(2)]
        h_ps = [bank[2:4], bank[4:6]]
        y_ps = [bank[6 + k][:, 0:D] for k in range(2)]

        in_const, in_ctx, in_w, in_few, in_bias = (sem(n) for n in ("in_const", "in_ctx", "in_w", "in_few", "in_bias"))
        in_x = [sem(f"in_x{b}") for b in range(B)]
        in_raw = [sem(f"in_raw{k}") for k in range(2)]
        padded = sem("padded")
        pad_ready = sem("pad_ready")
        consts_ready = sem("consts_ready")
        g_ready = sem("g_ready")
        var_ready, rstd_ready = sem("var_ready"), sem("rstd_ready")
        dve_step = sem("dve_step")
        pe_setup, dve_setup, act_setup = sem("pe_setup"), sem("dve_setup"), sem("act_setup")
        kv_stored = sem("kv_stored")
        ln_done, tp_done, xlnT_ready, xlnT_used = sem("ln_done"), sem("tp_done"), sem("xlnT_ready"), sem("xlnT_used")
        q_done, q_ready = sem("q_done"), sem("q_ready")
        score_done, prob_ready = sem("score_done"), sem("prob_ready")
        o_done, o_ready = sem("o_done"), sem("o_ready")
        proj_done, x_updated = sem("proj_done"), sem("x_updated")
        split_hi, split_lo = sem("split_hi"), sem("split_lo")
        late_in = sem("late_in")
        logits_done = sem("logits_done")
        diff_ready, sig_ready = sem("diff_ready"), sem("sig_ready")
        picked_ready, count_done, routed = sem("picked_ready"), sem("count_done"), sem("routed")
        rows_ready = sem("rows_ready")
        x_stored = [sem(f"x_stored{n}") for n in range(2)]
        shared_stored = sem("shared_stored")
        scattered = [sem(f"scattered{n}") for n in range(2)]
        b2_in = [sem(f"b2_in{n}") for n in range(2)]
        x_back = [sem(f"x_back{b}") for b in range(B)]
        out_stored = sem("out_stored")

        def per_layer(name):
            return [sem(f"{name}_{n}") for n in range(2)]

        row_in = [per_layer(f"row_in{k}") for k in range(2)]
        meta_in = [per_layer(f"meta_in{k}") for k in range(2)]
        rowT_done, xT_ready = per_layer("rowT_done"), per_layer("xT_ready")
        up_done, hi_done = per_layer("up_done"), per_layer("hi_done")
        gelu_done = [per_layer(f"gelu_done_half{h}") for h in range(2)]
        hid_ready = [per_layer(f"hid_ready_half{h}") for h in range(2)]
        turn_taken = per_layer("turn_taken")
        down_done, biased, weighed, y_ready, added = (per_layer(n) for n in ("down_done", "biased", "weighed", "y_ready", "added"))

        block = ctx.enter_context(nc.Block())

        unit_count = [2 * 2 * (E + 1), 2 * 2 * E]

        def unit(n, u):
            e, m, half = u // 4, (u // 2) % 2, u % 2
            if n == 0:
                e = (SHARED, *range(E))[e]
            return e, m, half

        def split_to(n, u, low):
            e, m, half = unit(n, u)
            at = 4096 * m + 2048 * low + 1024 * half
            return weights[:, e, at:at + 1024]

        def unit_no(n, u):
            return u + (unit_count[0] if n else 0)

        def w1_part(e, low, c, f):
            at = 2048 * low + 1024 * c + P * f
            return weights[:, bass.ds(e, 1), at:at + P].rearrange("p a b -> p (a b)")

        def w2_part(e, low, f):
            at = 4096 + 2048 * low + D * f
            return weights[:, bass.ds(e, 1), at:at + D].rearrange("p a b -> p (a b)")

        def tile_loop(eng, n, body):
            count = tiles[n]
            assert count % 2 == 1
            body(0, 0, 0)
            body(1, 0, 1)
            with eng.Fori(0, (count - 3) // 2) as t:
                body(2 * t + 2, t + 1, 0)
                body(2 * t + 3, t + 1, 1)
            body(count - 1, (count - 1) // 2, 0)

        def at_least(j, n):
            return j >= n if isinstance(j, int) else True

        def before_end(j, n, ahead):
            return j + ahead < tiles[n] if isinstance(j, int) else True

        def attend0_src(w):
            return a[("L0_xattn_Wq", "L0_xattn_Wk", "L0_xattn_Wv", "L0_xattn_Wo", "L1_xattn_Wq", "L1_xattn_Wk",
                      "L1_xattn_Wv")[w]]

        x_rows = a["x"].rearrange("b s d -> (b s) d")

        def batch_of(rows, b):
            return rows[b * S:(b + 1) * S, :].rearrange("(t p) d -> p t d", p=P)

        @block.sync
        def _(sp):
            sp.dma_start(const_sb[:, :], const[:, EARLY:]).then_inc(in_const, 16)
            sp.dma_start(const_early, const[:, 0:EARLY]).then_inc(in_const, 16)
            sp.dma_start(ctx_in[:, :, :], a["ctx_1024"].rearrange("b s d -> (b s) d").rearrange("(t p) d -> p t d", p=P)).then_inc(in_ctx, 16)
            for w in range(7):
                sp.dma_start(w_in[:, w, :, :], attend0_src(w).rearrange("(c p) i -> p c i", p=P)).then_inc(in_w, 16)
            sp.dma_start(few[0:E, 0:F], a["L0_ffn_b1"]).then_inc(in_few, 16)
            sp.dma_start(few[E:E + 1, 0:F], a["L0_ffn_sb1"].rearrange("(a f) -> a f", a=1)).then_inc(in_few, 16)
            sp.dma_start(few[0:E, F:2 * F], a["L1_ffn_b1"]).then_inc(in_few, 16)
            sp.dma_start(gate_rows, a["L0_ffn_gate_w"]).then_inc(in_few, 16)
            sp.dma_start(gate_cols[:, 1, :, :], a["L1_ffn_Wr"].rearrange("(c p) e -> p c e", p=P)).then_inc(in_few, 16)
            sp.dma_start(bq_rows, a["L1_xattn_bq"].rearrange("(c p) -> c p", p=P)).then_inc(in_few, 16)
            sp.dma_start(kv1_bias[:, 0, :], a["L1_xattn_bk"].partition_broadcast(P)).then_inc(in_bias, 16)
            sp.dma_start(kv1_bias[:, 1, :], a["L1_xattn_bv"].partition_broadcast(P)).then_inc(in_bias, 16)
            sp.dma_start(gates[:, 0:2], a["g_xattn"].partition_broadcast(P)).then_inc(in_bias, 16)
            sp.dma_start(gates[:, 2:4], a["g_ffn"].partition_broadcast(P)).then_inc(in_bias, 16)
            for b in range(B):
                sp.dma_start(x_sb[:, TB * b:TB * b + TB, :], batch_of(x_rows, b)).then_inc(in_x[b], 16)

            def load_unit(n, u):
                k = unit_no(n, u)
                if k >= 2:
                    sp.wait_ge(split_lo, k - 1)
                e, m, half = unit(n, u)
                if e == SHARED:
                    src = (a["L0_ffn_sW1"], a["L0_ffn_sW2"])[m]
                else:
                    src = a[f"L{n}_ffn_W{m + 1}"][e, :, :]
                if m == 0:
                    sp.dma_start(raw[:, k % 2, :], src[half * P:half * P + P, :]).then_inc(in_raw[k % 2], 16)
                else:
                    sp.dma_start(raw[:, k % 2, :].rearrange("p (f d) -> p f d", f=FC // 2),
                                 src[half * F // 2:(half + 1) * F // 2, :].rearrange("(f p) d -> p f d", p=P))\
                      .then_inc(in_raw[k % 2], 16)

            def store_kv():
                sp.wait_ge(act_setup, 5)
                sp.wait_ge(dve_setup, 9)
                sp.dma_start(kv_dram, kvm_out).then_inc(kv_stored, 16)
                sp.dma_start(kv_bias_dram, kvb_out).then_inc(kv_stored, 16)

            for u in range(2):
                load_unit(0, u)
            sp.wait_ge(pad_ready, 1)
            for n in range(2):
                sp.dma_start(sorted_rows[n][shared_tiles[n] * P:(tiles[n] + 1) * P, :].rearrange("(j p) r -> p j r", p=P),
                             padding_row[:, :].bitcast(I32).unsqueeze(1).broadcast_to([P, ROUTED + 1, ROW // 2])).then_inc(padded, 16)
                sp.dma_start(x_sum[n][T:T + P, :], padding_row[:, 0:2 * D].bitcast(F32)).then_inc(padded, 16)
            store_kv()
            for u in range(2, unit_count[0]):
                load_unit(0, u)

            def after_routing(n):
                for b in range(B):
                    sp.wait_ge(x_updated, 4 * B * n + TB * (b + 1))
                    sp.dma_start(batch_of(x_sum[n], b), x_sb[:, TB * b:TB * b + TB, :]).then_inc(x_stored[n], 16)
                if n == 0:
                    sp.wait_ge(rows_ready, 1)
                    sp.dma_start(sorted_rows[0][0:T, :].rearrange("(t p) r -> p t r", p=P), row_words).then_inc(shared_stored, 16)
                    sp.wait_ge(shared_stored, 16)
                sp.wait_ge(x_stored[n], 16 * B)
                sp.wait_ge(ln_done, 8 * (n + 1))
                if n == 0:
                    sp.dma_start(b2_rows[:, 0:E, :], a["L0_ffn_b2"].partition_broadcast(P)).then_inc(b2_in[0], 16)
                    sp.dma_start(b2_rows[:, E, :], a["L0_ffn_sb2"].partition_broadcast(P)).then_inc(b2_in[0], 16)
                else:
                    sp.dma_start(b2_rows[:, 0:E, :], a["L1_ffn_b2"].partition_broadcast(P)).then_inc(b2_in[1], 16)

            def ffn_loads(n):
                def rows(j, q, k):
                    sp.dma_start(rows_in_words[:, k, :], sorted_rows[n][bass.ds(j * P, P), :]).then_inc(row_in[k][n], 16)

                def body(j, q, k):
                    if at_least(j, 2):
                        sp.wait_ge(added[n], 16 * (j - 1))
                    sp.dma_start(meta[:, k, :].bitcast(I32), sorted_rows[n][bass.ds(j * P, P), D:ROW // 2]).then_inc(meta_in[k][n], 16)
                    if before_end(j, n, 2):
                        sp.wait_ge(rowT_done[n], j + 1)
                        rows(j + 2, q + 1, k)

                if not shared_tiles[n]:
                    sp.wait_ge(scattered[n], 2 * TT * 16)
                rows(0, 0, 0)
                rows(1, 0, 1)
                if shared_tiles[n]:
                    sp.wait_ge(scattered[n], 2 * TT * 16)
                tile_loop(sp, n, body)
                sp.wait_ge(row_in[1][n], 16 * ((tiles[n] + 1) // 2))

            after_routing(0)
            ffn_loads(0)
            sp.wait_ge(added[0], 16 * tiles[0])
            for b in range(B):
                sp.dma_start(x_sb[:, TB * b:TB * b + TB, :], batch_of(x_sum[0], b)).then_inc(x_back[b], 16)
            sp.wait_ge(down_done[0], tiles[0])
            sp.wait_ge(kv_stored, 32)
            sp.dma_start(kvm.rearrange("p b c e -> p (b c e)"), kv_dram).then_inc(late_in, 16)
            sp.dma_start(kvb.rearrange("p b d -> p (b d)"), kv_bias_dram).then_inc(late_in, 16)
            sp.dma_start(gamma, a["L1_xattn_ln_gamma"].partition_broadcast(P)).then_inc(late_in, 16)
            sp.dma_start(beta, a["L1_xattn_ln_beta"].partition_broadcast(P)).then_inc(late_in, 16)
            for u in range(unit_count[1]):
                load_unit(1, u)
            after_routing(1)
            ffn_loads(1)
            sp.wait_ge(added[1], 16 * tiles[1])
            sp.dma_start(out.rearrange("b s d -> (b s) d"), x_sum[1][0:T, :]).then_inc(out_stored, 16)
            sp.wait_ge(out_stored, 16)

        @block.gpsimd
        def _(pool):
            nc.gpsimd.memset(padding_row[:, 0:2 * D + 8], 0.0).then_inc(consts_ready, 1)
            nc.gpsimd.memset(ones16[:, :], 1.0).then_inc(consts_ready, 1)
            nc.gpsimd.memset(picked16[:, TT, :], 0.0).then_inc(consts_ready, 1)
            nc.gpsimd.memset(minus_half[:, :], -0.5).then_inc(consts_ready, 1)
            pool.wait_ge(consts_ready, 4)

            def reciprocal_roots(first, count):
                for i in range(first, first + count):
                    pool.wait_ge(var_ready, i + 1)
                    nc.gpsimd.tensor_tensor(ln_rstd[:, :], ln_rstd[:, :], minus_half[:, :], ALU.pow).then_inc(rstd_ready, 1)

            def scatter(n):
                pool.wait_ge(routed, n + 1)
                pool.wait_ge(padded, 64)
                for i in range(TT):
                    for k in range(2):
                        nc.gpsimd.indirect_dma_start(
                            out=sorted_rows[n], out_offset=bass.IndirectOffsetOnAxis(ap=place[k][:, i:i + 1], axis=0),
                            in_=row_words[:, i, :], in_offset=None).then_inc(scattered[n], 16)

            def add_results(n):
                def body(j, q, k):
                    pool.wait_ge(y_ready[n], j + 1)
                    pool.wait_ge(meta_in[k][n], 16 * (q + 1))
                    if at_least(j, 1):
                        pool.wait_ge(added[n], 16 * j)
                    pool.wait_ge(x_stored[n], 16 * B)
                    pool.sem_inc(turn_taken[n], 1)
                    nc.gpsimd.indirect_dma_start(
                        out=x_sum[n], out_offset=bass.IndirectOffsetOnAxis(ap=meta[:, k, M_TOK:M_TOK + 1].bitcast(I32), axis=0),
                        in_=y_sb[:, k, :], in_offset=None, compute_op=ALU.add).then_inc(added[n], 16)

                tile_loop(pool, n, body)

            for n in range(2):
                reciprocal_roots(2 * B * n, 2 * B + B * n)
                scatter(n)
                add_results(n)

        @block.tensor
        def _(pe):
            pe.wait_ge(in_const, 32)
            pe.wait_ge(in_ctx, 16)
            for c in range(DC):
                for t in range(2):
                    m = nc.tensor.transpose(bank[6][:, c * D + t * P:c * D + t * P + P], ctx_in[:, t, c * P:c * P + P], ident)
            m.then_inc(pe_setup, 1)
            pe.wait_ge(in_w, 16 * 7)
            for i, w in enumerate((0, 1, 2, 3, 5, 6)):
                for c in range(DC):
                    for o in range(DC):
                        m = nc.tensor.transpose(bank[i][:, c * D + o * P:c * D + o * P + P], w_in[:, w, o, c * P:c * P + P], ident)
            m.then_inc(pe_setup, 1)
            pe.wait_ge(in_few, 16 * 6)
            for n in range(2):
                ne = E + 1 - n
                for f in range(FC):
                    at = 128 * n + f * ne
                    nc.tensor.transpose(bank[7][:, at:at + ne], b1_rows[n][0:ne, f * P:f * P + P], ident[0:ne, 0:ne])
            for c in range(DC):
                m = nc.tensor.transpose(bank[7][:, 256 + c * E:256 + c * E + E], gate_rows[:, c * P:c * P + P], ident[0:E, 0:E])
            m = nc.tensor.transpose(bank[7][:, 256 + DC * E:256 + DC * E + DC], bq_rows, ident[0:DC, 0:DC])
            m.then_inc(pe_setup, 1)
            pe.wait_ge(act_setup, 1)
            pe.wait_ge(dve_setup, 4)
            for o in range(DC):
                for c in range(DC):
                    m = nc.tensor.matmul(bank[0][:, o * D:o * D + D], wT[:, 1, c, o * P:o * P + P], ctxT[:, c, :], start=c == 0, stop=c == DC - 1)
            for b in range(B):
                for c in range(DC):
                    m = nc.tensor.matmul(bank[1 + b // 2][:, b % 2 * D:b % 2 * D + D], ctxT2[:, c, b, :], wT[:, 2, c, :], start=c == 0, stop=c == DC - 1)
            m.then_inc(pe_setup, 1)
            for w in range(2):
                for t in range(2):
                    for c in range(DC):
                        m = nc.tensor.matmul(bank[3 + w][:, t * D:t * D + D], ctxT[:, c, t * P:t * P + P], wT1[:, w, c, :], start=c == 0, stop=c == DC - 1)
            m.then_inc(pe_setup, 1)
            pe.wait_ge(dve_setup, 7)
            for b in range(B):
                r = slice(SC * (b % 2), SC * (b % 2) + SC)
                for c in range(DC):
                    m = nc.tensor.matmul(bank[5 + b % 2][:, (b // 2 * DC + c) * P:(b // 2 * DC + c) * P + P], kv1[r, 0, b // 2, c * P:c * P + P],
                                         kv1[r, 1, b // 2, c * P:c * P + P], start=True, stop=True)
            m.then_inc(pe_setup, 1)
            pe.wait_ge(dve_setup, 8)
            for b in range(B):
                for c in range(DC):
                    for e in range(DC):
                        at = c * D + e * P
                        m = nc.tensor.matmul(bank[b][:, at:at + P], w_in[:, 4, e, c * P:c * P + P], kv_block[:, b, e, :], start=True, stop=True)
            m.then_inc(pe_setup, 1)
            for b in range(B):
                for e in range(DC):
                    at = b % 2 * D + e * P
                    m = nc.tensor.matmul(bank[4 + b // 2][:, at:at + P], bq_wide[:, e, :], kv_block[:, b, e, :], start=True, stop=True)
            m.then_inc(pe_setup, 1)
            pe.wait_ge(act_setup, 5)
            pe.wait_ge(dve_setup, 9)

            def transposed(s):
                pe.wait_ge(ln_done, s + 1)
                if s:
                    pe.wait_ge(xlnT_ready, s)
                for c in range(DC):
                    for t in range(TB):
                        m = nc.tensor.transpose(tp_ps[c][:, t * P:t * P + P], xln[:, s % 2, t, c * P:c * P + P], ident)
                m.then_inc(tp_done, 1)

            transposed(0)
            for b in range(B):
                pe.wait_ge(xlnT_ready, b + 1)
                if b:
                    pe.wait_ge(o_ready, b)
                for o in range(DC):
                    for c in range(DC):
                        m = nc.tensor.matmul(q_ps[o][:, :], wT[:, 0, c, o * P:o * P + P], xlnT[:, b % 2, c, :], start=c == 0, stop=c == DC - 1)
                m.then_inc(q_done, 1)
                m2 = transposed(b + 1)
                pe.wait_ge(q_ready, b + 1)
                for h in range(HP):
                    n = HP * b + h
                    if n >= 2:
                        pe.wait_ge(prob_ready, n - 1)
                    c, g = h // 4, 32 * (h % 4)
                    nc.tensor.matmul(s_ps[h % 2][:, :], k_heads[g:g + 32, c, b, :], qT[g:g + 32, c, :], start=True, stop=True).then_inc(score_done, 1)
                for h in range(HP):
                    pe.wait_ge(prob_ready, HP * b + h + 1)
                    c, g = h // 4, 32 * (h % 4)
                    m = nc.tensor.matmul(q_ps[c][g:g + 32, :], v_heads[:, b, 32 * h:32 * h + 32], probs[:, h, :], start=True, stop=True)
                m.then_inc(o_done, 1)
                pe.wait_ge(o_ready, b + 1)
                for t in range(TB):
                    n = TB * b + t
                    if n >= 2:
                        pe.wait_ge(x_updated, n - 1)
                    for c in range(DC):
                        m = nc.tensor.matmul(p_ps[n % 2][:, 0:D], oT[:, c, t * P:t * P + P], wT[:, 3, c, :], start=c == 0, stop=c == DC - 1)
                    m.then_inc(proj_done, 1)

            def logits(n, s):
                pe.wait_ge(xlnT_ready, s + 1)
                for t in range(TB):
                    i = TB * (s % B) + t
                    for c in range(DC):
                        m = nc.tensor.matmul(p_ps[0][:, i * E:i * E + E], xlnT[:, s % 2, c, t * P:t * P + P], gate_cols[:, n, c, :], start=c == 0, stop=c == DC - 1)
                m.then_inc(xlnT_used, 1)

            def route(n):
                pe.wait_ge(x_updated, TT * (n + 1))
                for b in range(B):
                    s = 8 * n + 4 + b
                    logits(n, s)
                    if b < B - 1:
                        transposed(s + 1)
                m = None
                pe.wait_ge(picked_ready, n + 1)
                counts = p_ps[1][:, 0:(TT + 1) * E]
                m = nc.tensor.matmul(counts, before16[:, :], picked16[:, :, :].rearrange("p t e -> p (t e)"), start=True, stop=False)
                for i in range(TT):
                    k = TT - i
                    m = nc.tensor.matmul(p_ps[1][:, (i + 1) * E:(TT + 1) * E], ones16[:, :],
                                         picked16[:, i, :].unsqueeze(1).broadcast_to([P, k, E]), start=False, stop=i == TT - 1)
                m.then_inc(count_done, 1)

            def ffn(n):
                pe.wait_ge(count_done, n + 1)
                pe.wait_ge(routed, n + 1)
                pe.wait_ge(split_lo, unit_count[0] + (unit_count[1] if n else 0))

                def turn(j, q, k):
                    pe.wait_ge(row_in[k][n], 16 * (q + 1))
                    if at_least(j, 2):
                        pe.wait_ge(xT_ready[n], j - 1)
                    for i in range(2 * DC):
                        m = nc.tensor.transpose(xT_ps[k][:, i * P:i * P + P], rows_in[:, k, i * P:i * P + P], ident16[:, :])
                    m.then_inc(rowT_done[n], 1)

                def up(j, q, k):
                    e = pe.value_load(tile_expert_i[0:1, bass.ds(j, 1)], min_val=0, max_val=E - n)
                    pe.wait_ge(xT_ready[n], j + 1)
                    for half in range(2):
                        if at_least(j, 2):
                            pe.wait_ge(gelu_done[half][n], j - 1)
                        for g in range(FC // 2):
                            f = half * FC // 2 + g
                            o = h_ps[k][half][:, g * P:g * P + P]
                            for c in range(DC):
                                hi, lo = xT[:, k, c * P:c * P + P], xT[:, k, (DC + c) * P:(DC + c) * P + P]
                                nc.tensor.matmul(o, w1_part(e, 0, c, f), hi, start=c == 0, stop=False)
                                nc.tensor.matmul(o, w1_part(e, 0, c, f), lo, start=False, stop=False)
                                m = nc.tensor.matmul(o, w1_part(e, 1, c, f), hi, start=False, stop=c == DC - 1)
                        m.then_inc(up_done[n], 1)

                def down(j, k):
                    e = pe.value_load(tile_expert_i[0:1, bass.ds(j, 1)], min_val=0, max_val=E - n)
                    if at_least(j, 2):
                        pe.wait_ge(weighed[n], j - 1)
                    for f in range(FC):
                        if f % (FC // 2) == 0:
                            pe.wait_ge(hid_ready[f // (FC // 2)][n], j + 1)
                        hi, lo = hid_hi[:, k, f * P:f * P + P], hid_lo[:, k, f * P:f * P + P]
                        nc.tensor.matmul(y_ps[k], hi, w2_part(e, 0, f), start=f == 0, stop=False)
                        nc.tensor.matmul(y_ps[k], hi, w2_part(e, 1, f), start=False, stop=False)
                        m = nc.tensor.matmul(y_ps[k], lo, w2_part(e, 0, f), start=False, stop=f == FC - 1)
                    m.then_inc(down_done[n], 1)

                def body(j, q, k):
                    if before_end(j, n, 1):
                        turn(j + 1, q + (1 if k else 0), 1 - k)
                    up(j, q, k)
                    if at_least(j, 1):
                        down(j - 1, 1 - k)

                turn(0, 0, 0)
                tile_loop(pe, n, body)
                down(tiles[n] - 1, (tiles[n] - 1) % 2)

            route(0)
            ffn(0)

            pe.wait_ge(late_in, 64)
            pe.wait_ge(weighed[0], tiles[0])
            transposed(8)
            for b in range(B):
                s = 8 + b
                pe.wait_ge(xlnT_ready, s + 1)
                for t in range(TB):
                    i = TB * b + t
                    if i >= 2:
                        pe.wait_ge(o_ready, B + i - 1)
                    for c in range(DC):
                        m = nc.tensor.matmul(p_ps[i % 2][:, 0:D], xlnT[:, s % 2, c, t * P:t * P + P], kvm[:, b, c, :], start=c == 0, stop=c == DC - 1)
                    m.then_inc(proj_done, 1)
                m.then_inc(xlnT_used, 1) if False else None
                transposed(s + 1)
            route(1)
            ffn(1)

        @block.scalar
        def _(act):
            act.wait_ge(in_bias, 64)
            nc.scalar.activation(gates[:, :], gates[:, :], ACT.Tanh).then_inc(g_ready, 1)
            act.wait_ge(pe_setup, 2)
            for i in range(4):
                m = nc.scalar.activation(wT[:, i, :, :].rearrange("p c o -> p (c o)"), bank[i][:, :], ACT.Copy)
            m.then_inc(act_setup, 1)
            act.wait_ge(pe_setup, 7)
            for b in range(B):
                nc.scalar.activation(kvm_out[:, b * 512:b * 512 + 512], bank[b][:, :], ACT.Copy).then_inc(act_setup, 1)

            def split(n, u):
                k = unit_no(n, u)
                act.wait_ge(in_raw[k % 2], 16 * (k // 2 + 1))
                nc.scalar.activation(split_to(n, u, 0), raw[:, k % 2, :], ACT.Copy, scale=W_SCALE).then_inc(split_hi, 1)

            def read_out(s):
                act.wait_ge(tp_done, s + 1)
                if s >= 2:
                    pass
                nc.scalar.activation(xlnT[:, s % 2, 0, :], tp_ps[0][:, :], ACT.Copy)
                nc.scalar.activation(xlnT[:, s % 2, 1, :], tp_ps[1][:, :], ACT.Copy).then_inc(xlnT_ready, 1)

            read_out(0)
            for b in range(B):
                act.wait_ge(q_done, b + 1)
                nc.scalar.activation(qT[:, 0, :], q_ps[0][:, :], ACT.Copy)
                nc.scalar.activation(qT[:, 1, :], q_ps[1][:, :], ACT.Copy).then_inc(q_ready, 1)
                read_out(b + 1)
                for h in range(HP):
                    act.wait_ge(score_done, HP * b + h + 1)
                    nc.scalar.activation(probs[:, h, :], s_ps[h % 2][:, :], ACT.Sigmoid, scale=float(DH) ** -0.5).then_inc(prob_ready, 1)
                act.wait_ge(o_done, b + 1)
                nc.scalar.activation(oT[:, 0, :], q_ps[0][:, :], ACT.Copy)
                nc.scalar.activation(oT[:, 1, :], q_ps[1][:, :], ACT.Copy).then_inc(o_ready, 1)

            def route(n):
                for b in range(1, B):
                    act.wait_ge(xlnT_used, 4 * n + b - 1) if b > 1 else None
                    read_out(8 * n + 4 + b)
                act.wait_ge(diff_ready, n + 1)
                nc.scalar.activation(gate_w[0][:, :], top[0][:, :], ACT.Sigmoid)
                nc.scalar.activation(gate_w[1][:, :], top[0][:, :], ACT.Sigmoid, scale=-1.0).then_inc(sig_ready, 1)

            def ffn(n):
                act.wait_ge(routed, n + 1)
                act.wait_ge(logits_done, n + 1)

                def body(j, q, k):
                    e = act.value_load(tile_expert_i[0:1, bass.ds(j, 1)], min_val=0, max_val=E - n)
                    for half in range(2):
                        act.wait_ge(up_done[n], 2 * j + half + 1)
                        if at_least(j, 2):
                            act.wait_ge(hid_ready[half][n], j - 1)
                        for g in range(FC // 2):
                            f = half * FC // 2 + g
                            m = nc.scalar.activation(hid[:, k, f * P:f * P + P], h_ps[k][half][:, g * P:g * P + P], ACT.Gelu,
                                                     bias=b1_cols[n][:, f, bass.ds(e, 1)], scale=1.0 / W_SCALE)
                        m.then_inc(gelu_done[half][n], 1)

                tile_loop(act, n, body)

            for u in range(unit_count[0]):
                split(0, u)
            route(0)
            ffn(0)
            for b in range(B + 1):
                if b >= 2:
                    pass
                read_out(8 + b)
            for u in range(unit_count[1]):
                split(1, u)
            route(1)
            ffn(1)

        @block.vector
        def _(dve):
            V = nc.vector
            chain, norms = [0], [0]

            def link(ins):
                chain[0] += 1
                ins.then_inc(dve_step, 1)
                dve.wait_ge(dve_step, chain[0])

            dve.wait_ge(in_const, 32)
            dve.wait_ge(consts_ready, 4)
            link(V.tensor_copy(padding_row[:, 2 * D:ROW].bitcast(I32)[:, M_TOK:M_TOK + 1], cst("trash")))
            V.tensor_copy(ident16[:, :], ident).then_inc(pad_ready, 1)
            link(V.tensor_copy(before16[:, :], cst("before")))
            dve.wait_ge(pe_setup, 1)
            ctx_ps = bank[6][:, :].rearrange("p (c s) -> p c s", c=DC)
            V.tensor_copy(ctxT[:, :, :], ctx_ps).then_inc(dve_setup, 1)
            for c in range(DC):
                m = V.tensor_copy(ctxT2[:, c, :, :].rearrange("p b (j s) -> p b j s", j=2),
                                  ctx_ps[:, c, :].rearrange("p (b s) -> p b s", b=B).unsqueeze(2).broadcast_to([P, B, 2, SC]))
            m.then_inc(dve_setup, 1)
            dve.wait_ge(pe_setup, 2)
            for w in range(2):
                m = V.tensor_copy(wT1[:, w, :, :].rearrange("p c o -> p (c o)"), bank[4 + w][:, :])
            m.then_inc(dve_setup, 1)
            dve.wait_ge(pe_setup, 3)
            for n in range(2):
                ne = E + 1 - n
                V.tensor_copy(b1_cols[n][:, :, :].rearrange("p f e -> p (f e)"), bank[7][:, 128 * n:128 * n + FC * ne])
            V.tensor_copy(gate_cols[:, 0, :, :].rearrange("p c e -> p (c e)"), bank[7][:, 256:256 + DC * E]).then_inc(dve_setup, 1)
            dve.wait_ge(pe_setup, 4)
            kT = bank[0][:, :].rearrange("p (c b s) -> p c b s", c=DC, b=B)
            for c in range(DC):
                for j in range(2):
                    V.tensor_scalar(k_heads[:, c, :, SC * j:SC * j + SC], kT[:, c, :, :], cst("kmask")[:, j:j + 1], None, ALU.mult)
            for b in range(B):
                m = V.tensor_tensor(v_heads[:, b, :], bank[1 + b // 2][:, b % 2 * D:b % 2 * D + D], cst("vmask"), ALU.mult)
            m.then_inc(dve_setup, 1)
            dve.wait_ge(pe_setup, 5)
            dve.wait_ge(in_bias, 64)
            for w in range(2):
                for t in range(2):
                    m = V.tensor_tensor(kv1[:, w, t, :], bank[3 + w][:, t * D:t * D + D], kv1_bias[:, w, :], ALU.add)
            m.then_inc(dve_setup, 1)
            V.tensor_copy(bq_wide[:, :, :], bank[7][:, 256 + DC * E:256 + DC * E + DC].unsqueeze(2).broadcast_to([P, DC, P])).then_inc(dve_setup, 1)
            dve.wait_ge(pe_setup, 6)
            for b in range(B):
                for c in range(DC):
                    at = (b // 2 * DC + c) * P
                    m = V.tensor_tensor(kv_block[:, b, c, :], bank[5 + b % 2][:, at:at + P], cst("kvmask"), ALU.mult)
            m.then_inc(dve_setup, 1)
            dve.wait_ge(pe_setup, 8)
            V.tensor_copy(kvb_out[:, 0:512], bank[4][:, :])
            V.tensor_copy(kvb_out[:, 512:1024], bank[5][:, :]).then_inc(dve_setup, 1)

            def split(n, u):
                k = unit_no(n, u)
                dve.wait_ge(split_hi, k + 1)
                V.scalar_tensor_tensor(split_to(n, u, 1), raw[:, k % 2, :], W_SCALE, split_to(n, u, 0), ALU.mult, ALU.subtract).then_inc(split_lo, 1)

            def normalise(src, dst):
                for t in range(TB):
                    m = V.bn_stats(ln_stats[:, t, :], src[:, t, :])
                link(m)
                for t in range(TB):
                    m = V.bn_aggr(ln_mv[:, t, :], ln_stats[:, t, :])
                link(m)
                V.tensor_scalar(ln_rstd[:, :], ln_mv[:, :, 1], EPS, None, ALU.add).then_inc(var_ready, 1)
                norms[0] += 1
                dve.wait_ge(rstd_ready, norms[0])
                for t in range(TB):
                    m = V.tensor_scalar(dst[:, t, :], src[:, t, :], ln_mv[:, t, 0:1], ln_rstd[:, t:t + 1], ALU.subtract, ALU.mult)
                return m

            def batch(b):
                return x_sb[:, TB * b:TB * b + TB, :]

            def layer_norm(s):
                if s >= 2:
                    dve.wait_ge(tp_done, s - 1)
                m = normalise(batch(s % B), xln[:, s % 2, :, :])
                link(m)
                nc.vector.engine_nop().then_inc(ln_done, 1) if False else None
                V.tensor_copy(ln_rstd[:, 0:1], ln_rstd[:, 0:1]).then_inc(ln_done, 1)

            def add_attention0(b):
                dve.wait_ge(g_ready, 1)
                for t in range(TB):
                    n = TB * b + t
                    dve.wait_ge(proj_done, n + 1)
                    m = V.scalar_tensor_tensor(x_sb[:, n, :], p_ps[n % 2][:, 0:D], gates[:, 0:1], x_sb[:, n, :], ALU.mult, ALU.add)
                    if t < TB - 1:
                        m.then_inc(x_updated, 1)
                m.then_inc(x_updated, 1)
                dve.wait_ge(x_updated, TB * b + TB)

            def rows(s):
                b = s % B
                hi = rows_out[:, TB * b:TB * b + TB, 0:D]
                link(V.tensor_copy(hi, xln[:, s % 2, :, :]))
                link(V.tensor_tensor(rows_out[:, TB * b:TB * b + TB, D:2 * D], xln[:, s % 2, :, :], hi, ALU.subtract))

            def wide(ap, n):
                return ap.unsqueeze(2).broadcast_to([P, TT, n])

            def route(n):
                dve.wait_ge(xlnT_used, 4 * (n + 1))
                V.tensor_copy(lg[:, :, :].rearrange("p t e -> p (t e)"), p_ps[0][:, 0:TT * E]).then_inc(logits_done, 1)
                dve.wait_ge(logits_done, n + 1)
                rev = cst("rev").unsqueeze(1).broadcast_to([P, TT, E])
                for k in range(2):
                    link(V.reduce_max(top[k][:, :], lg[:, :, :], AX))
                    link(V.tensor_tensor(r_a[:, :, :], lg[:, :, :], wide(top[k][:, :], E), ALU.is_equal))
                    link(V.tensor_tensor(r_a[:, :, :], r_a[:, :, :], rev, ALU.mult))
                    link(V.reduce_max(order[k][:, :], r_a[:, :, :], AX))
                    link(V.tensor_tensor(pick[k][:, :, :], rev, wide(order[k][:, :], E), ALU.is_equal))
                    if k == 0:
                        link(V.scalar_tensor_tensor(lg[:, :, :], pick[0][:, :, :], -3.0e38, lg[:, :, :], ALU.mult, ALU.add))
                V.tensor_tensor(picked16[:, 0:TT, :], pick[0][:, :, :], pick[1][:, :, :], ALU.add).then_inc(picked_ready, 1)
                V.tensor_tensor(top[0][:, :], top[0][:, :], top[1][:, :], ALU.subtract).then_inc(diff_ready, 1)
                dve.wait_ge(count_done, n + 1)
                counts = p_ps[1][:, 0:(TT + 1) * E]
                link(V.tensor_copy(r_a[:, :, :].rearrange("p t e -> p (t e)"), counts[:, 0:TT * E]))
                link(V.tensor_copy(n_tiles[:, :], counts[:, TT * E:(TT + 1) * E]))
                full = cst("full").unsqueeze(1).broadcast_to([P, E, TT])
                need = lg[:, :, :].rearrange("p t e -> p (t e)").rearrange("p (e t) -> p e t", e=E)
                link(V.tensor_tensor(need, n_tiles[:, :].unsqueeze(2).broadcast_to([P, E, TT]), full, ALU.is_gt))
                link(V.reduce_sum(n_tiles[:, :], need, AX))
                upto = lg[:, 0:E, :]
                link(V.tensor_tensor(upto, n_tiles[:, :].unsqueeze(1).broadcast_to([P, E, E]),
                                     cst("upto").rearrange("p (e i) -> p e i", e=E), ALU.mult))
                link(V.reduce_sum(end_tile[:, :], upto, AX))
                link(V.tensor_tensor(base_row[:, :], end_tile[:, :], n_tiles[:, :], ALU.subtract))
                link(V.tensor_scalar(base_row[:, :], base_row[:, :], float(P), float(P * shared_tiles[n]), ALU.mult, ALU.add))
                link(V.tensor_tensor(r_a[:, :, :], r_a[:, :, :], base_row[:, :].unsqueeze(1).broadcast_to([P, TT, E]), ALU.add))
                for k in range(2):
                    link(V.tensor_tensor(lg[:, :, :], pick[k][:, :, :], r_a[:, :, :], ALU.mult))
                    link(V.reduce_sum(top[1][:, :], lg[:, :, :], AX))
                    link(V.tensor_copy(place[k][:, :], top[1][:, :]))
                for first in range(0, ROUTED, TT):
                    m = min(TT, ROUTED - first)
                    past = lg[:, 0:m, :]
                    link(V.tensor_tensor(past, cst("tile")[:, first:first + m].unsqueeze(2).broadcast_to([P, m, E]),
                                         end_tile[:, :].unsqueeze(1).broadcast_to([P, m, E]), ALU.is_ge))
                    at = shared_tiles[n] + first
                    link(V.reduce_sum(tile_expert[:, at:at + m], past, AX))
                at = shared_tiles[n]
                link(V.tensor_scalar(tile_expert[:, at:at + ROUTED], tile_expert[:, at:at + ROUTED], float(E - 1), None, ALU.min))
                if at:
                    link(V.memset(tile_expert[:, 0:at], float(SHARED)))
                link(V.tensor_copy(tile_expert_i[:, 0:tiles[n]], tile_expert[:, 0:tiles[n]]))
                g = gates[:, 2 + n:3 + n]
                link(V.tensor_copy(rows_meta.bitcast(I32)[:, :, M_TOK], cst("token")))
                if n == 0:
                    link(V.memset(rows_meta[:, :, M_DW], 0.0))
                    link(V.memset(rows_meta[:, :, M_E1], 0.0))
                    link(V.tensor_copy(rows_meta[:, :, M_W2], g.broadcast_to([P, TT])))
                    V.tensor_copy(n_tiles[:, 0:1], n_tiles[:, 0:1]).then_inc(rows_ready, 1)
                    dve.wait_ge(shared_stored, 16)
                dve.wait_ge(sig_ready, n + 1)
                link(V.tensor_scalar(gate_w[0][:, :], gate_w[0][:, :], g, None, ALU.mult))
                link(V.tensor_scalar(gate_w[1][:, :], gate_w[1][:, :], g, None, ALU.mult))
                link(V.tensor_copy(rows_meta[:, :, M_W2], gate_w[1][:, :]))
                link(V.tensor_tensor(rows_meta[:, :, M_DW], gate_w[0][:, :], gate_w[1][:, :], ALU.subtract))
                V.tensor_scalar(rows_meta[:, :, M_E1], order[0][:, :], -1.0, float(E), ALU.mult, ALU.add).then_inc(routed, 1)

            def ffn(n):
                dve.wait_ge(b2_in[n], 32 if n == 0 else 16)

                def turned(j, k):
                    dve.wait_ge(rowT_done[n], j + 1)
                    if at_least(j, 2):
                        dve.wait_ge(up_done[n], 2 * (j - 1))
                    V.tensor_copy(xT[:, k, :], xT_ps[k]).then_inc(xT_ready[n], 1)

                def split_hidden(j, k):
                    if at_least(j, 2):
                        dve.wait_ge(down_done[n], j - 1)
                    for half in range(2):
                        f = slice(half * F // 2, (half + 1) * F // 2)
                        dve.wait_ge(gelu_done[half][n], j + 1)
                        V.tensor_copy(hid_hi[:, k, f], hid[:, k, f]).then_inc(hi_done[n], 1)
                        dve.wait_ge(hi_done[n], 2 * j + half + 1)
                        V.tensor_tensor(hid_lo[:, k, f], hid[:, k, f], hid_hi[:, k, f], ALU.subtract).then_inc(hid_ready[half][n], 1)

                def result(j, q, k):
                    e = dve.value_load(tile_expert_i[0:1, bass.ds(j, 1)], min_val=0, max_val=E - n)
                    dve.wait_ge(meta_in[k][n], 16 * (q + 1))
                    V.tensor_scalar(pick_w[:, k:k + 1], meta[:, k, M_E1:M_E1 + 1], tile_expert[:, bass.ds(j, 1)], meta[:, k, M_DW:M_DW + 1],
                                    ALU.is_equal, ALU.mult).then_inc(biased[n], 1)
                    dve.wait_ge(biased[n], 2 * j + 1)
                    V.tensor_tensor(pick_w[:, k:k + 1], pick_w[:, k:k + 1], meta[:, k, M_W2:M_W2 + 1], ALU.add).then_inc(biased[n], 1)
                    dve.wait_ge(down_done[n], j + 1)
                    if at_least(j, 2):
                        dve.wait_ge(added[n], 16 * (j - 1))
                    V.scalar_tensor_tensor(y_sb[:, k, :], y_ps[k], 1.0 / W_SCALE, b2_rows[:, bass.ds(e, 1), :].rearrange("p a d -> p (a d)"),
                                           ALU.mult, ALU.add).then_inc(weighed[n], 1)
                    dve.wait_ge(biased[n], 2 * j + 2)
                    dve.wait_ge(weighed[n], j + 1)
                    V.tensor_scalar(y_sb[:, k, :], y_sb[:, k, :], pick_w[:, k:k + 1], None, ALU.mult).then_inc(y_ready[n], 1)
                    V.tensor_copy(pick_w[:, k:k + 1], pick_w[:, k:k + 1]).then_inc(biased[n], 1) if False else None

                def body(j, q, k):
                    if before_end(j, n, 1):
                        turned(j + 1, 1 - k)
                    split_hidden(j, k)
                    if at_least(j, 1):
                        result(j - 1, q - (0 if k else 1), 1 - k)

                turned(0, 0)
                tile_loop(dve, n, body)
                result(tiles[n] - 1, (tiles[n] - 1) // 2, (tiles[n] - 1) % 2)

            for b in range(2):
                dve.wait_ge(in_x[b], 16)
                layer_norm(b)
            for b in range(B):
                add_attention0(b)
                if b < 2:
                    dve.wait_ge(in_x[b + 2], 16)
                if b < 3:
                    layer_norm(b + 2)
            for u in range(unit_count[0]):
                split(0, u)
            for s in range(4, 8):
                if s > 4:
                    layer_norm(s)
                rows(s)
            route(0)
            ffn(0)
            dve.wait_ge(late_in, 64)
            link(V.tensor_scalar(gamma, gamma, gates[:, 1:2], None, ALU.mult))
            link(V.tensor_scalar(beta, beta, gates[:, 1:2], None, ALU.mult))

            def add_attention1(b):
                s = 8 + b
                dve.wait_ge(tp_done, s + 1)
                u = xln[:, s % 2, :, :]
                link(V.tensor_tensor(u, u, kvb[:, b, :].unsqueeze(1).broadcast_to([P, TB, D]), ALU.add))
                for t in range(TB):
                    i = TB * b + t
                    dve.wait_ge(proj_done, TT + i + 1)
                    m = V.tensor_tensor(u[:, t, :], p_ps[i % 2][:, 0:D], u[:, t, :], ALU.add)
                    m.then_inc(o_ready, 1)
                dve.wait_ge(o_ready, B + TB * (b + 1))
                link(normalise(u, u))
                link(V.tensor_tensor(u, u, gamma.unsqueeze(1).broadcast_to([P, TB, D]), ALU.mult))
                link(V.tensor_tensor(u, u, beta.unsqueeze(1).broadcast_to([P, TB, D]), ALU.add))
                V.tensor_tensor(batch(b), batch(b), u, ALU.add).then_inc(x_updated, TB)
                dve.wait_ge(x_updated, TT + TB * (b + 1))

            for b in range(B):
                dve.wait_ge(x_back[b], 16)
                layer_norm(8 + b)
                add_attention1(b)
            layer_norm(12)
            for u in range(unit_count[1]):
                split(1, u)
            for s in range(12, 16):
                if s > 12:
                    layer_norm(s)
                rows(s)
            route(1)
            ffn(1)


def kernel(**inputs):
    import concourse.bacc as bacc
    from concourse.bass_utils import run_bass_kernel_spmd

    nc = bacc.Bacc("TRN2", target_bir_lowering=False, num_devices=1)
    arrays, aps = {}, {}
    for name in NAMES:
        arrays["in_" + name] = np.ascontiguousarray(inputs[name])
        aps[name] = nc.dram_tensor("in_" + name, arrays["in_" + name].shape, F32, kind="ExternalInput").ap()
    arrays["in_const"] = CONST
    const = nc.dram_tensor("in_const", CONST.shape, F32, kind="ExternalInput").ap()
    out = nc.dram_tensor("out", (B, S, D), F32, kind="ExternalOutput").ap()
    build(nc, aps, const, out)
    result = run_bass_kernel_spmd(nc, [arrays], core_ids=[0])
    return result.results[0]["out"]
```

```python
from contextlib import ExitStack

import numpy as np
import concourse.bass as bass
from concourse import mybir

F32 = mybir.dt.float32
F16 = mybir.dt.float16
BF16 = mybir.dt.bfloat16
I32 = mybir.dt.int32
U8 = mybir.dt.uint8
ACT = mybir.ActivationFunctionType
ALU = mybir.AluOpType
AX = mybir.AxisListType.X

P = 128
B, S, D = 4, 512, 256
SC, H, DH = 64, 16, 16
E, F = 8, 1024
T = B * S
TT = T // P
TB = S // P
DC = D // P
FC = F // P
HP = H // 2
SHARED = E
ROUTED = (2 * T + E * (P - 1)) // P
W_SCALE = 64.0
ROW = 2 * D + 8
M_W2, M_DW, M_TOK, M_E1 = range(4)
EPS = 1e-5
SLOT = 4 * 2048
SRING = 4
RAW = 2
RAW1 = RAW + 4


def constants():
    p = np.arange(P)
    c = {}
    c["before"] = (p[:, None] < p[None, :]) * 1.0
    c["vmask"] = ((np.arange(D)[None, :] // DH) % 2 == (p[:, None] // SC)) * 1.0
    c["kvmask"] = (p[:, None] // DH == p[None, :] // DH) * (float(DH) ** -0.5)
    c["kmask"] = ((p[:, None] // DH) % 2 == np.arange(2)[None, :]) * 1.0
    c["ident"] = np.eye(P)
    c["rev"] = np.broadcast_to(E - np.arange(E), (P, E))
    c["upto"] = np.broadcast_to((np.arange(E)[None, :] <= np.arange(E)[:, None]).reshape(-1), (P, E * E))
    c["full"] = np.broadcast_to(P * np.arange(TT), (P, TT))
    c["tile"] = np.broadcast_to(np.arange(ROUTED), (P, ROUTED))
    c["token"] = p[:, None] + P * np.arange(TT)[None, :]
    c["trash"] = T + p[:, None]
    at, where = 0, {}
    for k, v in c.items():
        where[k] = (at, v.shape[1])
        at += v.shape[1]
    return np.concatenate(list(c.values()), axis=1).astype(np.float32), where


CONST, WHERE = constants()
EARLY = WHERE["ident"][0]
NAMES = ["x", "ctx_1024", "g_xattn", "g_ffn", "L0_xattn_Wq", "L0_xattn_Wk", "L0_xattn_Wv", "L0_xattn_Wo",
         "L0_ffn_gate_w", "L0_ffn_W1", "L0_ffn_b1", "L0_ffn_W2", "L0_ffn_b2", "L0_ffn_sW1", "L0_ffn_sb1",
         "L0_ffn_sW2", "L0_ffn_sb2", "L1_xattn_Wq", "L1_xattn_bq", "L1_xattn_Wk", "L1_xattn_bk", "L1_xattn_Wv",
         "L1_xattn_bv", "L1_xattn_ln_gamma", "L1_xattn_ln_beta", "L1_ffn_Wr", "L1_ffn_W1", "L1_ffn_b1",
         "L1_ffn_W2", "L1_ffn_b2"]


def build(nc, a, const, out):
    with ExitStack() as ctx:
        def sb(name, shape, dt):
            return ctx.enter_context(nc.sbuf_tensor(name, shape, dt))

        def sem(name):
            return ctx.enter_context(nc.semaphore(name))

        def dram(name, shape, dt):
            return nc.dram_tensor(name, shape, dt, kind="Internal").ap()

        sorted_rows = [dram(f"sorted_rows{n}", [(ROUTED + 1) * P, ROW // 2], I32) for n in range(2)]
        x_sum = [dram(f"x_sum{n}", [T + P, D], F32) for n in range(2)]
        kv_dram = dram("kv_dram", [P, B * DC * D], F32)
        kv_bias_dram = dram("kv_bias_dram", [P, B * D], F32)

        weights = sb("weights", [P, E + 1, SLOT], F16)
        weights_at = nc.sbuf_base - 2 * (E + 1) * SLOT
        weight_bytes = weights[:, :, :].rearrange("p e w -> p (e w)").bitcast(U8)
        raw = sb("raw", [P, RAW, 1024], F32)
        const_sb = sb("const_sb", [P, CONST.shape[1] - EARLY], F32)
        const_early = weights[:, 3, :].bitcast(F32)[:, 2560:2560 + EARLY]

        def cst(name):
            at, n = WHERE[name]
            return const_early[:, at:at + n] if at < EARLY else const_sb[:, at - EARLY:at - EARLY + n]

        ident = cst("ident")
        ident16 = sb("ident16", [P, P], F16)
        before16 = sb("before16", [P, P], BF16)
        ones16 = sb("ones16", [P, P], BF16)
        gates = sb("gates", [P, 5], F32)
        b1_cols = [sb(f"b1_cols{n}", [P, FC, E + 1 - n], F32) for n in range(2)]
        gate_cols = sb("gate_cols", [P, 2, DC, E], F32)
        padding_row = sb("padding_row", [P, ROW], F16)
        sb2_row = padding_row[:, 0:2 * D].bitcast(F32)
        ln_stats = sb("ln_stats", [P, TB, 6], F32)
        ln_mv = sb("ln_mv", [P, TB, 2], F32)
        ln_rstd = sb("ln_rstd", [P, TB], F32)
        minus_half = sb("minus_half", [P, TB], F32)
        lg = sb("lg", [P, TT, E], F32)
        r_a = sb("r_a", [P, TT, E], F32)
        pick = [sb(f"pick{k}", [P, TT, E], F32) for k in range(2)]
        picked16 = sb("picked16", [P, TT + 1, E], BF16)
        top = [sb(f"top{k}", [P, TT], F32) for k in range(2)]
        order = [sb(f"order{k}", [P, TT], F32) for k in range(2)]
        gate_w = [sb(f"gate_w{k}", [P, TT], F32) for k in range(2)]
        place = [sb(f"place{k}", [P, TT], I32) for k in range(2)]
        n_tiles = sb("n_tiles", [P, E], F32)
        end_tile = sb("end_tile", [P, E], F32)
        base_row = sb("base_row", [P, E], F32)
        tile_expert = sb("tile_expert", [P, ROUTED], F32)
        tile_expert_i = sb("tile_expert_i", [P, ROUTED], I32)
        meta = sb("meta", [P, 2, 4], F32)
        pick_w = sb("pick_w", [P, 2], F32)

        x_arena = sb("x_arena", [P, TT * D], F32)
        x_sb = x_arena[:, :].rearrange("p (t d) -> p t d", t=TT)
        rows_in = x_arena[:, 0:ROW].bitcast(F16).rearrange("p (k r) -> p k r", k=2)
        rows_in_words = x_arena[:, 0:ROW].bitcast(I32).rearrange("p (k r) -> p k r", k=2)
        xT = x_arena[:, ROW:ROW + 512].bitcast(F16).rearrange("p (k r) -> p k r", k=2)
        y_sb = x_arena[:, ROW + 512:ROW + 1024].rearrange("p (k d) -> p k d", k=2)
        b2_at = ROW + 1024
        b2_rows = x_arena[:, b2_at:b2_at + E * D].rearrange("p (e d) -> p e d", e=E)
        work = sb("work", [P, 4096], F32)
        xln = work[:, 0:2048].rearrange("p (k t d) -> p k t d", k=2, t=TB)
        xlnT = work[:, 2048:4096].rearrange("p (k c s) -> p k c s", k=2, c=DC)
        hid = work[:, 0:2048].rearrange("p (k f) -> p k f", k=2)
        hid_hi = work[:, 2048:3072].bitcast(F16).rearrange("p (k f) -> p k f", k=2)
        hid_lo = work[:, 3072:4096].bitcast(F16).rearrange("p (k f) -> p k f", k=2)
        s_xT = work[:, 0:1024].bitcast(F16).rearrange("p (k s) -> p k s", k=2 * DC)
        s_hid = work[:, 1024:2048].rearrange("p (k s) -> p k s", k=2)
        s_pair = work[:, 2048:4096].bitcast(F16).rearrange("p (k l s) -> p k l s", k=SRING, l=2)
        row_arena = sb("row_arena", [P, TT * ROW // 2], F32)
        rows_out = row_arena[:, :].bitcast(F16).rearrange("p (t r) -> p t r", t=TT)
        row_words = row_arena[:, :].bitcast(I32).rearrange("p (t r) -> p t r", t=TT)
        rows_meta = row_arena[:, :].rearrange("p (t r) -> p t r", t=TT)[:, :, D:D + 4]
        k_heads = row_arena[:, 0:1024].rearrange("p (c b m) -> p c b m", c=DC, b=B)
        v_heads = row_arena[:, 1024:2048].rearrange("p (b d) -> p b d", b=B)
        ctx_in = row_arena[:, 2048:2560].rearrange("p (t d) -> p t d", t=2)
        ctxT = row_arena[:, 2560:3072].rearrange("p (c s) -> p c s", c=DC)
        ctxT2 = row_arena[:, 3072:4096].rearrange("p (c b m) -> p c b m", c=DC, b=B)
        att = weights[:, 6:8, :].rearrange("p e w -> p (e w)").bitcast(F32)
        probs = att[:, 0:4096].rearrange("p (h s) -> p h s", h=HP)
        wT = att[:, 4096:6144].rearrange("p (w c o) -> p w c o", w=4, c=DC)
        qT = att[:, 6144:7168].rearrange("p (c s) -> p c s", c=DC)
        oT = att[:, 7168:8192].rearrange("p (c s) -> p c s", c=DC)
        pre = weights[:, 4:6, :].rearrange("p e w -> p (e w)").bitcast(F32)
        w_in = pre[:, 0:3584].rearrange("p (w c i) -> p w c i", w=7, c=DC)
        wT1 = pre[:, 3584:4608].rearrange("p (w c o) -> p w c o", w=2, c=DC)
        kv1 = pre[:, 4608:5632].rearrange("p (w t d) -> p w t d", w=2, t=2)
        kv1_bias = pre[:, 5632:6144].rearrange("p (w d) -> p w d", w=2)
        kv_block = pre[:, 6144:7168].rearrange("p (b c e) -> p b c e", b=B, c=DC)
        bq_wide = pre[:, 7168:7424].rearrange("p (c m) -> p c m", c=DC)
        b1_in = pre[:, 7424:8192]
        few = weights[0:16, 3, :].bitcast(F32)
        b1_rows = [few[0:E + 1, 0:F], few[0:E, F:2 * F]]
        gate_rows = few[0:E, 2 * F:2 * F + D]
        bq_rows = few[0:DC, 2 * F + D:2 * F + D + P]
        kv_out = weights[:, 2, :].bitcast(F32)
        kvm_out = kv_out[:, 0:2048]
        kvb_out = kv_out[:, 2048:3072]
        late = row_arena[:, :]
        kvm = late[:, 0:2048].rearrange("p (b c e) -> p b c e", b=B, c=DC)
        kvb = late[:, 2048:3072].rearrange("p (b d) -> p b d", b=B)
        gamma = late[:, 3072:3328]
        beta = late[:, 3328:3584]

        bank = [ctx.enter_context(nc.psum_tensor(f"bank{i}", [P, 512], F32)) for i in range(8)]
        tp_ps, q_ps, s_ps, p_ps = bank[0:2], bank[2:4], bank[4:6], bank[6:8]
        xT_ps = [bank[k][:, 0:256].bitcast(F16) for k in range(2)]
        h_ps = [bank[2:4], bank[4:6]]
        y_ps = bank[6:8]
        s_h_ps, s_y_ps = bank[0:2], bank[2:6]
        s_xT_ps = bank[6][:, :].bitcast(F16).rearrange("p (c r) -> p c r", c=2 * DC)

        in_const, in_ctx, in_w, in_few, in_bias, in_sb2 = (sem(n) for n in ("in_const", "in_ctx", "in_w", "in_few", "in_bias", "in_sb2"))
        in_x = [sem(f"in_x{b}") for b in range(B)]
        in_raw = [sem(f"in_raw{k}") for k in range(RAW1)]
        padded = sem("padded")
        pad_ready = sem("pad_ready")
        consts_ready = sem("consts_ready")
        g_ready = sem("g_ready")
        var_ready, rstd_ready = sem("var_ready"), sem("rstd_ready")
        dve_step = sem("dve_step")
        pe_setup, dve_setup, act_setup = sem("pe_setup"), sem("dve_setup"), sem("act_setup")
        kv_stored = sem("kv_stored")
        ln_done, tp_done, xlnT_ready, xlnT_used = sem("ln_done"), sem("tp_done"), sem("xlnT_ready"), sem("xlnT_used")
        q_done, q_ready = sem("q_done"), sem("q_ready")
        score_done, prob_ready = sem("score_done"), sem("prob_ready")
        o_done, o_ready = sem("o_done"), sem("o_ready")
        proj_done, x_updated = sem("proj_done"), sem("x_updated")
        split_hi, split_lo = sem("split_hi"), sem("split_lo")
        late_in = sem("late_in")
        logits_done = sem("logits_done")
        diff_ready, sig_ready = sem("diff_ready"), sem("sig_ready")
        picked_ready, count_done, routed = sem("picked_ready"), sem("count_done"), sem("routed")
        rows_hi, rows_lo = sem("rows_hi"), sem("rows_lo")
        x_stored = [[sem(f"x_stored{n}_{b}") for b in range(B)] for n in range(2)]
        s_turned, s_xT_ready, s_up_done, s_gelu_done = sem("s_turned"), sem("s_xT_ready"), sem("s_up_done"), sem("s_gelu_done")
        s_hi_done, s_down_done = sem("s_hi_done"), sem("s_down_done")
        s_lo_done = [sem(f"s_lo_done{k}") for k in range(2)]
        s_biased, s_added = sem("s_biased"), sem("s_added")
        scattered = [sem(f"scattered{n}") for n in range(2)]
        b2_in = [sem(f"b2_in{n}") for n in range(2)]
        x_back = [sem(f"x_back{b}") for b in range(B)]
        out_stored = sem("out_stored")

        def per_layer(name):
            return [sem(f"{name}_{n}") for n in range(2)]

        row_in = [per_layer(f"row_in{k}") for k in range(2)]
        meta_in = [per_layer(f"meta_in{k}") for k in range(2)]
        rowT_done, xT_ready = per_layer("rowT_done"), per_layer("xT_ready")
        up_done, hi_done = per_layer("up_done"), per_layer("hi_done")
        gelu_done = [per_layer(f"gelu_done_half{h}") for h in range(2)]
        hid_ready = [per_layer(f"hid_ready_half{h}") for h in range(2)]
        turn_taken = per_layer("turn_taken")
        down_done, biased, y_read, y_ready, added = (per_layer(n) for n in ("down_done", "biased", "y_read", "y_ready", "added"))

        block = ctx.enter_context(nc.Block())

        POOL_BLOCKS = 2 * FC

        def low_ready(eng, m):
            if m < POOL_BLOCKS:
                eng.wait_ge(s_lo_done[0], m + 1)
            else:
                eng.wait_ge(s_lo_done[1], m - POOL_BLOCKS + 1)

        unit_count = [2 * 2 * (E + 1), 2 * 2 * E]

        def unit(n, u):
            e, m, half = u // 4, (u // 2) % 2, u % 2
            if n == 0:
                e = (SHARED, *range(E))[e]
            return e, m, half

        def split_to(n, u, low):
            e, m, half = unit(n, u)
            if m == 0:
                at = 2048 * low + 1024 * half
                return weights[:, e, at:at + 1024].rearrange("p (g d) -> p g d", d=D)
            at = 4096 + 2048 * half
            return weights[:, e, at:at + 2048].rearrange("p (f l d) -> p f l d", f=FC // 2, l=2)[:, :, low, :]

        def unit_no(n, u):
            return u + (unit_count[0] if n else 0)

        def raw_no(n, u):
            return u % (RAW1 if n else RAW)

        def raw_at(n, u):
            k = raw_no(n, u)
            if k < RAW:
                return raw[:, k, :].rearrange("p (g d) -> p g d", d=D)
            return weights[:, SHARED, :].bitcast(F32)[:, 1024 * (k - RAW):1024 * (k - RAW + 1)].rearrange("p (g d) -> p g d", d=D)

        def raw_loaded(n, u):
            k = raw_no(n, u)
            before = unit_count[0] // RAW if n and k < RAW else 0
            return 16 * (before + u // (RAW1 if n else RAW) + 1)

        class BlockAddress:

            def __init__(self, name, at, count, stationary):
                self.reg = nc.tensor.alloc_register(name)
                self.start = weights_at + (2 * (count - 1) if stationary else 0)
                self.at, self.count = 2 * at, count

            def point(self, expert_at):
                nc.tensor.reg_alu(self.reg, expert_at, self.start + self.at, ALU.add)

            def block(self, count=None):
                value = bass.RuntimeValue.of_register_unchecked(
                    self.reg, min_val=self.start + self.at, max_val=self.start + self.at + 2 * SLOT * (E - 1),
                    guaranteed_mod_val=0, out_of_modulus=2)
                return weight_bytes[:, bass.ds(value - self.start, 2 * (count or self.count))].bitcast(F16)

        def tile_loop(eng, n, body):
            assert ROUTED % 2 == 1
            last = body(0, 0, 0, None)
            body(1, 0, 1, last)
            with eng.Fori(0, (ROUTED - 3) // 2) as t:
                last = body(2 * t + 2, t + 1, 0, None)
                body(2 * t + 3, t + 1, 1, last)
            body(ROUTED - 1, (ROUTED - 1) // 2, 0, None)

        def at_least(j, n):
            return j >= n if isinstance(j, int) else True

        def before_end(j, ahead):
            return j + ahead < ROUTED if isinstance(j, int) else True

        def expert_of(eng, j):
            e = eng.value_load(tile_expert_i[0:1, bass.ds(j, 1)])
            return nc.s_assert_within(e, 0, E - 1, skip_runtime_bounds_check_because="route() clamps the experts to 0 .. E - 1")

        def attention_splits(b):
            total = unit_count[0] - 4 * 2
            at = [total * i // (2 * B) for i in range(2 * B + 1)]
            return range(at[2 * b], at[2 * b + 1]), range(at[2 * b + 1], at[2 * b + 2])

        def attention1_splits(b):
            return range(unit_count[1] * b // B, unit_count[1] * (b + 1) // B)

        def shared_splits(m):
            first = unit_count[0] - 4 * 2
            if m % 2 == 0 and 0 <= m < FC:
                return first + m // 2
            if m % 2 == 0 and 2 * FC <= m < 3 * FC:
                return first + 4 + (m - 2 * FC) // 2
            return None

        def attend0_src(w):
            return a[("L0_xattn_Wq", "L0_xattn_Wk", "L0_xattn_Wv", "L0_xattn_Wo", "L1_xattn_Wq", "L1_xattn_Wk",
                      "L1_xattn_Wv")[w]]

        x_rows = a["x"].rearrange("b s d -> (b s) d")

        def batch_of(rows, b):
            return rows[b * S:(b + 1) * S, :].rearrange("(t p) d -> p t d", p=P)

        @block.sync
        def _(sp):
            sp.dma_start(const_sb[:, :], const[:, EARLY:]).then_inc(in_const, 16)
            sp.dma_start(const_early, const[:, 0:EARLY]).then_inc(in_const, 16)
            sp.dma_start(ctx_in[:, :, :], a["ctx_1024"].rearrange("b s d -> (b s) d").rearrange("(t p) d -> p t d", p=P)).then_inc(in_ctx, 16)
            for w in range(7):
                sp.dma_start(w_in[:, w, :, :], attend0_src(w).rearrange("(c p) i -> p c i", p=P)).then_inc(in_w, 16)
            sp.dma_start(few[0:E, 0:F], a["L0_ffn_b1"]).then_inc(in_few, 16)
            sp.dma_start(few[E:E + 1, 0:F], a["L0_ffn_sb1"].rearrange("(a f) -> a f", a=1)).then_inc(in_few, 16)
            sp.dma_start(few[0:E, F:2 * F], a["L1_ffn_b1"]).then_inc(in_few, 16)
            sp.dma_start(gate_rows, a["L0_ffn_gate_w"]).then_inc(in_few, 16)
            sp.dma_start(gate_cols[:, 1, :, :], a["L1_ffn_Wr"].rearrange("(c p) e -> p c e", p=P)).then_inc(in_few, 16)
            sp.dma_start(bq_rows, a["L1_xattn_bq"].rearrange("(c p) -> c p", p=P)).then_inc(in_few, 16)
            sp.dma_start(kv1_bias[:, 0, :], a["L1_xattn_bk"].partition_broadcast(P)).then_inc(in_bias, 16)
            sp.dma_start(kv1_bias[:, 1, :], a["L1_xattn_bv"].partition_broadcast(P)).then_inc(in_bias, 16)
            sp.dma_start(gates[:, 0:2], a["g_xattn"].partition_broadcast(P)).then_inc(in_bias, 16)
            sp.dma_start(gates[:, 2:4], a["g_ffn"].partition_broadcast(P)).then_inc(in_bias, 16)
            for b in range(B):
                sp.dma_start(x_sb[:, TB * b:TB * b + TB, :], batch_of(x_rows, b)).then_inc(in_x[b], 16)

            def load_unit(n, u):
                if n == 0 and u >= RAW:
                    sp.wait_ge(split_lo, u - RAW + 1)
                if n == 1 and u < RAW:
                    sp.wait_ge(split_lo, unit_count[0])
                elif n == 1 and u < RAW1:
                    sp.wait_ge(s_down_done, B * FC)
                elif n == 1:
                    sp.wait_ge(split_lo, unit_count[0] + u - RAW1 + 1)
                e, m, half = unit(n, u)
                if e == SHARED:
                    src = (a["L0_ffn_sW1"], a["L0_ffn_sW2"])[m]
                else:
                    src = a[f"L{n}_ffn_W{m + 1}"][e, :, :]
                if m == 0:
                    sp.dma_start(raw_at(n, u).rearrange("p g d -> p (g d)"), src[half * P:half * P + P, :]).then_inc(in_raw[raw_no(n, u)], 16)
                else:
                    sp.dma_start(raw_at(n, u), src[half * F // 2:(half + 1) * F // 2, :].rearrange("(f p) d -> p f d", p=P))\
                      .then_inc(in_raw[raw_no(n, u)], 16)

            def store_kv():
                sp.wait_ge(act_setup, 5)
                sp.wait_ge(dve_setup, 9)
                sp.dma_start(kv_dram, kvm_out).then_inc(kv_stored, 16)
                sp.dma_start(kv_bias_dram, kvb_out).then_inc(kv_stored, 16)

            for u in range(RAW):
                load_unit(0, u)
            sp.wait_ge(pad_ready, 1)
            for n in range(2):
                sp.dma_start(sorted_rows[n].rearrange("(j p) r -> p j r", p=P),
                             padding_row[:, :].bitcast(I32).unsqueeze(1).broadcast_to([P, ROUTED + 1, ROW // 2])).then_inc(padded, 16)
                sp.dma_start(x_sum[n][T:T + P, :], padding_row[:, 0:2 * D].bitcast(F32)).then_inc(padded, 16)
            sp.wait_ge(padded, 64)
            sp.dma_start(sb2_row, a["L0_ffn_sb2"].partition_broadcast(P)).then_inc(in_sb2, 16)
            store_kv()
            for u in range(RAW, unit_count[0]):
                load_unit(0, u)

            def store_x(n, b, ready, count):
                sp.wait_ge(ready, count)
                sp.dma_start(batch_of(x_sum[n], b), x_sb[:, TB * b:TB * b + TB, :]).then_inc(x_stored[n][b], 16)

            def ffn_loads(n, meanwhile):
                def rows(j, q, k):
                    sp.dma_start(rows_in_words[:, k, :], sorted_rows[n][bass.ds(j * P, P), :]).then_inc(row_in[k][n], 16)

                def body(j, q, k, last):
                    if before_end(j, 2):
                        sp.wait_ge(rowT_done[n], j + 1)
                        rows(j + 2, q + 1, k)
                    if at_least(j, 2):
                        sp.wait_ge(added[n], 16 * (j - 1))
                    sp.dma_start(meta[:, k, :].bitcast(I32), sorted_rows[n][bass.ds(j * P, P), D:ROW // 2]).then_inc(meta_in[k][n], 16)

                sp.wait_ge(ln_done, 8 * (n + 1))
                for b in range(2):
                    sp.wait_ge(x_stored[n][b], 16)
                sp.wait_ge(scattered[n], 2 * TT * 16)
                rows(0, 0, 0)
                rows(1, 0, 1)
                for b in range(2, B):
                    sp.wait_ge(x_stored[n][b], 16)
                sp.dma_start(b2_rows[:, :, :], a[f"L{n}_ffn_b2"].partition_broadcast(P)).then_inc(b2_in[n], 16)
                meanwhile()
                tile_loop(sp, n, body)
                sp.wait_ge(row_in[1][n], 16 * ((ROUTED + 1) // 2))

            def load_ahead():
                sp.wait_ge(s_turned, 2 * B)
                sp.wait_ge(kv_stored, 32)
                sp.dma_start(kvm.rearrange("p b c e -> p (b c e)"), kv_dram).then_inc(late_in, 16)
                sp.dma_start(kvb.rearrange("p b d -> p (b d)"), kv_bias_dram).then_inc(late_in, 16)
                sp.dma_start(gamma, a["L1_xattn_ln_gamma"].partition_broadcast(P)).then_inc(late_in, 16)
                sp.dma_start(beta, a["L1_xattn_ln_beta"].partition_broadcast(P)).then_inc(late_in, 16)
                for u in range(RAW1):
                    load_unit(1, u)

            for b in range(B):
                store_x(0, b, s_added, TB * (b + 1))
            ffn_loads(0, load_ahead)
            sp.wait_ge(added[0], 16 * ROUTED)
            for b in range(B):
                sp.dma_start(x_sb[:, TB * b:TB * b + TB, :], batch_of(x_sum[0], b)).then_inc(x_back[b], 16)
            for u in range(RAW1, unit_count[1]):
                load_unit(1, u)
            for b in range(B):
                store_x(1, b, x_updated, TT + TB * (b + 1))
            ffn_loads(1, lambda: None)
            sp.wait_ge(added[1], 16 * ROUTED)
            sp.dma_start(out.rearrange("b s d -> (b s) d"), x_sum[1][0:T, :]).then_inc(out_stored, 16)
            sp.wait_ge(out_stored, 16)

        @block.gpsimd
        def _(pool):
            nc.gpsimd.memset(padding_row[:, 0:2 * D + 8], 0.0).then_inc(consts_ready, 1)
            nc.gpsimd.memset(ones16[:, :], 1.0).then_inc(consts_ready, 1)
            nc.gpsimd.memset(picked16[:, TT, :], 0.0).then_inc(consts_ready, 1)
            nc.gpsimd.memset(minus_half[:, :], -0.5).then_inc(consts_ready, 1)
            pool.wait_ge(consts_ready, 4)

            def reciprocal_roots(first, count):
                for i in range(first, first + count):
                    pool.wait_ge(var_ready, i + 1)
                    nc.gpsimd.tensor_tensor(ln_rstd[:, :], ln_rstd[:, :], minus_half[:, :], ALU.pow).then_inc(rstd_ready, 1)

            def rows(s):
                b = s % B
                pool.wait_ge(rows_hi, s // 8 * B + b + 1)
                hi = rows_out[:, TB * b:TB * b + TB, 0:D]
                nc.gpsimd.tensor_tensor(rows_out[:, TB * b:TB * b + TB, D:2 * D], xln[:, s % 2, :, :], hi, ALU.subtract).then_inc(rows_lo, 1)

            def shared_low(m):
                pool.wait_ge(s_hi_done, m + 1)
                nc.gpsimd.tensor_tensor(s_pair[:, m % SRING, 1, :], s_hid[:, m % 2, :], s_pair[:, m % SRING, 0, :], ALU.subtract).then_inc(s_lo_done[0], 1)

            def scatter(n):
                pool.wait_ge(routed, n + 1)
                pool.wait_ge(rows_lo, B * (n + 1))
                pool.wait_ge(padded, 64)
                for i in range(TT):
                    for k in range(2):
                        nc.gpsimd.indirect_dma_start(
                            out=sorted_rows[n], out_offset=bass.IndirectOffsetOnAxis(ap=place[k][:, i:i + 1], axis=0),
                            in_=row_words[:, i, :], in_offset=None).then_inc(scattered[n], 16)

            def add_results(n):
                for b in range(B):
                    pool.wait_ge(x_stored[n][b], 16)

                def body(j, q, k, last):
                    pool.wait_ge(y_ready[n], j + 1)
                    pool.wait_ge(meta_in[k][n], 16 * (q + 1))
                    if at_least(j, 1):
                        pool.wait_ge(added[n], 16 * j)
                    pool.sem_inc(turn_taken[n], 1)
                    nc.gpsimd.indirect_dma_start(
                        out=x_sum[n], out_offset=bass.IndirectOffsetOnAxis(ap=meta[:, k, M_TOK:M_TOK + 1].bitcast(I32), axis=0),
                        in_=y_sb[:, k, :], in_offset=None, compute_op=ALU.add).then_inc(added[n], 16)

                tile_loop(pool, n, body)

            reciprocal_roots(0, B + 1)
            for s in range(4, 8):
                rows(s)
                if s < 7:
                    reciprocal_roots(s + 1, 1)
            for m in range(POOL_BLOCKS):
                shared_low(m)
            scatter(0)
            add_results(0)
            reciprocal_roots(2 * B, 2 * B + 1)
            for s in range(12, 16):
                rows(s)
                if s < 15:
                    reciprocal_roots(s + B + 1, 1)
            scatter(1)
            add_results(1)

        @block.tensor
        def _(pe):
            expert_at = [pe.alloc_register(f"expert_at{k}") for k in range(2)]
            w1_at = [[[BlockAddress(f"w1_at{f}_{c}_{l}", 2048 * l + 1024 * c + P * f, P, True) for l in range(2)]
                      for c in range(DC)] for f in range(FC)]
            w2_at = [BlockAddress(f"w2_at{f}", 4096 + 2 * D * f, 2 * D, False) for f in range(FC)]
            pe.wait_ge(in_const, 32)
            pe.wait_ge(in_ctx, 16)
            for c in range(DC):
                for t in range(2):
                    m = nc.tensor.transpose(bank[6][:, c * D + t * P:c * D + t * P + P], ctx_in[:, t, c * P:c * P + P], ident)
            m.then_inc(pe_setup, 1)
            pe.wait_ge(in_w, 16 * 7)
            for i, w in enumerate((0, 1, 2, 3, 5, 6)):
                for c in range(DC):
                    for o in range(DC):
                        m = nc.tensor.transpose(bank[i][:, c * D + o * P:c * D + o * P + P], w_in[:, w, o, c * P:c * P + P], ident)
            m.then_inc(pe_setup, 1)
            pe.wait_ge(in_few, 16 * 6)
            for n in range(2):
                ne = E + 1 - n
                for f in range(FC):
                    at = 128 * n + f * ne
                    nc.tensor.transpose(bank[7][:, at:at + ne], b1_rows[n][0:ne, f * P:f * P + P], ident[0:ne, 0:ne])
            for c in range(DC):
                m = nc.tensor.transpose(bank[7][:, 256 + c * E:256 + c * E + E], gate_rows[:, c * P:c * P + P], ident[0:E, 0:E])
            m = nc.tensor.transpose(bank[7][:, 256 + DC * E:256 + DC * E + DC], bq_rows, ident[0:DC, 0:DC])
            m.then_inc(pe_setup, 1)
            pe.wait_ge(act_setup, 1)
            pe.wait_ge(dve_setup, 4)
            for o in range(DC):
                for c in range(DC):
                    m = nc.tensor.matmul(bank[0][:, o * D:o * D + D], wT[:, 1, c, o * P:o * P + P], ctxT[:, c, :], start=c == 0, stop=c == DC - 1)
            for b in range(B):
                for c in range(DC):
                    m = nc.tensor.matmul(bank[1 + b // 2][:, b % 2 * D:b % 2 * D + D], ctxT2[:, c, b, :], wT[:, 2, c, :], start=c == 0, stop=c == DC - 1)
            m.then_inc(pe_setup, 1)
            for w in range(2):
                for t in range(2):
                    for c in range(DC):
                        m = nc.tensor.matmul(bank[3 + w][:, t * D:t * D + D], ctxT[:, c, t * P:t * P + P], wT1[:, w, c, :], start=c == 0, stop=c == DC - 1)
            m.then_inc(pe_setup, 1)
            pe.wait_ge(dve_setup, 7)
            for b in range(B):
                r = slice(SC * (b % 2), SC * (b % 2) + SC)
                for c in range(DC):
                    m = nc.tensor.matmul(bank[5 + b % 2][:, (b // 2 * DC + c) * P:(b // 2 * DC + c) * P + P], kv1[r, 0, b // 2, c * P:c * P + P],
                                         kv1[r, 1, b // 2, c * P:c * P + P], start=True, stop=True)
            m.then_inc(pe_setup, 1)
            pe.wait_ge(dve_setup, 8)
            for b in range(B):
                for c in range(DC):
                    for e in range(DC):
                        at = c * D + e * P
                        m = nc.tensor.matmul(bank[b][:, at:at + P], w_in[:, 4, e, c * P:c * P + P], kv_block[:, b, e, :], start=True, stop=True)
            m.then_inc(pe_setup, 1)
            for b in range(B):
                for e in range(DC):
                    at = b % 2 * D + e * P
                    m = nc.tensor.matmul(bank[4 + b // 2][:, at:at + P], bq_wide[:, e, :], kv_block[:, b, e, :], start=True, stop=True)
            m.then_inc(pe_setup, 1)
            pe.wait_ge(act_setup, 5)
            pe.wait_ge(dve_setup, 9)

            def transposed(s):
                pe.wait_ge(ln_done, s + 1)
                if s:
                    pe.wait_ge(xlnT_ready, s)
                for c in range(DC):
                    for t in range(TB):
                        m = nc.tensor.transpose(tp_ps[c][:, t * P:t * P + P], xln[:, s % 2, t, c * P:c * P + P], ident)
                m.then_inc(tp_done, 1)

            transposed(0)
            for b in range(B):
                pe.wait_ge(xlnT_ready, b + 1)
                if b:
                    pe.wait_ge(o_ready, b)
                for o in range(DC):
                    for c in range(DC):
                        m = nc.tensor.matmul(q_ps[o][:, :], wT[:, 0, c, o * P:o * P + P], xlnT[:, b % 2, c, :], start=c == 0, stop=c == DC - 1)
                m.then_inc(q_done, 1)
                transposed(b + 1)
                pe.wait_ge(q_ready, b + 1)
                for h in range(HP):
                    n = HP * b + h
                    if n >= 2:
                        pe.wait_ge(prob_ready, n - 1)
                    c, g = h // 4, 32 * (h % 4)
                    nc.tensor.matmul(s_ps[h % 2][:, :], k_heads[g:g + 32, c, b, :], qT[g:g + 32, c, :], start=True, stop=True).then_inc(score_done, 1)
                for h in range(HP):
                    pe.wait_ge(prob_ready, HP * b + h + 1)
                    c, g = h // 4, 32 * (h % 4)
                    m = nc.tensor.matmul(q_ps[c][g:g + 32, :], v_heads[:, b, 32 * h:32 * h + 32], probs[:, h, :], start=True, stop=True)
                m.then_inc(o_done, 1)
                pe.wait_ge(o_ready, b + 1)
                for t in range(TB):
                    n = TB * b + t
                    if n >= 2:
                        pe.wait_ge(x_updated, n - 1)
                    for c in range(DC):
                        m = nc.tensor.matmul(p_ps[n % 2][:, 0:D], oT[:, c, t * P:t * P + P], wT[:, 3, c, :], start=c == 0, stop=c == DC - 1)
                    m.then_inc(proj_done, 1)

            def logits(n, s):
                pe.wait_ge(xlnT_ready, s + 1)
                for t in range(TB):
                    i = TB * (s % B) + t
                    for c in range(DC):
                        m = nc.tensor.matmul(p_ps[0][:, i * E:i * E + E], xlnT[:, s % 2, c, t * P:t * P + P], gate_cols[:, n, c, :], start=c == 0, stop=c == DC - 1)
                m.then_inc(xlnT_used, 1)

            def router_logits(n):
                pe.wait_ge(x_updated, TT * (n + 1))
                for b in range(B):
                    s = 8 * n + 4 + b
                    logits(n, s)
                    if b < B - 1:
                        transposed(s + 1)

            def router_counts(n):
                pe.wait_ge(picked_ready, n + 1)
                counts = p_ps[1][:, 0:(TT + 1) * E]
                m = nc.tensor.matmul(counts, before16[:, :], picked16[:, :, :].rearrange("p t e -> p (t e)"), start=True, stop=False)
                for i in range(TT):
                    k = TT - i
                    m = nc.tensor.matmul(p_ps[1][:, (i + 1) * E:(TT + 1) * E], ones16[:, :],
                                         picked16[:, i, :].unsqueeze(1).broadcast_to([P, k, E]), start=False, stop=i == TT - 1)
                m.then_inc(count_done, 1)

            def shared_turn(i):
                if i:
                    pe.wait_ge(s_xT_ready, i)
                for t in range(2):
                    for c in range(2 * DC):
                        m = nc.tensor.transpose(s_xT_ps[:, c, t * P:t * P + P], rows_out[:, 2 * i + t, c * P:c * P + P], ident16[:, :])
                m.then_inc(s_turned, 1)

            def shared_up(m):
                b, f = m // FC, m % FC
                if f == 0:
                    pe.wait_ge(s_xT_ready, 2 * (b + 1))
                if m >= 2:
                    pe.wait_ge(s_gelu_done, m - 1)
                o = s_h_ps[m % 2][:, :]
                for c in range(DC):
                    hi, lo = s_xT[:, c, :], s_xT[:, DC + c, :]
                    w_hi, w_lo = (weights[:, SHARED, 2048 * l + 1024 * c + P * f:2048 * l + 1024 * c + P * f + P] for l in range(2))
                    nc.tensor.matmul(o, w_hi, hi, start=c == 0, stop=False)
                    nc.tensor.matmul(o, w_hi, lo, start=False, stop=False)
                    i = nc.tensor.matmul(o, w_lo, hi, start=False, stop=c == DC - 1)
                i.then_inc(s_up_done, 1)

            def shared_down(m):
                b, f = m // FC, m % FC
                low_ready(pe, m)
                at = 4096 + 2 * D * f
                for t in range(TB):
                    if f == 0 and b:
                        pe.wait_ge(s_added, TB * (b - 1) + t + 1)
                    hi, lo = (s_pair[:, m % SRING, l, t * P:t * P + P] for l in range(2))
                    if f < FC - 1:
                        nc.tensor.matmul(s_y_ps[t][:, :], hi, weights[:, SHARED, at:at + 2 * D], start=f == 0, stop=False)
                        i = nc.tensor.matmul(s_y_ps[t][:, 0:D], lo, weights[:, SHARED, at:at + D], start=False, stop=False)
                    else:
                        nc.tensor.matmul(s_y_ps[t][:, 0:D], lo, weights[:, SHARED, at:at + D], start=False, stop=False)
                        i = nc.tensor.matmul(s_y_ps[t][:, :], hi, weights[:, SHARED, at:at + 2 * D], start=False, stop=True)
                i.then_inc(s_down_done, 1)

            def shared_expert():
                pe.wait_ge(rows_lo, B)
                pe.wait_ge(logits_done, 1)
                pe.wait_ge(split_lo, 4)
                shared_turn(0)
                shared_turn(1)
                for m in range(B * FC):
                    b, f = m // FC, m % FC
                    if f == 0 and b:
                        shared_turn(2 * b + 1)
                        shared_down(m - 2)
                    shared_up(m)
                    if m >= 2 and f:
                        shared_down(m - 2)
                    if f == FC - 2 and b < B - 1:
                        shared_turn(2 * b + 2)
                    if m == FC:
                        router_counts(0)
                shared_down(B * FC - 2)
                shared_down(B * FC - 1)

            def ffn(n):
                pe.wait_ge(count_done, n + 1)
                pe.wait_ge(routed, n + 1)
                pe.wait_ge(split_lo, unit_count[0] + (unit_count[1] if n else 0))
                if n == 0:
                    pe.wait_ge(s_added, TT)

                def turn(j, q, k):
                    pe.wait_ge(row_in[k][n], 16 * (q + 1))
                    if at_least(j, 2):
                        pe.wait_ge(xT_ready[n], j - 1)
                    for i in range(2 * DC):
                        m = nc.tensor.transpose(xT_ps[k][:, i * P:i * P + P], rows_in[:, k, i * P:i * P + P], ident16[:, :])
                    m.then_inc(rowT_done[n], 1)

                def up(j, q, k):
                    pe.wait_ge(xT_ready[n], j + 1)
                    for half in range(2):
                        if at_least(j, 2):
                            pe.wait_ge(gelu_done[half][n], j - 1)
                        for g in range(FC // 2):
                            f = half * FC // 2 + g
                            o = h_ps[k][half][:, g * P:g * P + P]
                            for c in range(DC):
                                hi, lo = xT[:, k, c * P:c * P + P], xT[:, k, (DC + c) * P:(DC + c) * P + P]
                                nc.tensor.matmul(o, w1_at[f][c][0].block(), hi, start=c == 0, stop=False)
                                nc.tensor.matmul(o, w1_at[f][c][0].block(), lo, start=False, stop=False)
                                m = nc.tensor.matmul(o, w1_at[f][c][1].block(), hi, start=False, stop=c == DC - 1)
                        m.then_inc(up_done[n], 1)

                def down(j, k, after_block):
                    if at_least(j, 2):
                        pe.wait_ge(y_read[n], j - 1)
                    for f in range(FC):
                        if f % (FC // 2) == 0:
                            pe.wait_ge(hid_ready[f // (FC // 2)][n], j + 1)
                        hi, lo = hid_hi[:, k, f * P:f * P + P], hid_lo[:, k, f * P:f * P + P]
                        if f < FC - 1:
                            nc.tensor.matmul(y_ps[k][:, :], hi, w2_at[f].block(), start=f == 0, stop=False)
                            nc.tensor.matmul(y_ps[k][:, 0:D], lo, w2_at[f].block(D), start=False, stop=False)
                        else:
                            nc.tensor.matmul(y_ps[k][:, 0:D], lo, w2_at[f].block(D), start=False, stop=False)
                            m = nc.tensor.matmul(y_ps[k][:, :], hi, w2_at[f].block(), start=False, stop=True)
                        if f == FC - 1:
                            m.then_inc(down_done[n], 1)
                        after_block(f)

                def load_expert(j, k):
                    pe.reg_load(expert_at[k], tile_expert_i[0:1, bass.ds(j, 1)])
                    pe.reg_alu(expert_at[k], expert_at[k], 2 * SLOT, ALU.mult)

                w1_blocks = [w1_at[f][c][l] for f in range(FC) for c in range(DC) for l in range(2)]

                def body(j, q, k, last):
                    if before_end(j, 1):
                        turn(j + 1, q + (1 if k else 0), 1 - k)
                    up(j, q, k)

                    def after_block(f):
                        if f == 0 and before_end(j, 1):
                            load_expert(j + 1, 1 - k)
                        w2_at[f].point(expert_at[k])
                        if f and before_end(j, 1):
                            for i in range(len(w1_blocks) * (f - 1) // (FC - 1), len(w1_blocks) * f // (FC - 1)):
                                w1_blocks[i].point(expert_at[1 - k])

                    if at_least(j, 1):
                        down(j - 1, 1 - k, after_block)
                    else:
                        for f in range(FC):
                            after_block(f)

                load_expert(0, 0)
                for i in w1_blocks:
                    i.point(expert_at[0])
                turn(0, 0, 0)
                tile_loop(pe, n, body)
                down(ROUTED - 1, (ROUTED - 1) % 2, lambda f: None)

            router_logits(0)
            shared_expert()
            ffn(0)

            pe.wait_ge(late_in, 64)
            pe.wait_ge(y_read[0], ROUTED)
            transposed(8)
            for b in range(B):
                s = 8 + b
                pe.wait_ge(xlnT_ready, s + 1)
                for t in range(TB):
                    i = TB * b + t
                    if i >= 2:
                        pe.wait_ge(o_ready, B + i - 1)
                    for c in range(DC):
                        m = nc.tensor.matmul(p_ps[i % 2][:, 0:D], xlnT[:, s % 2, c, t * P:t * P + P], kvm[:, b, c, :], start=c == 0, stop=c == DC - 1)
                    m.then_inc(proj_done, 1)
                transposed(s + 1)
            router_logits(1)
            router_counts(1)
            ffn(1)

        @block.scalar
        def _(act):
            act.wait_ge(in_bias, 64)
            nc.scalar.activation(gates[:, 0:4], gates[:, 0:4], ACT.Tanh).then_inc(g_ready, 1)
            act.wait_ge(pe_setup, 2)
            for i in range(4):
                m = nc.scalar.activation(wT[:, i, :, :].rearrange("p c o -> p (c o)"), bank[i][:, :], ACT.Copy)
            m.then_inc(act_setup, 1)
            act.wait_ge(pe_setup, 7)
            for b in range(B):
                nc.scalar.activation(kvm_out[:, b * 512:b * 512 + 512], bank[b][:, :], ACT.Copy).then_inc(act_setup, 1)

            def split(n, u):
                act.wait_ge(in_raw[raw_no(n, u)], raw_loaded(n, u))
                nc.scalar.activation(split_to(n, u, 0), raw_at(n, u), ACT.Copy, scale=W_SCALE).then_inc(split_hi, 1)

            def read_out(s):
                act.wait_ge(tp_done, s + 1)
                nc.scalar.activation(xlnT[:, s % 2, 0, :], tp_ps[0][:, :], ACT.Copy)
                nc.scalar.activation(xlnT[:, s % 2, 1, :], tp_ps[1][:, :], ACT.Copy).then_inc(xlnT_ready, 1)

            read_out(0)
            for b in range(B):
                act.wait_ge(q_done, b + 1)
                nc.scalar.activation(qT[:, 0, :], q_ps[0][:, :], ACT.Copy)
                nc.scalar.activation(qT[:, 1, :], q_ps[1][:, :], ACT.Copy).then_inc(q_ready, 1)
                read_out(b + 1)
                for h in range(HP):
                    act.wait_ge(score_done, HP * b + h + 1)
                    nc.scalar.activation(probs[:, h, :], s_ps[h % 2][:, :], ACT.Sigmoid, scale=float(DH) ** -0.5).then_inc(prob_ready, 1)
                if b == 0:
                    act.wait_ge(pe_setup, 8)
                    act.wait_ge(dve_setup, 9)
                    act.wait_ge(kv_stored, 32)
                early, late_ = attention_splits(b)
                for u in early:
                    split(0, u)
                act.wait_ge(o_done, b + 1)
                nc.scalar.activation(oT[:, 0, :], q_ps[0][:, :], ACT.Copy)
                nc.scalar.activation(oT[:, 1, :], q_ps[1][:, :], ACT.Copy).then_inc(o_ready, 1)
                for u in late_:
                    split(0, u)

            def rows(s):
                b = s % B
                act.wait_ge(ln_done, s + 1)
                if s >= 8:
                    act.wait_ge(x_updated, 2 * TT)
                nc.scalar.activation(rows_out[:, TB * b:TB * b + TB, 0:D], xln[:, s % 2, :, :], ACT.Copy).then_inc(rows_hi, 1)

            def turn_logits(n):
                for b in range(B):
                    s = 8 * n + 4 + b
                    if b:
                        if b > 1:
                            act.wait_ge(xlnT_used, 4 * n + b - 1)
                        read_out(s)
                    rows(s)

            def weights_of_experts(n):
                act.wait_ge(diff_ready, n + 1)
                nc.scalar.activation(gate_w[0][:, :], top[0][:, :], ACT.Sigmoid)
                nc.scalar.activation(gate_w[1][:, :], top[0][:, :], ACT.Sigmoid, scale=-1.0).then_inc(sig_ready, 1)

            def shared_expert():
                for m in range(B * FC):
                    b, f = m // FC, m % FC
                    if f == 0:
                        for half in range(2):
                            act.wait_ge(s_turned, 2 * b + half + 1)
                            if half == 0 and b:
                                act.wait_ge(s_up_done, FC * b)
                            nc.scalar.activation(s_xT[:, :, half * 2 * P:(half + 1) * 2 * P], s_xT_ps, ACT.Copy).then_inc(s_xT_ready, 1)
                    act.wait_ge(s_up_done, m + 1)
                    if m >= 2:
                        low_ready(act, m - 2)
                    nc.scalar.activation(s_hid[:, m % 2, :], s_h_ps[m % 2][:, :], ACT.Gelu, bias=b1_cols[0][:, f, E:E + 1],
                                         scale=1.0 / W_SCALE).then_inc(s_gelu_done, 1)
                    act.wait_ge(s_gelu_done, m + 1)
                    if m >= SRING:
                        act.wait_ge(s_down_done, m - SRING + 1)
                    nc.scalar.activation(s_pair[:, m % SRING, 0, :], s_hid[:, m % 2, :], ACT.Copy).then_inc(s_hi_done, 1)
                    if m == FC // 2:
                        weights_of_experts(0)
                    u = shared_splits(m)
                    if u is not None:
                        split(0, u)

            def ffn(n):
                act.wait_ge(routed, n + 1)

                def body(j, q, k, last):
                    e = expert_of(act, j)
                    for half in range(2):
                        act.wait_ge(up_done[n], 2 * j + half + 1)
                        if at_least(j, 2):
                            act.wait_ge(hid_ready[half][n], j - 1)
                        for g in range(FC // 2):
                            f = half * FC // 2 + g
                            m = nc.scalar.activation(hid[:, k, f * P:f * P + P], h_ps[k][half][:, g * P:g * P + P], ACT.Gelu,
                                                     bias=b1_cols[n][:, f, bass.ds(e, 1)], scale=1.0 / W_SCALE)
                        m.then_inc(gelu_done[half][n], 1)

                tile_loop(act, n, body)

            turn_logits(0)
            act.wait_ge(proj_done, TT)
            shared_expert()
            ffn(0)
            act.wait_ge(down_done[0], ROUTED)
            for b in range(B):
                read_out(8 + b)
                for u in attention1_splits(b):
                    split(1, u)
            read_out(8 + B)
            turn_logits(1)
            weights_of_experts(1)
            ffn(1)

        @block.vector
        def _(dve):
            V = nc.vector
            chain, norms = [0], [0]

            def link(ins):
                chain[0] += 1
                ins.then_inc(dve_step, 1)
                dve.wait_ge(dve_step, chain[0])

            dve.wait_ge(in_const, 32)
            dve.wait_ge(consts_ready, 4)
            link(V.tensor_copy(padding_row[:, 2 * D:ROW].bitcast(I32)[:, M_TOK:M_TOK + 1], cst("trash")))
            V.tensor_copy(ident16[:, :], ident).then_inc(pad_ready, 1)
            link(V.tensor_copy(before16[:, :], cst("before")))
            dve.wait_ge(pe_setup, 1)
            ctx_ps = bank[6][:, :].rearrange("p (c s) -> p c s", c=DC)
            V.tensor_copy(ctxT[:, :, :], ctx_ps).then_inc(dve_setup, 1)
            for c in range(DC):
                m = V.tensor_copy(ctxT2[:, c, :, :].rearrange("p b (j s) -> p b j s", j=2),
                                  ctx_ps[:, c, :].rearrange("p (b s) -> p b s", b=B).unsqueeze(2).broadcast_to([P, B, 2, SC]))
            m.then_inc(dve_setup, 1)
            dve.wait_ge(pe_setup, 2)
            for w in range(2):
                m = V.tensor_copy(wT1[:, w, :, :].rearrange("p c o -> p (c o)"), bank[4 + w][:, :])
            m.then_inc(dve_setup, 1)
            dve.wait_ge(pe_setup, 3)
            for n in range(2):
                ne = E + 1 - n
                V.tensor_copy(b1_cols[n][:, :, :].rearrange("p f e -> p (f e)"), bank[7][:, 128 * n:128 * n + FC * ne])
            V.tensor_copy(gate_cols[:, 0, :, :].rearrange("p c e -> p (c e)"), bank[7][:, 256:256 + DC * E]).then_inc(dve_setup, 1)
            dve.wait_ge(pe_setup, 4)
            kT = bank[0][:, :].rearrange("p (c b s) -> p c b s", c=DC, b=B)
            for c in range(DC):
                for j in range(2):
                    V.tensor_scalar(k_heads[:, c, :, SC * j:SC * j + SC], kT[:, c, :, :], cst("kmask")[:, j:j + 1], None, ALU.mult)
            for b in range(B):
                m = V.tensor_tensor(v_heads[:, b, :], bank[1 + b // 2][:, b % 2 * D:b % 2 * D + D], cst("vmask"), ALU.mult)
            m.then_inc(dve_setup, 1)
            dve.wait_ge(pe_setup, 5)
            dve.wait_ge(in_bias, 64)
            for w in range(2):
                for t in range(2):
                    m = V.tensor_tensor(kv1[:, w, t, :], bank[3 + w][:, t * D:t * D + D], kv1_bias[:, w, :], ALU.add)
            m.then_inc(dve_setup, 1)
            V.tensor_copy(bq_wide[:, :, :], bank[7][:, 256 + DC * E:256 + DC * E + DC].unsqueeze(2).broadcast_to([P, DC, P])).then_inc(dve_setup, 1)
            dve.wait_ge(pe_setup, 6)
            for b in range(B):
                for c in range(DC):
                    at = (b // 2 * DC + c) * P
                    m = V.tensor_tensor(kv_block[:, b, c, :], bank[5 + b % 2][:, at:at + P], cst("kvmask"), ALU.mult)
            m.then_inc(dve_setup, 1)
            dve.wait_ge(pe_setup, 8)
            V.tensor_copy(kvb_out[:, 0:512], bank[4][:, :])
            V.tensor_copy(kvb_out[:, 512:1024], bank[5][:, :]).then_inc(dve_setup, 1)

            def split(n, u):
                dve.wait_ge(split_hi, unit_no(n, u) + 1)
                V.scalar_tensor_tensor(split_to(n, u, 1), raw_at(n, u), W_SCALE, split_to(n, u, 0), ALU.mult, ALU.subtract).then_inc(split_lo, 1)

            def normalise(src, dst):
                for t in range(TB):
                    m = V.bn_stats(ln_stats[:, t, :], src[:, t, :])
                link(m)
                for t in range(TB):
                    m = V.bn_aggr(ln_mv[:, t, :], ln_stats[:, t, :])
                link(m)
                V.tensor_scalar(ln_rstd[:, :], ln_mv[:, :, 1], EPS, None, ALU.add).then_inc(var_ready, 1)
                norms[0] += 1
                dve.wait_ge(rstd_ready, norms[0])
                for t in range(TB):
                    m = V.tensor_scalar(dst[:, t, :], src[:, t, :], ln_mv[:, t, 0:1], ln_rstd[:, t:t + 1], ALU.subtract, ALU.mult)
                return m

            def batch(b):
                return x_sb[:, TB * b:TB * b + TB, :]

            def layer_norm(s):
                if s >= 2:
                    dve.wait_ge(tp_done, s - 1)
                if s % 8 >= 6:
                    dve.wait_ge(rows_lo, s // 8 * B + s % 8 - 5)
                normalise(batch(s % B), xln[:, s % 2, :, :]).then_inc(ln_done, 1)

            def add_attention0(b):
                dve.wait_ge(g_ready, 1)
                for t in range(TB):
                    n = TB * b + t
                    dve.wait_ge(proj_done, n + 1)
                    m = V.scalar_tensor_tensor(x_sb[:, n, :], p_ps[n % 2][:, 0:D], gates[:, 0:1], x_sb[:, n, :], ALU.mult, ALU.add)
                    if t < TB - 1:
                        m.then_inc(x_updated, 1)
                m.then_inc(x_updated, 1)
                dve.wait_ge(x_updated, TB * b + TB)

            def wide(ap, n):
                return ap.unsqueeze(2).broadcast_to([P, TT, n])

            def pick_experts(n):
                dve.wait_ge(xlnT_used, 4 * (n + 1))
                V.tensor_copy(lg[:, :, :].rearrange("p t e -> p (t e)"), p_ps[0][:, 0:TT * E]).then_inc(logits_done, 1)
                dve.wait_ge(logits_done, n + 1)
                rev = cst("rev").unsqueeze(1).broadcast_to([P, TT, E])
                for k in range(2):
                    link(V.reduce_max(top[k][:, :], lg[:, :, :], AX))
                    link(V.tensor_tensor(r_a[:, :, :], lg[:, :, :], wide(top[k][:, :], E), ALU.is_equal))
                    link(V.tensor_tensor(r_a[:, :, :], r_a[:, :, :], rev, ALU.mult))
                    link(V.reduce_max(order[k][:, :], r_a[:, :, :], AX))
                    link(V.tensor_tensor(pick[k][:, :, :], rev, wide(order[k][:, :], E), ALU.is_equal))
                    if k == 0:
                        link(V.scalar_tensor_tensor(lg[:, :, :], pick[0][:, :, :], -3.0e38, lg[:, :, :], ALU.mult, ALU.add))
                V.tensor_tensor(picked16[:, 0:TT, :], pick[0][:, :, :], pick[1][:, :, :], ALU.add).then_inc(picked_ready, 1)
                V.tensor_tensor(top[0][:, :], top[0][:, :], top[1][:, :], ALU.subtract).then_inc(diff_ready, 1)

            def place_rows(n):
                dve.wait_ge(count_done, n + 1)
                counts = p_ps[1][:, 0:(TT + 1) * E]
                link(V.tensor_copy(r_a[:, :, :].rearrange("p t e -> p (t e)"), counts[:, 0:TT * E]))
                link(V.tensor_copy(n_tiles[:, :], counts[:, TT * E:(TT + 1) * E]))
                full = cst("full").unsqueeze(1).broadcast_to([P, E, TT])
                need = lg[:, :, :].rearrange("p t e -> p (t e)").rearrange("p (e t) -> p e t", e=E)
                link(V.tensor_tensor(need, n_tiles[:, :].unsqueeze(2).broadcast_to([P, E, TT]), full, ALU.is_gt))
                link(V.reduce_sum(n_tiles[:, :], need, AX))
                upto = lg[:, 0:E, :]
                link(V.tensor_tensor(upto, n_tiles[:, :].unsqueeze(1).broadcast_to([P, E, E]),
                                     cst("upto").rearrange("p (e i) -> p e i", e=E), ALU.mult))
                link(V.reduce_sum(end_tile[:, :], upto, AX))
                link(V.tensor_tensor(base_row[:, :], end_tile[:, :], n_tiles[:, :], ALU.subtract))
                link(V.tensor_scalar(base_row[:, :], base_row[:, :], float(P), None, ALU.mult))
                link(V.tensor_tensor(r_a[:, :, :], r_a[:, :, :], base_row[:, :].unsqueeze(1).broadcast_to([P, TT, E]), ALU.add))
                for k in range(2):
                    link(V.tensor_tensor(lg[:, :, :], pick[k][:, :, :], r_a[:, :, :], ALU.mult))
                    link(V.reduce_sum(top[1][:, :], lg[:, :, :], AX))
                    link(V.tensor_copy(place[k][:, :], top[1][:, :]))
                for first in range(0, ROUTED, TT):
                    m = min(TT, ROUTED - first)
                    past = lg[:, 0:m, :]
                    link(V.tensor_tensor(past, cst("tile")[:, first:first + m].unsqueeze(2).broadcast_to([P, m, E]),
                                         end_tile[:, :].unsqueeze(1).broadcast_to([P, m, E]), ALU.is_ge))
                    link(V.reduce_sum(tile_expert[:, first:first + m], past, AX))
                link(V.tensor_scalar(tile_expert[:, :], tile_expert[:, :], float(E - 1), None, ALU.min))
                link(V.tensor_copy(tile_expert_i[:, :], tile_expert[:, :]))
                g = gates[:, 2 + n:3 + n]
                link(V.tensor_copy(rows_meta.bitcast(I32)[:, :, M_TOK], cst("token")))
                dve.wait_ge(sig_ready, n + 1)
                link(V.tensor_scalar(gate_w[0][:, :], gate_w[0][:, :], g, None, ALU.mult))
                link(V.tensor_scalar(gate_w[1][:, :], gate_w[1][:, :], g, None, ALU.mult))
                link(V.tensor_copy(rows_meta[:, :, M_W2], gate_w[1][:, :]))
                link(V.tensor_tensor(rows_meta[:, :, M_DW], gate_w[0][:, :], gate_w[1][:, :], ALU.subtract))
                V.tensor_scalar(rows_meta[:, :, M_E1], order[0][:, :], -1.0, float(E), ALU.mult, ALU.add).then_inc(routed, 1)

            def shared_low(m):
                dve.wait_ge(s_hi_done, m + 1)
                V.tensor_tensor(s_pair[:, m % SRING, 1, :], s_hid[:, m % 2, :], s_pair[:, m % SRING, 0, :], ALU.subtract).then_inc(s_lo_done[1], 1)

            def shared_result(b):
                if b == 0:
                    dve.wait_ge(in_sb2, 16)
                    link(V.tensor_scalar(sb2_row, sb2_row, gates[:, 2:3], None, ALU.mult))
                    link(V.tensor_scalar(gates[:, 4:5], gates[:, 2:3], 1.0 / W_SCALE, None, ALU.mult))
                V.tensor_tensor(batch(b), batch(b), sb2_row.unsqueeze(1).broadcast_to([P, TB, D]), ALU.add).then_inc(s_biased, 1)
                dve.wait_ge(s_biased, (TB + 1) * b + 1)
                dve.wait_ge(s_down_done, FC * (b + 1))
                for t in range(TB):
                    x_tile = x_sb[:, TB * b + t, :]
                    V.scalar_tensor_tensor(x_tile, s_y_ps[t][:, 0:D], gates[:, 4:5], x_tile, ALU.mult, ALU.add).then_inc(s_biased, 1)
                for t in range(TB):
                    x_tile = x_sb[:, TB * b + t, :]
                    dve.wait_ge(s_biased, (TB + 1) * b + 2 + t)
                    V.scalar_tensor_tensor(x_tile, s_y_ps[t][:, D:2 * D], gates[:, 4:5], x_tile, ALU.mult, ALU.add).then_inc(s_added, 1)

            def ffn(n):
                dve.wait_ge(b2_in[n], 16)

                def turned(j, k):
                    dve.wait_ge(rowT_done[n], j + 1)
                    if at_least(j, 2):
                        dve.wait_ge(up_done[n], 2 * (j - 1))
                    V.tensor_copy(xT[:, k, :], xT_ps[k]).then_inc(xT_ready[n], 1)

                def split_hidden(j, k):
                    if at_least(j, 2):
                        dve.wait_ge(down_done[n], j - 1)
                    for half in range(2):
                        f = slice(half * F // 2, (half + 1) * F // 2)
                        dve.wait_ge(gelu_done[half][n], j + 1)
                        V.tensor_copy(hid_hi[:, k, f], hid[:, k, f]).then_inc(hi_done[n], 1)
                        dve.wait_ge(hi_done[n], 2 * j + half + 1)
                        V.tensor_tensor(hid_lo[:, k, f], hid[:, k, f], hid_hi[:, k, f], ALU.subtract).then_inc(hid_ready[half][n], 1)

                def result(j, q, k):
                    e = expert_of(dve, j)
                    dve.wait_ge(meta_in[k][n], 16 * (q + 1))
                    V.tensor_scalar(pick_w[:, k:k + 1], meta[:, k, M_E1:M_E1 + 1], tile_expert[:, bass.ds(j, 1)], meta[:, k, M_DW:M_DW + 1],
                                    ALU.is_equal, ALU.mult).then_inc(biased[n], 1)
                    dve.wait_ge(biased[n], 3 * j + 1)
                    V.tensor_tensor(pick_w[:, k:k + 1], pick_w[:, k:k + 1], meta[:, k, M_W2:M_W2 + 1], ALU.add).then_inc(biased[n], 1)
                    dve.wait_ge(down_done[n], j + 1)
                    if at_least(j, 2):
                        dve.wait_ge(added[n], 16 * (j - 1))
                    V.scalar_tensor_tensor(y_sb[:, k, :], y_ps[k][:, 0:D], 1.0 / W_SCALE, b2_rows[:, bass.ds(e, 1), :].rearrange("p a d -> p (a d)"),
                                           ALU.mult, ALU.add).then_inc(biased[n], 1)
                    dve.wait_ge(biased[n], 3 * j + 3)
                    V.scalar_tensor_tensor(y_sb[:, k, :], y_ps[k][:, D:2 * D], 1.0 / W_SCALE, y_sb[:, k, :], ALU.mult, ALU.add).then_inc(y_read[n], 1)
                    dve.wait_ge(y_read[n], j + 1)
                    V.tensor_scalar(y_sb[:, k, :], y_sb[:, k, :], pick_w[:, k:k + 1], None, ALU.mult).then_inc(y_ready[n], 1)

                def body(j, q, k, last):
                    if before_end(j, 1):
                        turned(j + 1, 1 - k)
                    split_hidden(j, k)
                    if at_least(j, 1):
                        result(j - 1, q - (0 if k else 1), 1 - k)

                turned(0, 0)
                tile_loop(dve, n, body)
                result(ROUTED - 1, (ROUTED - 1) // 2, (ROUTED - 1) % 2)

            for b in range(2):
                dve.wait_ge(in_x[b], 16)
                layer_norm(b)
            for b in range(B):
                early, late_ = attention_splits(b)
                for u in early:
                    split(0, u)
                add_attention0(b)
                if b < 2:
                    dve.wait_ge(in_x[b + 2], 16)
                if b < 3:
                    layer_norm(b + 2)
                for u in late_:
                    split(0, u)
            for s in range(5, 8):
                layer_norm(s)
            pick_experts(0)
            for m in range(FC):
                if shared_splits(m) is not None:
                    split(0, shared_splits(m))
            shared_result(0)
            place_rows(0)
            shared_result(1)
            for m in range(2 * FC, 4 * FC):
                shared_low(m)
                if shared_splits(m) is not None:
                    split(0, shared_splits(m))
                if m % FC == FC - 1:
                    shared_result(m // FC)
            ffn(0)
            dve.wait_ge(late_in, 64)
            link(V.tensor_scalar(gamma, gamma, gates[:, 1:2], None, ALU.mult))
            link(V.tensor_scalar(beta, beta, gates[:, 1:2], None, ALU.mult))

            def add_attention1(b):
                s = 8 + b
                dve.wait_ge(tp_done, s + 1)
                u = xln[:, s % 2, :, :]
                link(V.tensor_tensor(u, u, kvb[:, b, :].unsqueeze(1).broadcast_to([P, TB, D]), ALU.add))
                for t in range(TB):
                    i = TB * b + t
                    dve.wait_ge(proj_done, TT + i + 1)
                    m = V.tensor_tensor(u[:, t, :], p_ps[i % 2][:, 0:D], u[:, t, :], ALU.add)
                    m.then_inc(o_ready, 1)
                dve.wait_ge(o_ready, B + TB * (b + 1))
                link(normalise(u, u))
                link(V.tensor_tensor(u, u, gamma.unsqueeze(1).broadcast_to([P, TB, D]), ALU.mult))
                link(V.tensor_tensor(u, u, beta.unsqueeze(1).broadcast_to([P, TB, D]), ALU.add))
                V.tensor_tensor(batch(b), batch(b), u, ALU.add).then_inc(x_updated, TB)
                dve.wait_ge(x_updated, TT + TB * (b + 1))

            for b in range(B):
                dve.wait_ge(x_back[b], 16)
                layer_norm(8 + b)
                add_attention1(b)
                for u in attention1_splits(b):
                    split(1, u)
            for s in range(12, 16):
                layer_norm(s)
            pick_experts(1)
            place_rows(1)
            ffn(1)


def kernel(**inputs):
    import concourse.bacc as bacc
    from concourse.bass_utils import run_bass_kernel_spmd

    nc = bacc.Bacc("TRN2", target_bir_lowering=False, num_devices=1)
    arrays, aps = {}, {}
    for name in NAMES:
        arrays["in_" + name] = np.ascontiguousarray(inputs[name])
        aps[name] = nc.dram_tensor("in_" + name, arrays["in_" + name].shape, F32, kind="ExternalInput").ap()
    arrays["in_const"] = CONST
    const = nc.dram_tensor("in_const", CONST.shape, F32, kind="ExternalInput").ap()
    out = nc.dram_tensor("out", (B, S, D), F32, kind="ExternalOutput").ap()
    build(nc, aps, const, out)
    result = run_bass_kernel_spmd(nc, [arrays], core_ids=[0])
    return result.results[0]["out"]
```

```python
from contextlib import ExitStack

import numpy as np
import concourse.bass as bass
from concourse import mybir

F32 = mybir.dt.float32
F16 = mybir.dt.float16
BF16 = mybir.dt.bfloat16
I32 = mybir.dt.int32
U8 = mybir.dt.uint8
ACT = mybir.ActivationFunctionType
ALU = mybir.AluOpType
AX = mybir.AxisListType.X

P = 128
B, S, D = 4, 512, 256
SC, H, DH = 64, 16, 16
E, F = 8, 1024
T = B * S
TT = T // P
TB = S // P
DC = D // P
FC = F // P
HP = H // 2
SHARED = E
ROUTED = (2 * T + E * (P - 1)) // P
W_SCALE = 64.0
ROW = 2 * D + 6
M_W2, M_DW, M_E1 = range(3)
EPS = 1e-5
SLOT = 4 * 2048
SRING = 4
RAW = 2
RAW1 = RAW + 4


def constants():
    p = np.arange(P)
    c = {}
    c["before"] = (p[:, None] < p[None, :]) * 1.0
    c["vmask"] = ((np.arange(D)[None, :] // DH) % 2 == (p[:, None] // SC)) * 1.0
    c["kvmask"] = (p[:, None] // DH == p[None, :] // DH) * (float(DH) ** -0.5)
    c["kmask"] = ((p[:, None] // DH) % 2 == np.arange(2)[None, :]) * 1.0
    c["row"] = np.broadcast_to(np.arange(P), (P, P))
    c["ident"] = np.eye(P)
    c["rev"] = np.broadcast_to(E - np.arange(E), (P, E))
    c["upto"] = np.broadcast_to((np.arange(E)[None, :] <= np.arange(E)[:, None]).reshape(-1), (P, E * E))
    c["full"] = np.broadcast_to(P * np.arange(TT), (P, TT))
    c["tile"] = np.broadcast_to(np.arange(ROUTED + 2), (P, ROUTED + 2))
    c["token"] = 1 + p[:, None] + P * np.arange(TT)[None, :]
    c["trash"] = 1 + T + p[:, None]
    at, where = 0, {}
    for k, v in c.items():
        where[k] = (at, v.shape[1])
        at += v.shape[1]
    return np.concatenate(list(c.values()), axis=1).astype(np.float32), where


CONST, WHERE = constants()
EARLY = WHERE["ident"][0]
NAMES = ["x", "ctx_1024", "g_xattn", "g_ffn", "L0_xattn_Wq", "L0_xattn_Wk", "L0_xattn_Wv", "L0_xattn_Wo",
         "L0_ffn_gate_w", "L0_ffn_W1", "L0_ffn_b1", "L0_ffn_W2", "L0_ffn_b2", "L0_ffn_sW1", "L0_ffn_sb1",
         "L0_ffn_sW2", "L0_ffn_sb2", "L1_xattn_Wq", "L1_xattn_bq", "L1_xattn_Wk", "L1_xattn_bk", "L1_xattn_Wv",
         "L1_xattn_bv", "L1_xattn_ln_gamma", "L1_xattn_ln_beta", "L1_ffn_Wr", "L1_ffn_W1", "L1_ffn_b1",
         "L1_ffn_W2", "L1_ffn_b2"]


def build(nc, a, const, out):
    with ExitStack() as ctx:
        def sb(name, shape, dt):
            return ctx.enter_context(nc.sbuf_tensor(name, shape, dt))

        def sem(name):
            return ctx.enter_context(nc.semaphore(name))

        def dram(name, shape, dt):
            return nc.dram_tensor(name, shape, dt, kind="Internal").ap()

        token_rows = [dram(f"token_rows{n}", [T, ROW // 2], I32) for n in range(2)]
        x_sum = [dram(f"x_sum{n}", [T + P, D], F32) for n in range(2)]
        kv_dram = dram("kv_dram", [P, B * DC * D], F32)
        kv_bias_dram = dram("kv_bias_dram", [P, B * D], F32)

        weights = sb("weights", [P, E + 1, SLOT], F16)
        weights_at = nc.sbuf_base - 2 * (E + 1) * SLOT
        weight_bytes = weights[:, :, :].rearrange("p e w -> p (e w)").bitcast(U8)
        raw = sb("raw", [P, RAW, 1024], F32)
        const_sb = sb("const_sb", [P, CONST.shape[1] - EARLY], F32)
        const_early = weights[:, 4:6, :].rearrange("p e w -> p (e w)").bitcast(F32)[:, 7424:7424 + EARLY]

        def cst(name):
            at, n = WHERE[name]
            return const_early[:, at:at + n] if at < EARLY else const_sb[:, at - EARLY:at - EARLY + n]

        ident = cst("ident")
        ident16 = sb("ident16", [P, P], F16)
        before16 = sb("before16", [P, P], BF16)
        ones16 = sb("ones16", [P, P], BF16)
        gates = sb("gates", [P, 6], F32)
        b1_cols = [sb(f"b1_cols{n}", [P, FC, E + 1 - n], F32) for n in range(2)]
        gate_cols = sb("gate_cols", [P, 2, DC, E], F32)
        padding_row = sb("padding_row", [P, 2 * D], F16)
        sb2_row = padding_row[:, 0:2 * D].bitcast(F32)
        ln_stats = sb("ln_stats", [P, TB, 6], F32)
        ln_mv = sb("ln_mv", [P, 2, TB, 2], F32)
        ln_rstd = sb("ln_rstd", [P, 2, TB], F32)
        minus_half = sb("minus_half", [P, TB], F32)
        lg = sb("lg", [P, TT, E], F32)
        r_a = sb("r_a", [P, TT, E], F32)
        pick = [sb(f"pick{k}", [P, TT, E], F32) for k in range(2)]
        picked16 = sb("picked16", [P, TT + 1, E], BF16)
        top = [sb(f"top{k}", [P, TT], F32) for k in range(2)]
        order = [sb(f"order{k}", [P, TT], F32) for k in range(2)]
        r_b = r_a[:, :, :].rearrange("p t e -> p (t e)")
        place_i, row_i = (r_b[:, at:at + 2 * TT].bitcast(I32).rearrange("p (k t) -> p k t", k=2) for at in (0, 2 * TT))
        row_at, tile_at = (r_b[:, at:at + TT].bitcast(F16).rearrange("p (k t) -> p k t", k=2) for at in (4 * TT, 5 * TT))
        gate_w = [sb(f"gate_w{k}", [P, TT], F32) for k in range(2)]
        place = [sb(f"place{k}", [P, TT], F32) for k in range(2)]
        row16 = sb("row16", [P, P], F16)
        gather_row = sb("gather_row", [P, ROUTED + 1], I32)
        add_row = sb("add_row", [P, ROUTED + 1], I32)
        gather_now = sb("gather_now", [P, 2], I32)
        add_now = sb("add_now", [P, 2], I32)
        row_weight = lg[:, :, :].rearrange("p t e -> p (t e)")[:, 0:ROUTED]
        n_tiles = sb("n_tiles", [P, E], F32)
        end_tile = sb("end_tile", [P, E], F32)
        base_row = sb("base_row", [P, E], F32)
        tile_expert = sb("tile_expert", [P, ROUTED], F32)
        tile_expert_i = sb("tile_expert_i", [P, ROUTED], I32)
        pick_w = sb("pick_w", [P, 2], F32)

        x_arena = sb("x_arena", [P, TT * D], F32)
        x_sb = x_arena[:, :].rearrange("p (t d) -> p t d", t=TT)
        rows_in = x_arena[:, 0:ROW].bitcast(F16).rearrange("p (k r) -> p k r", k=2)
        rows_in_meta = x_arena[:, 0:ROW].rearrange("p (k r) -> p k r", k=2)[:, :, D:D + 3]
        rows_in_words = x_arena[:, 0:ROW].bitcast(I32).rearrange("p (k r) -> p k r", k=2)
        xT = x_arena[:, ROW:ROW + 512].bitcast(F16).rearrange("p (k r) -> p k r", k=2)
        y_sb = x_arena[:, ROW + 512:ROW + 1024].rearrange("p (k d) -> p k d", k=2)
        b2_at = ROW + 1024
        b2_rows = x_arena[:, b2_at:b2_at + E * D].rearrange("p (e d) -> p e d", e=E)
        work = sb("work", [P, 4096], F32)
        xln = work[:, 0:2048].rearrange("p (k t d) -> p k t d", k=2, t=TB)
        xlnT = work[:, 2048:4096].rearrange("p (k c s) -> p k c s", k=2, c=DC)
        hid = work[:, 0:2048].rearrange("p (k f) -> p k f", k=2)
        hid_hi = work[:, 2048:3072].bitcast(F16).rearrange("p (k f) -> p k f", k=2)
        hid_lo = work[:, 3072:4096].bitcast(F16).rearrange("p (k f) -> p k f", k=2)
        s_xT = work[:, 0:1024].bitcast(F16).rearrange("p (k s) -> p k s", k=2 * DC)
        s_hid = work[:, 1024:2048].rearrange("p (k s) -> p k s", k=2)
        s_pair = work[:, 2048:4096].bitcast(F16).rearrange("p (k l s) -> p k l s", k=SRING, l=2)
        row_arena = sb("row_arena", [P, TT * ROW // 2], F32)
        rows_out = row_arena[:, :].bitcast(F16).rearrange("p (t r) -> p t r", t=TT)
        row_words = row_arena[:, :].bitcast(I32).rearrange("p (t r) -> p t r", t=TT)
        rows_meta = row_arena[:, :].rearrange("p (t r) -> p t r", t=TT)[:, :, D:D + 3]
        ctx_in = row_arena[:, 0:512].rearrange("p (t d) -> p t d", t=2)
        ctxT2 = row_arena[:, 1024:2048].rearrange("p (c b m) -> p c b m", c=DC, b=B)
        k_pair = row_arena[:, 2088:3112].bitcast(F16).rearrange("p (l c b m) -> p l c b m", l=2, c=DC, b=B)
        v_pair = row_arena[:, 3112:4136].bitcast(F16).rearrange("p (l b d) -> p l b d", l=2, b=B)
        x_pair = work[:, :].bitcast(F16).rearrange("p (b l c s) -> p b l c s", b=B, l=2, c=DC)
        att = weights[:, 6:8, :].rearrange("p e w -> p (e w)").bitcast(F32)
        prob_pair = att[:, 0:4096].bitcast(F16).rearrange("p (h l s) -> p h l s", h=HP, l=2)
        xln0 = work[:, 2048:4096].rearrange("p (k t d) -> p k t d", k=2, t=TB)
        wq_pair = att[:, 4096:4608].bitcast(F16).rearrange("p (l c o) -> p l c o", l=2, c=DC)
        wo_pair = att[:, 4608:5120].bitcast(F16).rearrange("p (l c o) -> p l c o", l=2, c=DC)
        wT = att[:, 5120:6144].rearrange("p (w c o) -> p w c o", w=2, c=DC)
        q_pair = att[:, 6144:7168].bitcast(F16).rearrange("p (l c s) -> p l c s", l=2, c=DC)
        o_pair = [att[:, at:at + 1024].bitcast(F16).rearrange("p (l c s) -> p l c s", l=2, c=DC) for at in (7168, 5120)]
        pre = weights[:, 4:6, :].rearrange("p e w -> p (e w)").bitcast(F32)
        w_in = pre[:, 0:3584].rearrange("p (w c i) -> p w c i", w=7, c=DC)
        probs = pre[:, 0:1024].rearrange("p (k s) -> p k s", k=2)
        v_heads = pre[:, 1024:2048].rearrange("p (b d) -> p b d", b=B)
        wT1 = pre[:, 3584:4608].rearrange("p (w c o) -> p w c o", w=2, c=DC)
        kv1 = pre[:, 4608:5632].rearrange("p (w t d) -> p w t d", w=2, t=2)
        kv1_bias = pre[:, 5632:6144].rearrange("p (w d) -> p w d", w=2)
        kv_block = pre[:, 6144:7168].rearrange("p (b c e) -> p b c e", b=B, c=DC)
        ctxT = pre[:, 6144:6656].rearrange("p (c s) -> p c s", c=DC)
        bq_wide = pre[:, 7168:7424].rearrange("p (c m) -> p c m", c=DC)
        few = weights[0:2 * E + 1 + E + DC, 3, :].bitcast(F32)[:, 0:F]
        FEW_B1, FEW_GATE, FEW_BQ = (0, E + 1), 2 * E + 1, 3 * E + 1
        few_count = [FEW_BQ + DC] + [FEW_BQ] * (DC - 1) + [FEW_GATE] * (FC - DC)
        kvm_out = att[:, 0:2048]
        kvb_out = att[:, 2048:3072]
        scratch = [weights[:, e, :].bitcast(F32) for e in (E - 1, SHARED)]
        from_tile = [w[:, 0:TT * (ROUTED + 2)].rearrange("p (t i) -> p t i", t=TT) for w in scratch]
        tile_hot = [w[:, 704:704 + TT * (ROUTED + 1)].bitcast(F16).rearrange("p (k t i) -> p k t i", k=2, t=TT) for w in scratch]
        row_hot = [w[:, 1408:1408 + TT * P].bitcast(F16).rearrange("p (k t r) -> p k t r", k=2, t=TT) for w in scratch]
        late = weights[:, SHARED, :].bitcast(F32)
        kvm = late[:, 0:2048].rearrange("p (b c e) -> p b c e", b=B, c=DC)
        kvb = late[:, 2048:3072].rearrange("p (b d) -> p b d", b=B)
        gamma = late[:, 3072:3328]
        beta = late[:, 3328:3584]
        last_place = weights[:, E - 1, :].bitcast(F32)
        router_xln = last_place[:, 0:2048].rearrange("p (k t d) -> p k t d", k=2, t=TB)
        router_xlnT = last_place[:, 2048:4096].rearrange("p (k c s) -> p k c s", k=2, c=DC)

        bank = [ctx.enter_context(nc.psum_tensor(f"bank{i}", [P, 512], F32)) for i in range(8)]
        tp_ps, q_ps, o_ps, s_ps, p_ps = bank[0:2], bank[0:2], bank[2:4], bank[4:6], bank[6:8]
        kv_ps = bank[2:4]

        def attended_ps(i):
            return bank[2 + 2 * (i // TB % 2) + i % TB // 2][:, i % 2 * D:i % 2 * D + D]

        few_ps = bank[7][:, 0:FC * 32].rearrange("p (f r) -> p f r", f=FC)
        xT_ps = [bank[k][:, 0:256].bitcast(F16) for k in range(2)]
        h_ps = [bank[2:4], bank[4:6]]

        def turn_ps(s):
            return s_ps if s == 0 else tp_ps

        def normed(s):
            return xln0[:, s, :, :] if s < 2 else xln[:, s % 2, :, :]

        y_ps = bank[6:8]
        s_h_ps, s_y_ps = bank[0:2], bank[2:6]
        s_xT_ps = bank[6][:, :].bitcast(F16).rearrange("p (c r) -> p c r", c=2 * DC)

        in_const, in_ctx, in_w, in_w1, in_few, in_bias, in_sb2 = (sem(n) for n in ("in_const", "in_ctx", "in_w", "in_w1", "in_few", "in_bias", "in_sb2"))
        in_x = [sem(f"in_x{b}") for b in range(B)]
        in_raw = [sem(f"in_raw{k}") for k in range(RAW + 8 + 16 + 1)]
        padded = sem("padded")
        pad_ready = sem("pad_ready")
        consts_ready = sem("consts_ready")
        g_ready = sem("g_ready")
        var_ready, rstd_ready = sem("var_ready"), sem("rstd_ready")
        dve_step = sem("dve_step")
        pe_setup, dve_setup, act_setup = sem("pe_setup"), sem("dve_setup"), sem("act_setup")
        kv_stored = sem("kv_stored")
        ln_done, tp_done, xlnT_ready, xlnT_used = sem("ln_done"), sem("tp_done"), sem("xlnT_ready"), sem("xlnT_used")
        x_hi, x_pair_ready = sem("x_hi"), sem("x_pair_ready")
        q_done, q_hi, q_ready = sem("q_done"), sem("q_hi"), sem("q_ready")
        score_done, prob_hi = sem("score_done"), sem("prob_hi")
        prob_lo = [sem(f"prob_lo{k}") for k in range(2)]
        o_done, o_hi, o_ready = sem("o_done"), sem("o_hi"), sem("o_ready")
        attended, beta_ready, beta_added = sem("attended"), sem("beta_ready"), sem("beta_added")
        kvb_added = sem("kvb_added")
        proj_done, x_updated = sem("proj_done"), sem("x_updated")
        split_hi, scaled = sem("split_hi"), sem("scaled")
        split_lo = [sem(f"split_lo{k}") for k in range(2)]
        late_in = sem("late_in")
        router_ln_done, router_tp_done, router_xlnT_ready = sem("router_ln_done"), sem("router_tp_done"), sem("router_xlnT_ready")
        logits_done = sem("logits_done")
        diff_ready, sig_ready = sem("diff_ready"), sem("sig_ready")
        picked_ready, count_done, routed = sem("picked_ready"), sem("count_done"), sem("routed")
        rows_hi, rows_lo = sem("rows_hi"), sem("rows_lo")
        x_stored = [[sem(f"x_stored{n}_{b}") for b in range(B)] for n in range(2)]
        s_turned, s_xT_ready, s_up_done, s_gelu_done = sem("s_turned"), sem("s_xT_ready"), sem("s_up_done"), sem("s_gelu_done")
        s_hi_done, s_down_done = sem("s_hi_done"), sem("s_down_done")
        s_lo_done = sem("s_lo_done")
        s_biased, s_added = sem("s_biased"), sem("s_added")
        words_ready, hot_ready, table_done = (sem(n) for n in ("words_ready", "hot_ready", "table_done"))
        rows_stored = [sem(f"rows_stored{n}") for n in range(2)]
        b2_in = [sem(f"b2_in{n}") for n in range(2)]
        x_back = [sem(f"x_back{b}") for b in range(B)]
        out_stored = sem("out_stored")

        def per_layer(name):
            return [sem(f"{name}_{n}") for n in range(2)]

        row_in = [per_layer(f"row_in{k}") for k in range(2)]
        rowT_done, xT_ready = per_layer("rowT_done"), per_layer("xT_ready")
        up_done, hi_done = per_layer("up_done"), per_layer("hi_done")
        gelu_done = [per_layer(f"gelu_done_half{h}") for h in range(2)]
        hid_ready = [per_layer(f"hid_ready_half{h}") for h in range(2)]
        turn_taken, gather_at_ready, add_at_ready = per_layer("turn_taken"), per_layer("gather_at_ready"), per_layer("add_at_ready")
        half_picked, weight_picked = per_layer("half_picked"), per_layer("weight_picked")
        down_done, biased, y_read, y_ready, added = (per_layer(n) for n in ("down_done", "biased", "y_read", "y_ready", "added"))

        block = ctx.enter_context(nc.Block())

        unit_count = [2 * 2 * (E + 1), 2 * 2 * E]

        def unit(n, u):
            e, m, half = u // 4, (u // 2) % 2, u % 2
            if n == 0:
                e = (SHARED, *range(E))[e]
            return e, m, half

        def split_to(n, u, low):
            e, m, half = unit(n, u)
            if m == 0:
                at = 2048 * low + 1024 * half
                return weights[:, e, at:at + 1024].rearrange("p (g d) -> p g d", d=D)
            at = 4096 + 2048 * half
            return weights[:, e, at:at + 2048].rearrange("p (f l d) -> p f l d", f=FC // 2, l=2)[:, :, low, :]

        def unit_no(n, u):
            return u + (unit_count[0] if n else 0)

        AHEAD = 8
        PLACE = 12
        LAST_SPLITS = 22
        FINAL_SPLITS = 28

        ROWS_AT, LATE6_AT, LATE5_AT, WORK_AT = (RAW + 4 * i for i in range(4))
        PLACES1 = [*range(RAW), *range(ROWS_AT, ROWS_AT + 4), *range(LATE6_AT, LATE6_AT + 4), *range(LATE5_AT, LATE5_AT + 4),
                   *range(RAW), *range(LATE6_AT, LATE6_AT + 4), *range(RAW), *range(LATE6_AT, LATE6_AT + 4),
                   *range(WORK_AT, WORK_AT + 4), *range(RAW)]
        assert len(PLACES1) == unit_count[1]

        EXTRA = RAW + AHEAD + 16
        FIRST_EXTRA, LAST_EXTRA = 18, 27
        PLACES0 = [*range(RAW, RAW + AHEAD), *(u % RAW for u in range(AHEAD, FIRST_EXTRA - RAW)),
                   *((0, 1, EXTRA)[u % 3] for u in range(LAST_EXTRA - FIRST_EXTRA + RAW + 1)),
                   *(u % RAW for u in range(unit_count[0] - LAST_EXTRA - 1))]
        assert len(PLACES0) == unit_count[0] and PLACES0[FIRST_EXTRA] == EXTRA and PLACES0[LAST_EXTRA] == EXTRA
        PLACES = [PLACES0, PLACES1]

        def raw_no(n, u):
            k = PLACES[n][u]
            return AHEAD + k if n and k >= RAW else k

        def raw_at(n, u):
            k = raw_no(n, u)
            if k < RAW:
                return raw[:, k, :].rearrange("p (g d) -> p g d", d=D)
            if k == EXTRA:
                at = 3
                area = weights[:, 6, :].bitcast(F32)
            elif n == 0:
                at = k - RAW
                area = weights[:, PLACE // 4 - 1 + at // 4, :].bitcast(F32)
            else:
                at = PLACES1[u] - RAW
                area = (row_arena, weights[:, 6, :].bitcast(F32), weights[:, 5, :].bitcast(F32), work)[at // 4]
            return area[:, 1024 * (at % 4):1024 * (at % 4 + 1)].rearrange("p (g d) -> p g d", d=D)

        def last_user(n, u):
            before = [v for v in range(u) if PLACES[n][v] == PLACES[n][u]]
            return before[-1] if before else None

        def raw_loaded(n, u):
            before = PLACES0.count(PLACES1[u]) if n and PLACES1[u] < RAW else 0
            return 16 * (before + PLACES[n][:u + 1].count(PLACES[n][u]))

        def by_pool(n, u):
            return n == 1 and RAW1 <= u < FINAL_SPLITS and (u % 2 == 1 or u >= LAST_SPLITS)

        def split_done(eng, n, u):
            halves = [(m, v) for m in range(n + 1) for v in range(unit_count[m]) if m < n or v <= u]
            pools = sum(by_pool(m, v) for m, v in halves)
            eng.wait_ge(split_lo[0], len(halves) - pools)
            if pools:
                eng.wait_ge(split_lo[1], pools)

        class BlockAddress:

            def __init__(self, name, at, count, stationary):
                self.reg = nc.tensor.alloc_register(name)
                self.start = weights_at + (2 * (count - 1) if stationary else 0)
                self.at, self.count = 2 * at, count

            def point(self, expert_at):
                nc.tensor.reg_alu(self.reg, expert_at, self.start + self.at, ALU.add)

            def block(self, count=None):
                value = bass.RuntimeValue.of_register_unchecked(
                    self.reg, min_val=self.start + self.at, max_val=self.start + self.at + 2 * SLOT * (E - 1),
                    guaranteed_mod_val=0, out_of_modulus=2)
                return weight_bytes[:, bass.ds(value - self.start, 2 * (count or self.count))].bitcast(F16)

        def tile_loop(eng, n, body):
            assert ROUTED % 2 == 1
            last = body(0, 0, 0, None)
            body(1, 0, 1, last)
            with eng.Fori(0, (ROUTED - 3) // 2) as t:
                last = body(2 * t + 2, t + 1, 0, None)
                body(2 * t + 3, t + 1, 1, last)
            body(ROUTED - 1, (ROUTED - 1) // 2, 0, None)

        def at_least(j, n):
            return j >= n if isinstance(j, int) else True

        def before_end(j, ahead):
            return j + ahead < ROUTED if isinstance(j, int) else True

        def expert_of(eng, j):
            e = eng.value_load(tile_expert_i[0:1, bass.ds(j, 1)])
            return nc.s_assert_within(e, 0, E - 1, skip_runtime_bounds_check_because="route() clamps the experts to 0 .. E - 1")

        ATTENTION_SPLITS = 4 * 4

        def attention_splits(b, h):
            n = HP * b + h
            return range(ATTENTION_SPLITS * n // (B * HP), ATTENTION_SPLITS * (n + 1) // (B * HP))

        def attention1_splits(b):
            first, count = RAW1, LAST_SPLITS - RAW1
            return range(first + count * b // B, first + count * (b + 1) // B)

        shared_split_blocks = [*range(0, 6), 9, 10, *range(17, 23), *range(25, 31)]

        def shared_splits(first, end):
            return [ATTENTION_SPLITS + i for i, m in enumerate(shared_split_blocks) if first <= m < end]

        def attend0_src(w):
            return a[("L0_xattn_Wq", "L0_xattn_Wk", "L0_xattn_Wv", "L0_xattn_Wo", "L1_xattn_Wq", "L1_xattn_Wk",
                      "L1_xattn_Wv")[w]]

        x_rows = a["x"].rearrange("b s d -> (b s) d")

        def batch_of(rows, b):
            return rows[b * S:(b + 1) * S, :].rearrange("(t p) d -> p t d", p=P)

        @block.sync
        def _(sp):
            sp.dma_start(const_sb[:, :], const[:, EARLY:]).then_inc(in_const, 16)
            sp.dma_start(const_early, const[:, 0:EARLY]).then_inc(in_const, 16)
            sp.dma_start(ctx_in[:, :, :], a["ctx_1024"].rearrange("b s d -> (b s) d").rearrange("(t p) d -> p t d", p=P)).then_inc(in_ctx, 16)
            def load_w(w, ready):
                sp.dma_start(w_in[:, w, :, :], attend0_src(w).rearrange("(c p) i -> p c i", p=P)).then_inc(ready, 16)

            def load_x(b):
                sp.dma_start(x_sb[:, TB * b:TB * b + TB, :], batch_of(x_rows, b)).then_inc(in_x[b], 16)

            for w in range(4):
                load_w(w, in_w)
            load_x(0)
            sp.dma_start(few[0:E, :], a["L0_ffn_b1"]).then_inc(in_few, 16)
            sp.dma_start(few[E:E + 1, :], a["L0_ffn_sb1"].rearrange("(a f) -> a f", a=1)).then_inc(in_few, 16)
            sp.dma_start(few[FEW_B1[1]:FEW_B1[1] + E, :], a["L1_ffn_b1"]).then_inc(in_few, 16)
            sp.dma_start(few[FEW_GATE:FEW_GATE + E, 0:D], a["L0_ffn_gate_w"]).then_inc(in_few, 16)
            sp.dma_start(gate_cols[:, 1, :, :], a["L1_ffn_Wr"].rearrange("(c p) e -> p c e", p=P)).then_inc(in_few, 16)
            sp.dma_start(few[FEW_BQ:FEW_BQ + DC, 0:P], a["L1_xattn_bq"].rearrange("(c p) -> c p", p=P)).then_inc(in_few, 16)
            load_x(1)
            sp.dma_start(kv1_bias[:, 0, :], a["L1_xattn_bk"].partition_broadcast(P)).then_inc(in_bias, 16)
            sp.dma_start(kv1_bias[:, 1, :], a["L1_xattn_bv"].partition_broadcast(P)).then_inc(in_bias, 16)
            sp.dma_start(gates[:, 0:2], a["g_xattn"].partition_broadcast(P)).then_inc(in_bias, 16)
            sp.dma_start(gates[:, 2:4], a["g_ffn"].partition_broadcast(P)).then_inc(in_bias, 16)
            load_x(2)
            load_x(3)
            for w in range(4, 7):
                load_w(w, in_w1)

            def load_unit(n, u):
                if n == 0 and 4 <= u < AHEAD:
                    sp.wait_ge(pe_setup, 4)
                if n == 0 and last_user(0, u) is not None:
                    split_done(sp, 0, last_user(0, u))
                elif n == 0 and PLACES0[u] == EXTRA:
                    sp.wait_ge(o_done, DC * B)
                if n == 1:
                    if u < RAW:
                        split_done(sp, 0, unit_count[0] - 1)
                    elif last_user(1, u) is not None:
                        split_done(sp, 1, last_user(1, u))
                    elif PLACES1[u] >= WORK_AT:
                        sp.wait_ge(x_updated, 2 * TT)
                e, m, half = unit(n, u)
                if e == SHARED:
                    src = (a["L0_ffn_sW1"], a["L0_ffn_sW2"])[m]
                else:
                    src = a[f"L{n}_ffn_W{m + 1}"][e, :, :]
                if m == 0:
                    sp.dma_start(raw_at(n, u).rearrange("p g d -> p (g d)"), src[half * P:half * P + P, :]).then_inc(in_raw[raw_no(n, u)], 16)
                else:
                    sp.dma_start(raw_at(n, u), src[half * F // 2:(half + 1) * F // 2, :].rearrange("(f p) d -> p f d", p=P))\
                      .then_inc(in_raw[raw_no(n, u)], 16)

            def store_kv():
                sp.wait_ge(act_setup, 5)
                sp.wait_ge(dve_setup, 8)
                sp.dma_start(kv_dram, kvm_out).then_inc(kv_stored, 16)
                sp.dma_start(kv_bias_dram, kvb_out).then_inc(kv_stored, 16)

            for u in range(AHEAD + RAW):
                load_unit(0, u)
            sp.wait_ge(pad_ready, 1)
            for n in range(2):
                sp.dma_start(x_sum[n][T:T + P, :], padding_row[:, :].bitcast(F32)).then_inc(padded, 16)
            sp.wait_ge(padded, 32)
            sp.dma_start(sb2_row, a["L0_ffn_sb2"].partition_broadcast(P)).then_inc(in_sb2, 16)
            for u in range(AHEAD + RAW, 24):
                load_unit(0, u)

            def store_rows(n):
                sp.wait_ge(words_ready, n + 1)
                sp.wait_ge(rows_lo, B * (n + 1))
                sp.dma_start(token_rows[n].rearrange("(t p) r -> p t r", p=P), row_words).then_inc(rows_stored[n], 16)

            def store_x(n, b, ready, count):
                sp.wait_ge(ready, count)
                sp.dma_start(batch_of(x_sum[n], b), x_sb[:, TB * b:TB * b + TB, :]).then_inc(x_stored[n][b], 16)

            def biases(n):
                for b in range(B):
                    sp.wait_ge(x_stored[n][b], 16)
                sp.dma_start(b2_rows[:, :, :], a[f"L{n}_ffn_b2"].partition_broadcast(P)).then_inc(b2_in[n], 16)

            def load_ahead():
                sp.wait_ge(s_turned, 2 * B)
                sp.wait_ge(rows_stored[0], 16)
                sp.wait_ge(kv_stored, 32)
                sp.wait_ge(s_down_done, B * FC)
                sp.wait_ge(rowT_done[0], 4)
                sp.dma_start(kvm.rearrange("p b c e -> p (b c e)"), kv_dram).then_inc(late_in, 16)
                sp.dma_start(kvb.rearrange("p b d -> p (b d)"), kv_bias_dram).then_inc(late_in, 16)
                sp.dma_start(gamma, a["L1_xattn_ln_gamma"].partition_broadcast(P)).then_inc(late_in, 16)
                sp.dma_start(beta, a["L1_xattn_ln_beta"].partition_broadcast(P)).then_inc(late_in, 16)
                for u in range(RAW1):
                    sp.wait_ge(rowT_done[0], 6 + 2 * u)
                    load_unit(1, u)

            store_rows(0)
            store_kv()
            for u in range(24, 26):
                load_unit(0, u)
            store_x(0, 0, s_added, TB)
            for u in range(26, 30):
                load_unit(0, u)
            store_x(0, 1, s_added, TB * 2)
            for u in range(30, unit_count[0]):
                load_unit(0, u)
            for b in range(2, B):
                store_x(0, b, s_added, TB * (b + 1))
            biases(0)
            load_ahead()
            sp.wait_ge(added[0], 16 * ROUTED)
            for b in range(B):
                sp.dma_start(x_sb[:, TB * b:TB * b + TB, :], batch_of(x_sum[0], b)).then_inc(x_back[b], 16)
            for u in range(RAW1, 26):
                load_unit(1, u)
            for b in range(B):
                store_x(1, b, x_updated, TT + TB * (b + 1))
            for u in range(26, unit_count[1]):
                load_unit(1, u)
            store_rows(1)
            sp.wait_ge(router_ln_done, B)
            biases(1)
            sp.wait_ge(added[1], 16 * ROUTED)
            sp.dma_start(out.rearrange("b s d -> (b s) d"), x_sum[1][0:T, :]).then_inc(out_stored, 16)
            sp.wait_ge(out_stored, 16)

        @block.gpsimd
        def _(pool):
            nc.gpsimd.memset(padding_row[:, :], 0.0).then_inc(consts_ready, 1)
            nc.gpsimd.memset(ones16[:, :], 1.0).then_inc(consts_ready, 1)
            nc.gpsimd.memset(picked16[:, TT, :], 0.0).then_inc(consts_ready, 1)
            nc.gpsimd.memset(minus_half[:, :], -0.5).then_inc(consts_ready, 1)
            pool.wait_ge(consts_ready, 4)

            def reciprocal_roots(first, count):
                for i in range(first, first + count):
                    pool.wait_ge(var_ready, i + 1)
                    nc.gpsimd.tensor_tensor(ln_rstd[:, i % 2, :], ln_rstd[:, i % 2, :], minus_half[:, :], ALU.pow).then_inc(rstd_ready, 1)

            def rows(s):
                b = s % B
                pool.wait_ge(rows_hi, s // 8 * B + b + 1)
                hi = rows_out[:, TB * b:TB * b + TB, 0:D]
                nc.gpsimd.tensor_tensor(rows_out[:, TB * b:TB * b + TB, D:2 * D], xln[:, s % 2, :, :], hi, ALU.subtract).then_inc(rows_lo, 1)

            def router_rows_low(b):
                pool.wait_ge(rows_hi, B + b + 1)
                hi = rows_out[:, TB * b:TB * b + TB, 0:D]
                nc.gpsimd.tensor_tensor(rows_out[:, TB * b:TB * b + TB, D:2 * D], router_xln[:, b % 2, :, :], hi, ALU.subtract).then_inc(rows_lo, 1)

            def shared_low(m):
                pool.wait_ge(s_hi_done, m + 1)
                nc.gpsimd.tensor_tensor(s_pair[:, m % SRING, 1, :], s_hid[:, m % 2, :], s_pair[:, m % SRING, 0, :], ALU.subtract).then_inc(s_lo_done, 1)

            def gather(n, j, k):
                if at_least(j, 2):
                    pool.wait_ge(rowT_done[n], j - 1)
                    pool.wait_ge(weight_picked[n], j - 1)
                nc.gpsimd.tensor_copy(gather_now[:, k:k + 1], gather_row[:, bass.ds(j, 1)]).then_inc(gather_at_ready[n], 1)
                pool.wait_ge(gather_at_ready[n], j + 1)
                pool.sem_inc(turn_taken[n], 1)
                nc.gpsimd.indirect_dma_start(
                    out=rows_in_words[:, k, :], out_offset=None, in_=token_rows[n],
                    in_offset=bass.IndirectOffsetOnAxis(ap=gather_now[:, k:k + 1], axis=0)).then_inc(row_in[k][n], 16)

            def first_rows(n):
                pool.wait_ge(routed, n + 1)
                pool.wait_ge(rows_stored[n], 16)
                pool.wait_ge(x_stored[n][0], 16)
                gather(n, 0, 0)
                gather(n, 1, 1)

            def ffn_rows(n):

                def add(j, k):
                    if not (isinstance(j, int) and j == 0):
                        pool.wait_ge(added[n], 16 * j)
                    nc.gpsimd.tensor_copy(add_now[:, k:k + 1], add_row[:, bass.ds(j, 1)]).then_inc(add_at_ready[n], 1)
                    pool.wait_ge(y_ready[n], j + 1)
                    pool.wait_ge(add_at_ready[n], j + 1)
                    pool.sem_inc(turn_taken[n], 1)
                    nc.gpsimd.indirect_dma_start(
                        out=x_sum[n], out_offset=bass.IndirectOffsetOnAxis(ap=add_now[:, k:k + 1], axis=0),
                        in_=y_sb[:, k, :], in_offset=None, compute_op=ALU.add).then_inc(added[n], 16)

                def body(j, q, k, last):
                    if before_end(j, 2):
                        gather(n, j + 2, k)
                    if not at_least(j, 2) and j == 1:
                        pool.wait_ge(padded, 32)
                        for b in range(B):
                            pool.wait_ge(x_stored[n][b], 16)
                    if at_least(j, 2):
                        add(j - 2, k)

                tile_loop(pool, n, body)
                for j in (ROUTED - 2, ROUTED - 1):
                    add(j, j % 2)
                pool.wait_ge(row_in[1][n], 16 * ((ROUTED + 1) // 2))

            def split(n, u):
                pool.wait_ge(scaled, sum(by_pool(n, v) for v in range(u + 1)))
                nc.gpsimd.tensor_tensor(split_to(n, u, 1), raw_at(n, u), split_to(n, u, 0), ALU.subtract).then_inc(split_lo[1], 1)

            def probs_low(n):
                pool.wait_ge(prob_hi, n + 1)
                h = n % HP
                nc.gpsimd.tensor_tensor(prob_pair[:, h, 1, :], probs[:, n % 2, :], prob_pair[:, h, 0, :], ALU.subtract).then_inc(prob_lo[1], 1)

            reciprocal_roots(0, 2)
            for b in range(B):
                reciprocal_roots(b + 2, 1)
                for h in range(1, HP, 2):
                    probs_low(HP * b + h)
                if b >= 2:
                    rows(b + 2)
            reciprocal_roots(6, 2)
            rows(6)
            rows(7)
            for m in range(B * FC):
                shared_low(m)
                if m == 26:
                    first_rows(0)
            ffn_rows(0)
            pool.wait_ge(beta_ready, 1)
            roots = 2 * B
            reciprocal_roots(roots, 2)
            roots += 2

            def add_beta(b):
                pool.wait_ge(ln_done, 9 + b)
                nc.gpsimd.tensor_tensor(x_sb[:, TB * b:TB * b + TB, :], x_sb[:, TB * b:TB * b + TB, :],
                                        beta.unsqueeze(1).broadcast_to([P, TB, D]), ALU.add).then_inc(beta_added, 1)

            def add_kvb(b):
                pool.wait_ge(tp_done, 9 + b)
                u = normed(8 + b)
                nc.gpsimd.tensor_tensor(u, u, kvb[:, b, :].unsqueeze(1).broadcast_to([P, TB, D]), ALU.add).then_inc(kvb_added, 1)

            add_kvb(0)
            add_beta(0)
            add_kvb(1)
            add_beta(1)
            later = [u for b in range(1, B) for u in attention1_splits(b) if by_pool(1, u)]
            for u in attention1_splits(0):
                if by_pool(1, u):
                    split(1, u)
            for b in range(B):
                reciprocal_roots(roots, 1)
                if 1 <= b <= 2:
                    router_rows_low(b - 1)
                if b >= 2:
                    split(1, later.pop(0))
                norms = 2 if b < B - 2 else 1
                reciprocal_roots(roots + 1, norms)
                roots += 1 + norms
                if b < B - 2:
                    add_kvb(b + 2)
                    add_beta(b + 2)
                elif b == 2:
                    split(1, later.pop(0))
                    split(1, later.pop(0))
            router_rows_low(2)
            for u in later:
                split(1, u)
            router_rows_low(3)
            for u in range(LAST_SPLITS, FINAL_SPLITS):
                split(1, u)
            first_rows(1)
            ffn_rows(1)

        @block.tensor
        def _(pe):
            expert_at = [pe.alloc_register(f"expert_at{k}") for k in range(2)]
            w1_at = [[[BlockAddress(f"w1_at{f}_{c}_{l}", 2048 * l + 1024 * c + P * f, P, True) for l in range(2)]
                      for c in range(DC)] for f in range(FC)]
            w2_at = [BlockAddress(f"w2_at{f}", 4096 + 2 * D * f, 2 * D, False) for f in range(FC)]
            pe.wait_ge(in_const, 32)
            pe.wait_ge(in_ctx, 16)
            for c in range(DC):
                for t in range(2):
                    m = nc.tensor.transpose(bank[6][:, c * D + t * P:c * D + t * P + P], ctx_in[:, t, c * P:c * P + P], ident)
            m.then_inc(pe_setup, 1)

            def weight_turned(i, w):
                for c in range(DC):
                    for o in range(DC):
                        m = nc.tensor.transpose(bank[i][:, c * D + o * P:c * D + o * P + P], w_in[:, w, o, c * P:c * P + P], ident)
                return m

            pe.wait_ge(in_w, 16 * 4)
            for w in range(4):
                m = weight_turned(w, w)
            m.then_inc(pe_setup, 1)
            def transposed(s):
                pe.wait_ge(ln_done, s + 1)
                if 2 <= s <= 4:
                    pe.wait_ge(x_pair_ready, s)
                elif s > 4:
                    pe.wait_ge(xlnT_ready, s - 4)
                for c in range(DC):
                    for t in range(TB):
                        m = nc.tensor.transpose(turn_ps(s)[c][:, t * P:t * P + P], normed(s)[:, t, c * P:c * P + P], ident)
                m.then_inc(tp_done, 1)

            transposed(0)
            pe.wait_ge(act_setup, 1)
            pe.wait_ge(dve_setup, 1)
            for o in range(DC):
                for c in range(DC):
                    m = nc.tensor.matmul(bank[2][:, o * D:o * D + D], wT[:, 0, c, o * P:o * P + P], ctxT[:, c, :], start=c == 0, stop=c == DC - 1)
            m.then_inc(pe_setup, 1)
            pe.wait_ge(in_few, 16 * 6)
            for f, rows in enumerate(few_count):
                m = nc.tensor.transpose(few_ps[:, f, 0:rows], few[0:rows, f * P:f * P + P], ident[0:rows, 0:rows])
            m.then_inc(pe_setup, 1)
            pe.wait_ge(in_w1, 16 * 3)
            pe.wait_ge(x_pair_ready, 1)
            for w in range(2):
                m = weight_turned(4 + w, 5 + w)
            m.then_inc(pe_setup, 1)
            def product_of_pairs(out, lhs, rhs, first, last):
                nc.tensor.matmul(out, lhs[0], rhs[0], start=first, stop=False)
                nc.tensor.matmul(out, lhs[0], rhs[1], start=False, stop=False)
                return nc.tensor.matmul(out, lhs[1], rhs[0], start=False, stop=last)

            def values(b, c):
                for l in range(2):
                    pe.wait_ge(prob_lo[l], HP // 2 * b + (c + 1) * 2)
                if b:
                    pe.wait_ge(o_ready, DC * (b - 1) + c + 1)
                for lv, lp in ((0, 0), (0, 1), (1, 0)):
                    for i in range(4):
                        h, g = 4 * c + i, 32 * i
                        m = nc.tensor.matmul(o_ps[c][g:g + 32, :], v_pair[:, lv, b, 32 * h:32 * h + 32], prob_pair[:, h, lp, :],
                                             start=lv + lp == 0, stop=lv == 1)
                m.then_inc(o_done, 1)

            def project(b):
                pe.wait_ge(o_ready, DC * (b + 1))
                for t in range(TB):
                    n = TB * b + t
                    if n >= 2:
                        pe.wait_ge(x_updated, n - 1)
                    for c in range(DC):
                        m = product_of_pairs(p_ps[n % 2][:, 0:D], [o_pair[b % 2][:, l, c, t * P:t * P + P] for l in range(2)],
                                             [wo_pair[:, l, c, :] for l in range(2)], c == 0, c == DC - 1)
                    m.then_inc(proj_done, 1)

            def queries(b):
                pe.wait_ge(x_pair_ready, b + 1)
                for o in range(DC):
                    for c in range(DC):
                        m = product_of_pairs(q_ps[o][:, :], [wq_pair[:, l, c, o * P:o * P + P] for l in range(2)],
                                             [x_pair[:, b, l, c, :] for l in range(2)], c == 0, c == DC - 1)
                m.then_inc(q_done, 1)

            def scores(b, h):
                n = HP * b + h
                if n >= 2:
                    pe.wait_ge(prob_hi, n - 1)
                c, g = h // 4, 32 * (h % 4)
                m = product_of_pairs(s_ps[h % 2][:, :], [k_pair[g:g + 32, l, c, b, :] for l in range(2)],
                                     [q_pair[g:g + 32, l, c, :] for l in range(2)], True, True)
                m.then_inc(score_done, 1)

            def head_values(b):
                if b == 0:
                    pe.wait_ge(act_setup, 4)
                    pe.wait_ge(dve_setup, 2)
                for c in range(DC):
                    m = nc.tensor.matmul(bank[6 + b // 2][:, b % 2 * D:b % 2 * D + D], ctxT2[:, c, b, :], wT[:, 1, c, :], start=c == 0, stop=c == DC - 1)
                if b == B - 1:
                    m.then_inc(pe_setup, 1)

            pe.wait_ge(dve_setup, 3)
            queries(0)
            pe.wait_ge(dve_setup, 4)
            pe.wait_ge(act_setup, 3)
            for b in range(B):
                pe.wait_ge(q_ready, b + 1)
                for h in range(HP):
                    scores(b, h)
                    if h == 0:
                        transposed(b + 1)
                    if 2 <= h < 2 + B and not b:
                        head_values(h - 2)
                    if h == 2 and b:
                        values(b - 1, 1)
                    if h == 4 and b:
                        project(b - 1)
                    if h == 6 and b < B - 1:
                        queries(b + 1)
                if b == 0:
                    pe.wait_ge(dve_setup, 5)
                values(b, 0)
            values(B - 1, 1)
            project(B - 1)

            def logits(n, s):
                pe.wait_ge(xlnT_ready, s - 3)
                for t in range(TB):
                    i = TB * (s % B) + t
                    for c in range(DC):
                        m = nc.tensor.matmul(p_ps[0][:, i * E:i * E + E], xlnT[:, s % 2, c, t * P:t * P + P], gate_cols[:, n, c, :], start=c == 0, stop=c == DC - 1)
                m.then_inc(xlnT_used, 1)

            def router_logits(n, between):
                pe.wait_ge(x_updated, TT * (n + 1))
                for b in range(B):
                    s = 8 * n + 4 + b
                    logits(n, s)
                    if b < B - 1:
                        transposed(s + 1)
                    between(b)

            def second_keys(step):
                if step == 0:
                    for w in range(2):
                        for t in range(2):
                            for c in range(DC):
                                m = nc.tensor.matmul(kv_ps[w][:, t * D:t * D + D], ctxT[:, c, t * P:t * P + P], wT1[:, w, c, :], start=c == 0, stop=c == DC - 1)
                    m.then_inc(pe_setup, 1)
                elif step == 1:
                    pe.wait_ge(dve_setup, 6)
                    for b in range(B):
                        r = slice(SC * (b % 2), SC * (b % 2) + SC)
                        for c in range(DC):
                            m = nc.tensor.matmul(s_ps[b % 2][:, (b // 2 * DC + c) * P:(b // 2 * DC + c) * P + P], kv1[r, 0, b // 2, c * P:c * P + P],
                                                 kv1[r, 1, b // 2, c * P:c * P + P], start=True, stop=True)
                    m.then_inc(pe_setup, 1)
                elif step == 2:
                    pe.wait_ge(dve_setup, 7)
                    for b in range(B):
                        for c in range(DC):
                            for e in range(DC):
                                at = c * D + e * P
                                m = nc.tensor.matmul(bank[2 + b][:, at:at + P], w_in[:, 4, e, c * P:c * P + P], kv_block[:, b, e, :], start=True, stop=True)
                    m.then_inc(pe_setup, 1)
                else:
                    pe.wait_ge(act_setup, 5)
                    for b in range(B):
                        for e in range(DC):
                            at = b % 2 * D + e * P
                            m = nc.tensor.matmul(kv_ps[b // 2][:, at:at + P], bq_wide[:, e, :], kv_block[:, b, e, :], start=True, stop=True)
                    m.then_inc(pe_setup, 1)

            def router_counts(n):
                pe.wait_ge(picked_ready, n + 1)
                counts = p_ps[1][:, 0:(TT + 1) * E]
                m = nc.tensor.matmul(counts, before16[:, :], picked16[:, :, :].rearrange("p t e -> p (t e)"), start=True, stop=False)
                for i in range(TT):
                    k = TT - i
                    m = nc.tensor.matmul(p_ps[1][:, (i + 1) * E:(TT + 1) * E], ones16[:, :],
                                         picked16[:, i, :].unsqueeze(1).broadcast_to([P, k, E]), start=False, stop=i == TT - 1)
                m.then_inc(count_done, 1)

            def row_table(n):
                pe.wait_ge(hot_ready, n + 1)
                for k in range(2):
                    for i in range(TT):
                        m = nc.tensor.matmul(p_ps[1][:, D:D + ROUTED + 1], row_hot[n][:, k, i, :], tile_hot[n][:, k, i, :],
                                             start=k + i == 0, stop=k == 1 and i == TT - 1)
                m.then_inc(table_done, 1)

            def shared_turn(i):
                if i:
                    pe.wait_ge(s_xT_ready, i)
                for t in range(2):
                    for c in range(2 * DC):
                        m = nc.tensor.transpose(s_xT_ps[:, c, t * P:t * P + P], rows_out[:, 2 * i + t, c * P:c * P + P], ident16[:, :])
                m.then_inc(s_turned, 1)

            def shared_up(m):
                b, f = m // FC, m % FC
                if f == 0:
                    pe.wait_ge(s_xT_ready, 2 * (b + 1))
                if m >= 2:
                    pe.wait_ge(s_gelu_done, m - 1)
                o = s_h_ps[m % 2][:, :]
                for c in range(DC):
                    hi, lo = s_xT[:, c, :], s_xT[:, DC + c, :]
                    w_hi, w_lo = (weights[:, SHARED, 2048 * l + 1024 * c + P * f:2048 * l + 1024 * c + P * f + P] for l in range(2))
                    nc.tensor.matmul(o, w_hi, hi, start=c == 0, stop=False)
                    nc.tensor.matmul(o, w_hi, lo, start=False, stop=False)
                    i = nc.tensor.matmul(o, w_lo, hi, start=False, stop=c == DC - 1)
                i.then_inc(s_up_done, 1)

            def shared_down(m):
                b, f = m // FC, m % FC
                pe.wait_ge(s_lo_done, m + 1)
                if m == 0:
                    pe.wait_ge(dve_setup, 8)
                at = 4096 + 2 * D * f
                for t in range(TB):
                    if f == 0 and b:
                        pe.wait_ge(s_added, TB * (b - 1) + t + 1)
                    hi, lo = (s_pair[:, m % SRING, l, t * P:t * P + P] for l in range(2))
                    if f < FC - 1:
                        nc.tensor.matmul(s_y_ps[t][:, :], hi, weights[:, SHARED, at:at + 2 * D], start=f == 0, stop=False)
                        i = nc.tensor.matmul(s_y_ps[t][:, 0:D], lo, weights[:, SHARED, at:at + D], start=False, stop=False)
                    else:
                        nc.tensor.matmul(s_y_ps[t][:, 0:D], lo, weights[:, SHARED, at:at + D], start=False, stop=False)
                        i = nc.tensor.matmul(s_y_ps[t][:, :], hi, weights[:, SHARED, at:at + 2 * D], start=False, stop=True)
                i.then_inc(s_down_done, 1)

            def shared_expert():
                pe.wait_ge(rows_lo, B)
                pe.wait_ge(logits_done, 1)
                split_done(pe, 0, 3)
                shared_turn(0)
                shared_turn(1)
                for m in range(B * FC):
                    b, f = m // FC, m % FC
                    if f == 0 and b:
                        shared_turn(2 * b + 1)
                        shared_down(m - 2)
                    shared_up(m)
                    if m >= 2 and f:
                        shared_down(m - 2)
                    if f == FC - 2 and b < B - 1:
                        shared_turn(2 * b + 2)
                    if m == FC:
                        router_counts(0)
                    if m == 17:
                        row_table(0)
                shared_down(B * FC - 2)
                shared_down(B * FC - 1)

            def ffn(n):
                pe.wait_ge(count_done, n + 1)
                pe.wait_ge(routed, n + 1)

                def turn(j, q, k):
                    pe.wait_ge(row_in[k][n], 16 * (q + 1))
                    if at_least(j, 2):
                        pe.wait_ge(xT_ready[n], j - 1)
                    for i in range(2 * DC):
                        m = nc.tensor.transpose(xT_ps[k][:, i * P:i * P + P], rows_in[:, k, i * P:i * P + P], ident16[:, :])
                    m.then_inc(rowT_done[n], 1)

                def up(j, q, k):
                    pe.wait_ge(xT_ready[n], j + 1)
                    if n == 0 and not at_least(j, 2):
                        pe.wait_ge(s_added, TT - 2 if j == 0 else TT)
                    for half in range(2):
                        if at_least(j, 2):
                            pe.wait_ge(gelu_done[half][n], j - 1)
                        for g in range(FC // 2):
                            f = half * FC // 2 + g
                            o = h_ps[k][half][:, g * P:g * P + P]
                            for c in range(DC):
                                hi, lo = xT[:, k, c * P:c * P + P], xT[:, k, (DC + c) * P:(DC + c) * P + P]
                                nc.tensor.matmul(o, w1_at[f][c][0].block(), hi, start=c == 0, stop=False)
                                nc.tensor.matmul(o, w1_at[f][c][0].block(), lo, start=False, stop=False)
                                m = nc.tensor.matmul(o, w1_at[f][c][1].block(), hi, start=False, stop=c == DC - 1)
                        m.then_inc(up_done[n], 1)

                def down(j, k, after_block):
                    if at_least(j, 2):
                        pe.wait_ge(y_read[n], j - 1)
                    for f in range(FC):
                        if f % (FC // 2) == 0:
                            pe.wait_ge(hid_ready[f // (FC // 2)][n], j + 1)
                        hi, lo = hid_hi[:, k, f * P:f * P + P], hid_lo[:, k, f * P:f * P + P]
                        if f < FC - 1:
                            nc.tensor.matmul(y_ps[k][:, :], hi, w2_at[f].block(), start=f == 0, stop=False)
                            nc.tensor.matmul(y_ps[k][:, 0:D], lo, w2_at[f].block(D), start=False, stop=False)
                        else:
                            nc.tensor.matmul(y_ps[k][:, 0:D], lo, w2_at[f].block(D), start=False, stop=False)
                            m = nc.tensor.matmul(y_ps[k][:, :], hi, w2_at[f].block(), start=False, stop=True)
                        if f == FC - 1:
                            m.then_inc(down_done[n], 1)
                        after_block(f)

                def load_expert(j, k):
                    pe.reg_load(expert_at[k], tile_expert_i[0:1, bass.ds(j, 1)])
                    pe.reg_alu(expert_at[k], expert_at[k], 2 * SLOT, ALU.mult)

                w1_blocks = [w1_at[f][c][l] for f in range(FC) for c in range(DC) for l in range(2)]

                def body(j, q, k, last):
                    if before_end(j, 1):
                        turn(j + 1, q + (1 if k else 0), 1 - k)
                    up(j, q, k)

                    def after_block(f):
                        if f == 0 and before_end(j, 1):
                            load_expert(j + 1, 1 - k)
                        w2_at[f].point(expert_at[k])
                        if f and before_end(j, 1):
                            for i in range(len(w1_blocks) * (f - 1) // (FC - 1), len(w1_blocks) * f // (FC - 1)):
                                w1_blocks[i].point(expert_at[1 - k])

                    if at_least(j, 1):
                        down(j - 1, 1 - k, after_block)
                    else:
                        for f in range(FC):
                            after_block(f)

                load_expert(0, 0)
                for i in w1_blocks:
                    i.point(expert_at[0])
                turn(0, 0, 0)
                split_done(pe, n, unit_count[n] - 1)
                tile_loop(pe, n, body)
                down(ROUTED - 1, (ROUTED - 1) % 2, lambda f: None)

            pe.wait_ge(act_setup, 4)
            router_logits(0, second_keys)
            shared_expert()
            ffn(0)

            pe.wait_ge(late_in, 64)
            pe.wait_ge(y_read[0], ROUTED)

            def attention1(b):
                s = 8 + b
                pe.wait_ge(xlnT_ready, s - 3)
                if b >= 2:
                    pe.wait_ge(attended, TB * (b - 1))
                for t in range(TB):
                    i = TB * b + t
                    for c in range(DC):
                        m = nc.tensor.matmul(attended_ps(i), xlnT[:, s % 2, c, t * P:t * P + P], kvm[:, b, c, :], start=c == 0, stop=c == DC - 1)
                    m.then_inc(proj_done, 1)

            def router1(b, after):
                pe.wait_ge(router_ln_done, b + 1)
                pe.wait_ge(xlnT_ready, after - 3)
                if b:
                    pe.wait_ge(router_xlnT_ready, b)
                for c in range(DC):
                    for t in range(TB):
                        m = nc.tensor.transpose(tp_ps[c][:, t * P:t * P + P], router_xln[:, b % 2, t, c * P:c * P + P], ident)
                m.then_inc(router_tp_done, 1)
                pe.wait_ge(router_xlnT_ready, b + 1)
                for t in range(TB):
                    i = TB * b + t
                    for c in range(DC):
                        m = nc.tensor.matmul(p_ps[0][:, i * E:i * E + E], router_xlnT[:, b % 2, c, t * P:t * P + P], gate_cols[:, 1, c, :], start=c == 0, stop=c == DC - 1)
                m.then_inc(xlnT_used, 1)

            transposed(8)
            transposed(9)
            attention1(0)
            attention1(1)
            for b in range(B):
                if b < B - 2:
                    if b:
                        pe.wait_ge(router_xlnT_ready, b)
                    transposed(10 + b)
                router1(b, min(10 + b, 8 + B - 1))
                if b < B - 2:
                    attention1(b + 2)
            router_counts(1)
            row_table(1)
            ffn(1)

        @block.scalar
        def _(act):
            act.wait_ge(in_bias, 64)
            nc.scalar.activation(gates[:, 0:4], gates[:, 0:4], ACT.Tanh).then_inc(g_ready, 1)
            act.wait_ge(pe_setup, 2)
            for i in range(2):
                m = nc.scalar.activation(wT[:, i, :, :].rearrange("p c o -> p (c o)"), bank[1 + i][:, :], ACT.Copy)
            m.then_inc(act_setup, 1)
            for pair, i in ((wq_pair, 0), (wo_pair, 3)):
                m = nc.scalar.activation(pair[:, 0, :, :].rearrange("p c o -> p (c o)"), bank[i][:, :], ACT.Copy, scale=W_SCALE)
            m.then_inc(act_setup, 1)

            def split(n, u):
                act.wait_ge(in_raw[raw_no(n, u)], raw_loaded(n, u))
                if n == 0 and u == 4 * 7 + 3:
                    split_done(act, 0, LAST_EXTRA)
                if n == 1 and u % 4 == 0 and u >= 4 * 5:
                    split_done(act, 1, u - 1 if u > 4 * 5 else LATE5_AT + 3)
                    if u == 4 * (E - 1):
                        act.wait_ge(xlnT_used, 2 * B)
                        act.wait_ge(rows_lo, 2 * B)
                if n == 1 and u == 4 * 6 + 2:
                    split_done(act, 1, u - 1)
                nc.scalar.activation(split_to(n, u, 0), raw_at(n, u), ACT.Copy, scale=W_SCALE).then_inc(split_hi, 1)
                if by_pool(n, u):
                    act.wait_ge(split_hi, unit_no(n, u) + 1)
                    nc.scalar.activation(raw_at(n, u), raw_at(n, u), ACT.Copy, scale=W_SCALE).then_inc(scaled, 1)

            def read_out(s):
                act.wait_ge(tp_done, s + 1)
                nc.scalar.activation(xlnT[:, s % 2, 0, :], tp_ps[0][:, :], ACT.Copy)
                nc.scalar.activation(xlnT[:, s % 2, 1, :], tp_ps[1][:, :], ACT.Copy).then_inc(xlnT_ready, 1)

            def rows(s):
                b = s % B
                act.wait_ge(ln_done, s + 1)
                if s >= 8:
                    act.wait_ge(x_updated, 2 * TT)
                nc.scalar.activation(rows_out[:, TB * b:TB * b + TB, 0:D], xln[:, s % 2, :, :], ACT.Copy).then_inc(rows_hi, 1)

            def turn_logits(n, b, rows_too):
                s = 8 * n + 4 + b
                if b > 1:
                    act.wait_ge(xlnT_used, 4 * n + b - 1)
                if b or n == 0:
                    read_out(s)
                if rows_too:
                    rows(s)

            def x_high(s):
                act.wait_ge(tp_done, s + 1)
                for c in range(DC):
                    nc.scalar.activation(x_pair[:, s, 0, c, :], turn_ps(s)[c][:, :], ACT.Copy).then_inc(x_hi, 1)

            def q_high(b):
                act.wait_ge(q_done, b + 1)
                for c in range(DC):
                    nc.scalar.activation(q_pair[:, 0, c, :], q_ps[c][:, :], ACT.Copy, scale=1.0 / W_SCALE).then_inc(q_hi, 1)

            def o_high(b, c):
                act.wait_ge(o_done, DC * b + c + 1)
                if b >= 2:
                    act.wait_ge(proj_done, TB * (b - 1))
                nc.scalar.activation(o_pair[b % 2][:, 0, c, :], o_ps[c][:, :], ACT.Copy).then_inc(o_hi, 1)

            def few_columns():
                act.wait_ge(pe_setup, 4)
                for n in range(2):
                    nc.scalar.activation(b1_cols[n][:, :, :], few_ps[:, :, FEW_B1[n]:FEW_B1[n] + E + 1 - n], ACT.Copy)
                nc.scalar.activation(bq_wide[:, :, :], few_ps[:, 0, FEW_BQ:FEW_BQ + DC].unsqueeze(2).broadcast_to([P, DC, P]), ACT.Copy)
                nc.scalar.activation(gate_cols[:, 0, :, :], few_ps[:, 0:DC, FEW_GATE:FEW_GATE + E], ACT.Copy).then_inc(act_setup, 1)

            x_high(0)
            act.wait_ge(pe_setup, 5)
            for w in range(2):
                m = nc.scalar.activation(wT1[:, w, :, :].rearrange("p c o -> p (c o)"), s_ps[w][:, :], ACT.Copy)
            m.then_inc(act_setup, 1)
            q_high(0)
            for b in range(B):
                for h in range(HP):
                    n = HP * b + h
                    act.wait_ge(score_done, n + 1)
                    if n >= 2:
                        act.wait_ge(prob_lo[h % 2], n // 2)
                    nc.scalar.activation(probs[:, n % 2, :], s_ps[h % 2][:, :], ACT.Sigmoid, scale=float(DH) ** -0.5)
                    if b and h % 4 == 0:
                        act.wait_ge(o_done, DC * (b - 1) + h // 4 + 1)
                    nc.scalar.activation(prob_pair[:, h, 0, :], s_ps[h % 2][:, :], ACT.Sigmoid, scale=float(DH) ** -0.5).then_inc(prob_hi, 1)
                    if h == 0 and b:
                        o_high(b - 1, 0)
                    if h == 1:
                        if b < B - 1:
                            x_high(b + 1)
                        else:
                            turn_logits(0, 0, False)
                    if h == 1 and not b:
                        few_columns()
                    if h == 3 and b:
                        o_high(b - 1, 1)
                    for u in attention_splits(b, h):
                        split(0, u)
                if b < B - 1:
                    q_high(b + 1)
                if b >= 2:
                    rows(b + 2)
            for c in range(DC):
                o_high(B - 1, c)
            turn_logits(0, 1, False)
            turn_logits(0, 2, True)
            turn_logits(0, 3, True)
            act.wait_ge(pe_setup, 9)
            for b in range(B):
                m = nc.scalar.activation(kvm_out[:, b * 512:b * 512 + 512], bank[2 + b][:, :], ACT.Copy)
            m.then_inc(act_setup, 1)

            def weights_of_experts(n):
                act.wait_ge(diff_ready, n + 1)
                nc.scalar.activation(gate_w[0][:, :], top[0][:, :], ACT.Sigmoid)
                nc.scalar.activation(gate_w[1][:, :], top[0][:, :], ACT.Sigmoid, scale=-1.0).then_inc(sig_ready, 1)

            def shared_expert():
                def turned(b, half):
                    act.wait_ge(s_turned, 2 * b + half + 1)
                    nc.scalar.activation(s_xT[:, :, half * 2 * P:(half + 1) * 2 * P], s_xT_ps, ACT.Copy).then_inc(s_xT_ready, 1)

                turned(0, 0)
                turned(0, 1)
                weights_of_experts(0)
                for m in range(B * FC):
                    b, f = m // FC, m % FC
                    last_block = f == FC - 1 and b < B - 1
                    act.wait_ge(s_up_done, m + 1)
                    if last_block:
                        turned(b + 1, 0)
                    if m >= 2:
                        act.wait_ge(s_lo_done, m - 1)
                    nc.scalar.activation(s_hid[:, m % 2, :], s_h_ps[m % 2][:, :], ACT.Gelu, bias=b1_cols[0][:, f, E:E + 1],
                                         scale=1.0 / W_SCALE).then_inc(s_gelu_done, 1)
                    if last_block:
                        turned(b + 1, 1)
                    act.wait_ge(s_gelu_done, m + 1)
                    if m >= SRING:
                        act.wait_ge(s_down_done, m - SRING + 1)
                    nc.scalar.activation(s_pair[:, m % SRING, 0, :], s_hid[:, m % 2, :], ACT.Copy).then_inc(s_hi_done, 1)
                    for u in shared_splits(m, m + 1):
                        if u == 28:
                            act.wait_ge(kv_stored, 32)
                        if u == 32:
                            act.wait_ge(table_done, 1)
                        split(0, u)

            def ffn(n):
                act.wait_ge(routed, n + 1)

                def body(j, q, k, last):
                    e = expert_of(act, j)
                    for half in range(2):
                        act.wait_ge(up_done[n], 2 * j + half + 1)
                        if at_least(j, 2):
                            act.wait_ge(hid_ready[half][n], j - 1)
                        for g in range(FC // 2):
                            f = half * FC // 2 + g
                            m = nc.scalar.activation(hid[:, k, f * P:f * P + P], h_ps[k][half][:, g * P:g * P + P], ACT.Gelu,
                                                     bias=b1_cols[n][:, f, bass.ds(e, 1)], scale=1.0 / W_SCALE)
                        m.then_inc(gelu_done[half][n], 1)

                tile_loop(act, n, body)

            shared_expert()
            ffn(0)
            act.wait_ge(down_done[0], ROUTED)
            for u in range(RAW1):
                split(1, u)

            def router_read_out(b):
                act.wait_ge(router_tp_done, b + 1)
                nc.scalar.activation(router_xlnT[:, b % 2, 0, :], tp_ps[0][:, :], ACT.Copy)
                nc.scalar.activation(router_xlnT[:, b % 2, 1, :], tp_ps[1][:, :], ACT.Copy).then_inc(router_xlnT_ready, 1)
                if b == 0:
                    split_done(act, 1, RAW1 - 1)
                nc.scalar.activation(rows_out[:, TB * b:TB * b + TB, 0:D], router_xln[:, b % 2, :, :], ACT.Copy).then_inc(rows_hi, 1)

            read_out(8)
            read_out(9)
            for b in range(B):
                for u in attention1_splits(b):
                    split(1, u)
                if b < B - 2:
                    read_out(10 + b)
                router_read_out(b)
            for u in range(LAST_SPLITS, LAST_SPLITS + 2):
                split(1, u)
            weights_of_experts(1)
            for u in range(LAST_SPLITS + 2, unit_count[1]):
                split(1, u)
            ffn(1)

        @block.vector
        def _(dve):
            V = nc.vector
            chain, norms = [0], [0]

            def link(ins):
                chain[0] += 1
                ins.then_inc(dve_step, 1)
                dve.wait_ge(dve_step, chain[0])

            dve.wait_ge(in_const, 32)
            dve.wait_ge(consts_ready, 4)
            V.tensor_copy(row16[:, :], cst("row"))
            V.tensor_copy(ident16[:, :], ident).then_inc(pad_ready, 1)
            link(V.tensor_copy(before16[:, :], cst("before")))
            dve.wait_ge(pe_setup, 1)
            ctx_ps = bank[6][:, :].rearrange("p (c s) -> p c s", c=DC)
            V.tensor_copy(ctxT[:, :, :], ctx_ps).then_inc(dve_setup, 1)
            for c in range(DC):
                m = V.tensor_copy(ctxT2[:, c, :, :].rearrange("p b (j s) -> p b j s", j=2),
                                  ctx_ps[:, c, :].rearrange("p (b s) -> p b s", b=B).unsqueeze(2).broadcast_to([P, B, 2, SC]))
            m.then_inc(dve_setup, 1)

            def weight_pairs():
                dve.wait_ge(act_setup, 2)
                for pair, i in ((wq_pair, 0), (wo_pair, 3)):
                    m = V.scalar_tensor_tensor(pair[:, 1, :, :].rearrange("p c o -> p (c o)"), bank[i][:, :], W_SCALE,
                                               pair[:, 0, :, :].rearrange("p c o -> p (c o)"), ALU.mult, ALU.subtract)
                m.then_inc(dve_setup, 1)

            def keys():
                dve.wait_ge(pe_setup, 3)
                kT = bank[2][:, :].rearrange("p (c b s) -> p c b s", c=DC, b=B)
                for c in range(DC):
                    for j in range(2):
                        m = V.tensor_scalar(k_pair[:, 0, c, :, SC * j:SC * j + SC], kT[:, c, :, :], cst("kmask")[:, j:j + 1], None, ALU.mult)
                link(m)
                for c in range(DC):
                    for j in range(2):
                        m = V.scalar_tensor_tensor(k_pair[:, 1, c, :, SC * j:SC * j + SC], kT[:, c, :, :], cst("kmask")[:, j:j + 1],
                                                   k_pair[:, 0, c, :, SC * j:SC * j + SC], ALU.mult, ALU.subtract)
                m.then_inc(dve_setup, 1)

            def head_values():
                dve.wait_ge(pe_setup, 6)
                for b in range(B):
                    m = V.tensor_tensor(v_heads[:, b, :], bank[6 + b // 2][:, b % 2 * D:b % 2 * D + D], cst("vmask"), ALU.mult)
                link(m)
                link(V.tensor_copy(v_pair[:, 0, :, :], v_heads[:, :, :]))
                V.tensor_tensor(v_pair[:, 1, :, :], v_heads[:, :, :], v_pair[:, 0, :, :], ALU.subtract).then_inc(dve_setup, 1)

            def second_keys(step):
                if step == 0:
                    dve.wait_ge(in_bias, 64)
                    dve.wait_ge(pe_setup, 7)
                    for w in range(2):
                        for t in range(2):
                            m = V.tensor_tensor(kv1[:, w, t, :], kv_ps[w][:, t * D:t * D + D], kv1_bias[:, w, :], ALU.add)
                    m.then_inc(dve_setup, 1)
                elif step == 1:
                    dve.wait_ge(pe_setup, 8)
                    for b in range(B):
                        for c in range(DC):
                            at = (b // 2 * DC + c) * P
                            m = V.tensor_tensor(kv_block[:, b, c, :], s_ps[b % 2][:, at:at + P], cst("kvmask"), ALU.mult)
                    m.then_inc(dve_setup, 1)
                else:
                    dve.wait_ge(pe_setup, 10)
                    V.tensor_copy(kvb_out[:, 0:512], kv_ps[0][:, :])
                    V.tensor_copy(kvb_out[:, 512:1024], kv_ps[1][:, :]).then_inc(dve_setup, 1)

            def split(n, u):
                dve.wait_ge(split_hi, unit_no(n, u) + 1)
                V.scalar_tensor_tensor(split_to(n, u, 1), raw_at(n, u), W_SCALE, split_to(n, u, 0), ALU.mult, ALU.subtract).then_inc(split_lo[0], 1)

            def moments(src):
                k = norms[0] % 2
                norms[0] += 1
                for t in range(TB):
                    m = V.bn_stats(ln_stats[:, t, :], src[:, t, :])
                link(m)
                for t in range(TB):
                    m = V.bn_aggr(ln_mv[:, k, t, :], ln_stats[:, t, :])
                link(m)
                V.tensor_scalar(ln_rstd[:, k, :], ln_mv[:, k, :, 1], EPS, None, ALU.add).then_inc(var_ready, 1)
                return norms[0]

            def normalise(src, dst, number):
                k = (number - 1) % 2
                dve.wait_ge(rstd_ready, number)
                for t in range(TB):
                    m = V.tensor_scalar(dst[:, t, :], src[:, t, :], ln_mv[:, k, t, 0:1], ln_rstd[:, k, t:t + 1], ALU.subtract, ALU.mult)
                return m

            def batch(b):
                return x_sb[:, TB * b:TB * b + TB, :]

            def norm_begin(s):
                if s < B:
                    dve.wait_ge(in_x[s], 16)
                return moments(batch(s % B))

            def norm_end(s, number):
                if s in (2, 3):
                    dve.wait_ge(q_done, s - 1)
                elif s >= 4:
                    dve.wait_ge(tp_done, s - 1)
                if s % 8 >= 6:
                    dve.wait_ge(rows_lo, s // 8 * B + s % 8 - 5)
                normalise(batch(s % B), normed(s), number).then_inc(ln_done, 1)

            def x_low(s):
                for c in range(DC):
                    dve.wait_ge(x_hi, DC * s + c + 1)
                    m = V.tensor_tensor(x_pair[:, s, 1, c, :], turn_ps(s)[c][:, :], x_pair[:, s, 0, c, :], ALU.subtract)
                m.then_inc(x_pair_ready, 1)

            def add_attention0(b):
                for t in range(TB):
                    n = TB * b + t
                    dve.wait_ge(proj_done, n + 1)
                    V.scalar_tensor_tensor(x_sb[:, n, :], p_ps[n % 2][:, 0:D], gates[:, 5:6], x_sb[:, n, :], ALU.mult, ALU.add).then_inc(x_updated, 1)
                dve.wait_ge(x_updated, TB * b + TB)

            def q_low(b):
                for c in range(DC):
                    dve.wait_ge(q_hi, DC * b + c + 1)
                    m = V.scalar_tensor_tensor(q_pair[:, 1, c, :], q_ps[c][:, :], 1.0 / W_SCALE, q_pair[:, 0, c, :], ALU.mult, ALU.subtract)
                m.then_inc(q_ready, 1)

            def o_low(b, c):
                dve.wait_ge(o_hi, DC * b + c + 1)
                V.tensor_tensor(o_pair[b % 2][:, 1, c, :], o_ps[c][:, :], o_pair[b % 2][:, 0, c, :], ALU.subtract).then_inc(o_ready, 1)

            def attention0(b):
                number = norm_begin(b + 2)
                for h in range(0, HP, 2):
                    n = HP * b + h
                    dve.wait_ge(prob_hi, n + 1)
                    V.tensor_tensor(prob_pair[:, h, 1, :], probs[:, n % 2, :], prob_pair[:, h, 0, :], ALU.subtract).then_inc(prob_lo[0], 1)
                    if h == 0:
                        if b:
                            o_low(b - 1, 0)
                        if b < B - 1:
                            x_low(b + 1)
                    if h == 2:
                        if b:
                            o_low(b - 1, 1)
                        norm_end(b + 2, number)
                    if h == 4:
                        if b:
                            add_attention0(b - 1)
                    for u in attention_splits(b, h):
                        split(0, u)
                    if h == 6 and not b:
                        head_values()
                    if h == 6 and b < B - 1:
                        q_low(b + 1)
                    for u in attention_splits(b, h + 1):
                        split(0, u)

            def wide(ap, n):
                return ap.unsqueeze(2).broadcast_to([P, TT, n])

            def pick_experts(n):
                dve.wait_ge(xlnT_used, 4 * (n + 1))
                V.tensor_copy(lg[:, :, :].rearrange("p t e -> p (t e)"), p_ps[0][:, 0:TT * E]).then_inc(logits_done, 1)
                dve.wait_ge(logits_done, n + 1)
                rev = cst("rev").unsqueeze(1).broadcast_to([P, TT, E])
                for k in range(2):
                    link(V.reduce_max(top[k][:, :], lg[:, :, :], AX))
                    link(V.tensor_tensor(r_a[:, :, :], lg[:, :, :], wide(top[k][:, :], E), ALU.is_equal))
                    link(V.tensor_tensor(r_a[:, :, :], r_a[:, :, :], rev, ALU.mult))
                    link(V.reduce_max(order[k][:, :], r_a[:, :, :], AX))
                    link(V.tensor_tensor(pick[k][:, :, :], rev, wide(order[k][:, :], E), ALU.is_equal))
                    if k == 0:
                        link(V.scalar_tensor_tensor(lg[:, :, :], pick[0][:, :, :], -3.0e38, lg[:, :, :], ALU.mult, ALU.add))
                V.tensor_tensor(picked16[:, 0:TT, :], pick[0][:, :, :], pick[1][:, :, :], ALU.add).then_inc(picked_ready, 1)
                V.tensor_tensor(top[0][:, :], top[0][:, :], top[1][:, :], ALU.subtract).then_inc(diff_ready, 1)

            def place_rows(n):
                dve.wait_ge(count_done, n + 1)
                counts = p_ps[1][:, 0:(TT + 1) * E]
                link(V.tensor_copy(r_a[:, :, :].rearrange("p t e -> p (t e)"), counts[:, 0:TT * E]))
                link(V.tensor_copy(n_tiles[:, :], counts[:, TT * E:(TT + 1) * E]))
                full = cst("full").unsqueeze(1).broadcast_to([P, E, TT])
                need = lg[:, :, :].rearrange("p t e -> p (t e)").rearrange("p (e t) -> p e t", e=E)
                link(V.tensor_tensor(need, n_tiles[:, :].unsqueeze(2).broadcast_to([P, E, TT]), full, ALU.is_gt))
                link(V.reduce_sum(n_tiles[:, :], need, AX))
                upto = lg[:, 0:E, :]
                link(V.tensor_tensor(upto, n_tiles[:, :].unsqueeze(1).broadcast_to([P, E, E]),
                                     cst("upto").rearrange("p (e i) -> p e i", e=E), ALU.mult))
                link(V.reduce_sum(end_tile[:, :], upto, AX))
                link(V.tensor_tensor(base_row[:, :], end_tile[:, :], n_tiles[:, :], ALU.subtract))
                link(V.tensor_scalar(base_row[:, :], base_row[:, :], float(P), None, ALU.mult))
                link(V.tensor_tensor(r_a[:, :, :], r_a[:, :, :], base_row[:, :].unsqueeze(1).broadcast_to([P, TT, E]), ALU.add))
                for k in range(2):
                    link(V.tensor_tensor(lg[:, :, :], pick[k][:, :, :], r_a[:, :, :], ALU.mult))
                    link(V.reduce_sum(place[k][:, :], lg[:, :, :], AX))
                for k in range(2):
                    link(V.tensor_copy(place_i[:, k, :], place[k][:, :]))
                link(V.tensor_scalar(row_i[:, :, :], place_i[:, :, :], P - 1, None, ALU.bitwise_and))
                link(V.tensor_copy(row_at[:, :, :], row_i[:, :, :]))
                link(V.tensor_scalar(row_i[:, :, :], place_i[:, :, :], P.bit_length() - 1, None, ALU.arith_shift_right))
                link(V.tensor_copy(tile_at[:, :, :], row_i[:, :, :]))
                for k in range(2):
                    link(V.tensor_tensor(from_tile[n][:, :, 0:ROUTED + 1], cst("tile")[:, 0:ROUTED + 1].unsqueeze(1).broadcast_to([P, TT, ROUTED + 1]),
                                         wide(tile_at[:, k, :], ROUTED + 1), ALU.is_equal))
                    link(V.tensor_tensor(tile_hot[n][:, k, :, :], from_tile[n][:, :, 0:ROUTED + 1], wide(cst("token"), ROUTED + 1), ALU.mult))
                    m = V.tensor_tensor(row_hot[n][:, k, :, :], row16[:, :].unsqueeze(1).broadcast_to([P, TT, P]), wide(row_at[:, k, :], P), ALU.is_equal)
                m.then_inc(hot_ready, 1)
                for first in range(0, ROUTED, TT):
                    m = min(TT, ROUTED - first)
                    past = lg[:, 0:m, :]
                    link(V.tensor_tensor(past, cst("tile")[:, first:first + m].unsqueeze(2).broadcast_to([P, m, E]),
                                         end_tile[:, :].unsqueeze(1).broadcast_to([P, m, E]), ALU.is_ge))
                    link(V.reduce_sum(tile_expert[:, first:first + m], past, AX))
                link(V.tensor_scalar(tile_expert[:, :], tile_expert[:, :], float(E - 1), None, ALU.min))
                link(V.tensor_copy(tile_expert_i[:, :], tile_expert[:, :]))

            def row_tokens(n):
                dve.wait_ge(table_done, n + 1)
                table = p_ps[1][:, D:D + ROUTED + 1]
                padding = from_tile[n][:, 0, 0:ROUTED + 1]
                link(V.tensor_scalar(padding, table, 0.0, cst("trash"), ALU.is_equal, ALU.mult))
                link(V.scalar_tensor_tensor(padding, table, -1.0, padding, ALU.add, ALU.add))
                link(V.tensor_copy(add_row[:, :], padding))
                link(V.tensor_scalar(padding, table, -1.0, 0.0, ALU.add, ALU.max))
                V.tensor_copy(gather_row[:, :], padding).then_inc(routed, 1)

            def row_words_of(n):
                dve.wait_ge(sig_ready, n + 1)
                dve.wait_ge(rows_hi, B * (n + 1))
                g = gates[:, 2 + n:3 + n]
                link(V.tensor_scalar(gate_w[0][:, :], gate_w[0][:, :], g, None, ALU.mult))
                link(V.tensor_scalar(gate_w[1][:, :], gate_w[1][:, :], g, None, ALU.mult))
                V.tensor_copy(rows_meta[:, :, M_W2], gate_w[1][:, :])
                V.tensor_tensor(rows_meta[:, :, M_DW], gate_w[0][:, :], gate_w[1][:, :], ALU.subtract)
                V.tensor_scalar(rows_meta[:, :, M_E1], order[0][:, :], -1.0, float(E), ALU.mult, ALU.add).then_inc(words_ready, 1)

            def shared_result(b):
                if b == 0:
                    dve.wait_ge(in_sb2, 16)
                    link(V.tensor_scalar(sb2_row, sb2_row, gates[:, 2:3], None, ALU.mult))
                V.tensor_tensor(batch(b), batch(b), sb2_row.unsqueeze(1).broadcast_to([P, TB, D]), ALU.add).then_inc(s_biased, 1)
                dve.wait_ge(s_biased, (TB + 1) * b + 1)
                dve.wait_ge(s_down_done, FC * (b + 1))
                for first in range(0, TB, 2):
                    for t in (first, first + 1):
                        x_tile = x_sb[:, TB * b + t, :]
                        V.scalar_tensor_tensor(x_tile, s_y_ps[t][:, 0:D], gates[:, 4:5], x_tile, ALU.mult, ALU.add).then_inc(s_biased, 1)
                    for t in (first, first + 1):
                        x_tile = x_sb[:, TB * b + t, :]
                        dve.wait_ge(s_biased, (TB + 1) * b + 2 + t)
                        V.scalar_tensor_tensor(x_tile, s_y_ps[t][:, D:2 * D], gates[:, 4:5], x_tile, ALU.mult, ALU.add).then_inc(s_added, 1)

            def ffn(n):
                def turned(j, k):
                    dve.wait_ge(rowT_done[n], j + 1)
                    if at_least(j, 2):
                        dve.wait_ge(up_done[n], 2 * (j - 1))
                    V.tensor_copy(xT[:, k, :], xT_ps[k]).then_inc(xT_ready[n], 1)

                def pick_weight(j, k):
                    words = rows_in_meta[:, k, :]
                    V.tensor_scalar(pick_w[:, k:k + 1], words[:, M_E1:M_E1 + 1], tile_expert[:, bass.ds(j, 1)], words[:, M_DW:M_DW + 1],
                                    ALU.is_equal, ALU.mult).then_inc(half_picked[n], 1)
                    dve.wait_ge(half_picked[n], j + 1)
                    V.tensor_tensor(row_weight[:, bass.ds(j, 1)], pick_w[:, k:k + 1], words[:, M_W2:M_W2 + 1], ALU.add).then_inc(weight_picked[n], 1)

                def split_hidden(j, k):
                    if at_least(j, 2):
                        dve.wait_ge(down_done[n], j - 1)
                    for half in range(2):
                        f = slice(half * F // 2, (half + 1) * F // 2)
                        dve.wait_ge(gelu_done[half][n], j + 1)
                        V.tensor_copy(hid_hi[:, k, f], hid[:, k, f]).then_inc(hi_done[n], 1)
                        dve.wait_ge(hi_done[n], 2 * j + half + 1)
                        V.tensor_tensor(hid_lo[:, k, f], hid[:, k, f], hid_hi[:, k, f], ALU.subtract).then_inc(hid_ready[half][n], 1)

                def result(j, q, k):
                    e = expert_of(dve, j)
                    if not at_least(j, 1):
                        dve.wait_ge(b2_in[n], 16)
                    dve.wait_ge(down_done[n], j + 1)
                    if at_least(j, 2):
                        dve.wait_ge(added[n], 16 * (j - 1))
                    V.scalar_tensor_tensor(y_sb[:, k, :], y_ps[k][:, 0:D], 1.0 / W_SCALE, b2_rows[:, bass.ds(e, 1), :].rearrange("p a d -> p (a d)"),
                                           ALU.mult, ALU.add).then_inc(biased[n], 1)
                    dve.wait_ge(biased[n], j + 1)
                    V.scalar_tensor_tensor(y_sb[:, k, :], y_ps[k][:, D:2 * D], 1.0 / W_SCALE, y_sb[:, k, :], ALU.mult, ALU.add).then_inc(y_read[n], 1)
                    dve.wait_ge(y_read[n], j + 1)
                    dve.wait_ge(weight_picked[n], j + 1)
                    V.tensor_scalar(y_sb[:, k, :], y_sb[:, k, :], row_weight[:, bass.ds(j, 1)], None, ALU.mult).then_inc(y_ready[n], 1)

                def body(j, q, k, last):
                    if before_end(j, 1):
                        turned(j + 1, 1 - k)
                    split_hidden(j, k)
                    if before_end(j, 1):
                        pick_weight(j + 1, 1 - k)
                    if at_least(j, 1):
                        result(j - 1, q - (0 if k else 1), 1 - k)

                dve.wait_ge(x_stored[n][0], 16)
                dve.wait_ge(x_stored[n][1], 16)
                turned(0, 0)
                pick_weight(0, 0)
                tile_loop(dve, n, body)
                result(ROUTED - 1, (ROUTED - 1) // 2, (ROUTED - 1) % 2)

            first = norm_begin(0)
            weight_pairs()
            norm_end(0, first)
            second = norm_begin(1)
            x_low(0)
            keys()
            norm_end(1, second)
            dve.wait_ge(g_ready, 1)
            link(V.tensor_scalar(gates[:, 4:5], gates[:, 2:3], 1.0 / W_SCALE, None, ALU.mult))
            link(V.tensor_scalar(gates[:, 5:6], gates[:, 0:1], 1.0 / W_SCALE, None, ALU.mult))
            q_low(0)
            for b in range(B):
                attention0(b)
            for c in range(DC):
                o_low(B - 1, c)
            third = norm_begin(6)
            add_attention0(B - 1)
            last = norm_begin(7)
            norm_end(6, third)
            norm_end(7, last)
            second_keys(0)
            second_keys(1)
            pick_experts(0)
            second_keys(2)
            row_words_of(0)
            for u in shared_splits(0, FC):
                split(0, u)
            shared_result(0)
            place_rows(0)
            for u in shared_splits(FC, 2 * FC):
                split(0, u)
            shared_result(1)
            row_tokens(0)
            for u in shared_splits(2 * FC, 3 * FC):
                split(0, u)
            shared_result(2)
            for u in shared_splits(3 * FC, 4 * FC):
                split(0, u)
            shared_result(3)
            ffn(0)
            dve.wait_ge(late_in, 64)
            link(V.tensor_scalar(gamma, gamma, gates[:, 1:2], None, ALU.mult))
            V.tensor_scalar(beta, beta, gates[:, 1:2], None, ALU.mult).then_inc(beta_ready, 1)

            def sums1(b):
                u = normed(8 + b)
                dve.wait_ge(kvb_added, b + 1)
                for t in range(TB):
                    i = TB * b + t
                    if t % 2 == 0:
                        dve.wait_ge(proj_done, TT + i + 2)
                    V.tensor_tensor(u[:, t, :], attended_ps(i), u[:, t, :], ALU.add).then_inc(attended, 1)
                dve.wait_ge(attended, TB * (b + 1))
                return moments(u)

            def add_attention1(b, number):
                u = normed(8 + b)
                k = (number - 1) % 2
                for t in range(TB):
                    m = V.scalar_tensor_tensor(u[:, t, :], u[:, t, :], ln_mv[:, k, t, 0:1], gamma, ALU.subtract, ALU.mult)
                link(m)
                dve.wait_ge(rstd_ready, number)
                dve.wait_ge(beta_added, b + 1)
                for t in range(TB):
                    x_tile = x_sb[:, TB * b + t, :]
                    V.scalar_tensor_tensor(x_tile, u[:, t, :], ln_rstd[:, k, t:t + 1], x_tile, ALU.mult, ALU.add).then_inc(x_updated, 1)
                dve.wait_ge(x_updated, TT + TB * (b + 1))

            for u in range(RAW1 - 1):
                split(1, u)
            numbers = []
            for b in range(2):
                dve.wait_ge(x_back[b], 16)
                numbers.append(norm_begin(8 + b))
            norm_end(8, numbers[0])
            norm_end(9, numbers[1])
            split(1, RAW1 - 1)

            def router_norm_end(b, number):
                if b >= 2:
                    dve.wait_ge(router_tp_done, b - 1)
                    dve.wait_ge(rows_lo, B + b - 1)
                normalise(batch(b), router_xln[:, b % 2, :, :], number).then_inc(router_ln_done, 1)

            later = [u for b in range(1, B) for u in attention1_splits(b) if not by_pool(1, u)]
            for u in attention1_splits(0):
                if not by_pool(1, u):
                    split(1, u)
            for b in range(B):
                add_attention1(b, sums1(b))
                if b < B - 2:
                    dve.wait_ge(x_back[b + 2], 16)
                    next_number = norm_begin(10 + b)
                number = moments(batch(b))
                if b < B - 2:
                    norm_end(10 + b, next_number)
                router_norm_end(b, number)
                for u in (later[0:0], later[0:1], later[1:4], later[4:])[b]:
                    split(1, u)
            pick_experts(1)
            row_words_of(1)
            place_rows(1)
            row_tokens(1)
            for u in range(FINAL_SPLITS, unit_count[1]):
                split(1, u)
            ffn(1)


def kernel(**inputs):
    import concourse.bacc as bacc
    from concourse.bass_utils import run_bass_kernel_spmd

    nc = bacc.Bacc("TRN2", target_bir_lowering=False, num_devices=1)
    arrays, aps = {}, {}
    for name in NAMES:
        arrays["in_" + name] = np.ascontiguousarray(inputs[name])
        aps[name] = nc.dram_tensor("in_" + name, arrays["in_" + name].shape, F32, kind="ExternalInput").ap()
    arrays["in_const"] = CONST
    const = nc.dram_tensor("in_const", CONST.shape, F32, kind="ExternalInput").ap()
    out = nc.dram_tensor("out", (B, S, D), F32, kind="ExternalOutput").ap()
    build(nc, aps, const, out)
    result = run_bass_kernel_spmd(nc, [arrays], core_ids=[0])
    return result.results[0]["out"]
```
